# Optimizing a Trainium2 kernel written in Bass

```python
import numpy as np
import jax
import jax.numpy as jnp

def _softmax(x, axis=-1):
    return jax.nn.softmax(x, axis=axis)

def _gelu(x):
    return jax.nn.gelu(x, approximate=True)

def _silu(x):
    return jax.nn.silu(x)

def _sigmoid(x):
    return jax.nn.sigmoid(x)

def _layernorm(x, axis=-1, eps=1e-05):
    m = jnp.mean(x, axis=axis, keepdims=True)
    v = jnp.var(x, axis=axis, keepdims=True)
    return (x - m) / jnp.sqrt(v + eps)

def _scatter_add(tgt, idx, src, axis=0):
    return tgt.at[idx].add(src)

def _segment_sum(src, seg, n):
    return jax.ops.segment_sum(src, seg, n)
kernel_name = 'mk_early_fusion_embed_d1_tok_img512_r4_f5a298'

def setup_inputs(seed: int=0):
    np.random.seed(seed)
    _w = jnp.asarray

    def _rec_inputs():
        import jax
        import jax.numpy as jnp
        _rk = jax.random.key(seed)
        x = -0.000147625 + 0.999875 * jax.random.normal(jax.random.fold_in(_rk, 1), (64, 3, 224, 224), jnp.float32)
        x_txt = jax.random.randint(jax.random.fold_in(_rk, 51), (64, 128), 0, 5, jnp.int32)
        return (x, x_txt)
    x, x_txt = _rec_inputs()

    def _L0_tok_setup():
        import jax, jax.numpy as jnp
        import numpy as np
        N_PATCHES = 8
        PATCH = 28
        C = 3
        IN_D = C * PATCH * PATCH
        HID = 128
        SEQ = N_PATCHES * N_PATCHES + 1

        def _positional_embedding(seq_len, dim):
            i = np.arange(seq_len)[:, None].astype(np.float32)
            j = np.arange(dim)[None, :].astype(np.float32)
            ang = i / np.power(100000.0, j / dim)
            pe = np.where(j % 2 == 0, np.sin(ang), np.cos(ang))
            return jnp.asarray(pe, dtype=jnp.float32)
        key = jax.random.key(seed)
        k1, k2, k3, k4 = jax.random.split(key, 4)
        B = 64
        X = jax.random.normal(k1, (B, C, 224, 224), dtype=jnp.float32)
        bound = 1.0 / np.sqrt(IN_D)
        W = jax.random.uniform(k2, (HID, IN_D), minval=-bound, maxval=bound, dtype=jnp.float32)
        b = jax.random.uniform(k3, (HID,), minval=-bound, maxval=bound, dtype=jnp.float32)
        class_token = jax.random.uniform(k4, (1, HID), dtype=jnp.float32)
        pos_embed = _positional_embedding(SEQ, HID)
        return {'X': X, 'W': W, 'b': b, 'class_token': class_token, 'pos_embed': pos_embed}
    _L0_tok_all = _L0_tok_setup()
    _L0_tok_in = {k: v for k, v in _L0_tok_all.items() if k in ('W', 'b', 'class_token', 'pos_embed')}
    del _L0_tok_all

    def _L0_txt_setup():
        import jax, jax.numpy as jnp
        import numpy as np
        NUM_CLASSES = 5
        FEATURES = 128
        key = jax.random.key(seed)
        k1, k2, k3 = jax.random.split(key, 3)
        X = jax.random.randint(k1, (32, 2048), 0, NUM_CLASSES, dtype=jnp.int64)
        W = jax.random.normal(k2, (FEATURES, NUM_CLASSES), dtype=jnp.float32) / np.sqrt(NUM_CLASSES)
        b = jax.random.normal(k3, (FEATURES,), dtype=jnp.float32) * 0.01
        return {'X': X, 'W': W, 'b': b}
    _L0_txt_all = _L0_txt_setup()
    _L0_txt_in = {k: v for k, v in _L0_txt_all.items() if k in ('W', 'b')}
    del _L0_txt_all

    def _L0_attn_setup():
        import jax, jax.numpy as jnp
        import numpy as np
        NUM_HEADS = 8
        NUM_LANDMARKS = 64
        TOPK_LANDMARKS = 4
        key = jax.random.key(seed)
        k1, k2, k3, k4 = jax.random.split(key, 4)
        B, N, C = (1, 512, 128)
        return {'x': jax.random.normal(k1, (B, N, C), jnp.float32), 'w_qkv': jax.random.normal(k2, (3 * C, C), jnp.float32) * 0.02, 'w_proj': jax.random.normal(k3, (C, C), jnp.float32) * 0.02, 'b_proj': jax.random.normal(k4, (C,), jnp.float32) * 0.02}
    _L0_attn_all = _L0_attn_setup()
    _L0_attn_in = {k: v for k, v in _L0_attn_all.items() if k in ('w_qkv', 'w_proj', 'b_proj')}
    del _L0_attn_all

    def _L0_ffn_setup():
        import jax, jax.numpy as jnp
        import numpy as np
        B, S, D, F, E, K, H = (4, 256, 128, 512, 8, 2, 8)
        HEAD_DIM = D // H

        def _layernorm(x, g, b):
            m = x.mean(-1, keepdims=True)
            v = ((x - m) ** 2).mean(-1, keepdims=True)
            return (x - m) * jax.lax.rsqrt(v + 1e-05) * g + b

        def _expert(x, Wqkv, bqkv, Wo, bo, g1, be1, W1, bf1, W2, bf2, g2, be2):
            b, s, d = x.shape
            qkv = x @ Wqkv.T + bqkv
            q, k, v = jnp.split(qkv, 3, axis=-1)
            to_heads = lambda t: t.reshape(b, s, H, HEAD_DIM).transpose(0, 2, 1, 3)
            q, k, v = (to_heads(q), to_heads(k), to_heads(v))
            scale = 1.0 / np.sqrt(HEAD_DIM).astype(np.float32)
            attn = jax.nn.softmax(jnp.einsum('bhqd,bhkd->bhqk', q * scale, k), axis=-1)
            ctx = jnp.einsum('bhqk,bhkd->bhqd', attn, v).transpose(0, 2, 1, 3).reshape(b, s, d)
            ctx = ctx @ Wo.T + bo
            x = _layernorm(x + ctx, g1, be1)
            h = jax.nn.gelu(x @ W1.T + bf1, approximate=False)
            h = jax.nn.gelu(h @ W2.T + bf2, approximate=False)
            return _layernorm(x + h, g2, be2)
        key = jax.random.key(seed)
        ks = jax.random.split(key, 8)
        s = 0.02
        return {'x': jax.random.normal(ks[0], (B, S, D), jnp.float32), 'gate_Wk': jax.random.normal(ks[1], (D, D), jnp.float32) * s, 'gate_bk': jnp.zeros((D,), jnp.float32), 'expert_queries': jax.random.normal(ks[2], (E, D), jnp.float32), 'Wqkv': jax.random.normal(ks[3], (E, 3 * D, D), jnp.float32) * s, 'bqkv': jnp.zeros((E, 3 * D), jnp.float32), 'Wo': jax.random.normal(ks[4], (E, D, D), jnp.float32) * s, 'bo': jnp.zeros((E, D), jnp.float32), 'g1': jnp.ones((E, D), jnp.float32), 'be1': jnp.zeros((E, D), jnp.float32), 'W1': jax.random.normal(ks[5], (E, F, D), jnp.float32) * s, 'bf1': jnp.zeros((E, F), jnp.float32), 'W2': jax.random.normal(ks[6], (E, D, F), jnp.float32) * s, 'bf2': jnp.zeros((E, D), jnp.float32), 'g2': jnp.ones((E, D), jnp.float32), 'be2': jnp.zeros((E, D), jnp.float32)}
    _L0_ffn_all = _L0_ffn_setup()
    _L0_ffn_in = {k: v for k, v in _L0_ffn_all.items() if k in ('gate_Wk', 'gate_bk', 'expert_queries', 'Wqkv', 'bqkv', 'Wo', 'bo', 'g1', 'be1', 'W1', 'bf1', 'W2', 'bf2', 'g2', 'be2')}
    del _L0_ffn_all
    return {'x': x, 'x_txt': x_txt, 'L0_tok_W': _L0_tok_in['W'], 'L0_tok_b': _L0_tok_in['b'], 'L0_tok_class_token': _L0_tok_in['class_token'], 'L0_tok_pos_embed': _L0_tok_in['pos_embed'], 'L0_txt_W': _L0_txt_in['W'], 'L0_txt_b': _L0_txt_in['b'], 'L0_attn_w_qkv': _L0_attn_in['w_qkv'], 'L0_attn_w_proj': _L0_attn_in['w_proj'], 'L0_attn_b_proj': _L0_attn_in['b_proj'], 'L0_ffn_gate_Wk': _L0_ffn_in['gate_Wk'], 'L0_ffn_gate_bk': _L0_ffn_in['gate_bk'], 'L0_ffn_expert_queries': _L0_ffn_in['expert_queries'], 'L0_ffn_Wqkv': _L0_ffn_in['Wqkv'], 'L0_ffn_bqkv': _L0_ffn_in['bqkv'], 'L0_ffn_Wo': _L0_ffn_in['Wo'], 'L0_ffn_bo': _L0_ffn_in['bo'], 'L0_ffn_g1': _L0_ffn_in['g1'], 'L0_ffn_be1': _L0_ffn_in['be1'], 'L0_ffn_W1': _L0_ffn_in['W1'], 'L0_ffn_bf1': _L0_ffn_in['bf1'], 'L0_ffn_W2': _L0_ffn_in['W2'], 'L0_ffn_bf2': _L0_ffn_in['bf2'], 'L0_ffn_g2': _L0_ffn_in['g2'], 'L0_ffn_be2': _L0_ffn_in['be2']}

def reference(x, x_txt, L0_tok_W, L0_tok_b, L0_tok_class_token, L0_tok_pos_embed, L0_txt_W, L0_txt_b, L0_attn_w_qkv, L0_attn_w_proj, L0_attn_b_proj, L0_ffn_gate_Wk, L0_ffn_gate_bk, L0_ffn_expert_queries, L0_ffn_Wqkv, L0_ffn_bqkv, L0_ffn_Wo, L0_ffn_bo, L0_ffn_g1, L0_ffn_be1, L0_ffn_W1, L0_ffn_bf1, L0_ffn_W2, L0_ffn_bf2, L0_ffn_g2, L0_ffn_be2):
    import jax
    import jax.numpy as jnp

    def _L0_tok_ref(X, W, b, class_token, pos_embed):
        import jax, jax.numpy as jnp
        import numpy as np
        N_PATCHES = 8
        PATCH = 28
        C = 3
        IN_D = C * PATCH * PATCH
        HID = 128
        SEQ = N_PATCHES * N_PATCHES + 1

        def _positional_embedding(seq_len, dim):
            i = np.arange(seq_len)[:, None].astype(np.float32)
            j = np.arange(dim)[None, :].astype(np.float32)
            ang = i / np.power(100000.0, j / dim)
            pe = np.where(j % 2 == 0, np.sin(ang), np.cos(ang))
            return jnp.asarray(pe, dtype=jnp.float32)
        B = X.shape[0]
        patches = X.reshape(B, C, N_PATCHES, PATCH, N_PATCHES, PATCH)
        patches = patches.transpose(0, 2, 4, 1, 3, 5).reshape(B, N_PATCHES * N_PATCHES, IN_D)
        tokens = jnp.einsum('bpi,hi->bph', patches, W) + b
        cls = jnp.broadcast_to(class_token[None, :, :], (B, 1, HID))
        tokens = jnp.concatenate([cls, tokens], axis=1)
        return tokens * pos_embed[None, :, :]

    def _L0_txt_ref(X, W, b):
        import jax, jax.numpy as jnp
        import numpy as np
        NUM_CLASSES = 5
        FEATURES = 128
        return jnp.take(W.T, X, axis=0) + b

    def _L0_attn_ref(x, w_qkv, w_proj, b_proj):
        import jax, jax.numpy as jnp
        import numpy as np
        NUM_HEADS = 8
        NUM_LANDMARKS = 64
        TOPK_LANDMARKS = 4
        B, N, C = x.shape
        H = NUM_HEADS
        Dh = C // H
        m = min(NUM_LANDMARKS, N)
        kl = min(TOPK_LANDMARKS, m)
        scale = Dh ** (-0.5)
        qkv = (x @ w_qkv.T).reshape(B, N, 3, H, Dh).transpose(2, 0, 3, 1, 4)
        q, k, v = (qkv[0], qkv[1], qkv[2])
        seg = -(-N // m)
        pad = seg * m - N

        def segmentize(t):
            if pad > 0:
                t = jnp.pad(t, ((0, 0), (0, 0), (0, pad), (0, 0)))
            return t.reshape(B, H, m, seg, Dh)
        k_seg = segmentize(k)
        v_seg = segmentize(v)
        centroids = k_seg.mean(axis=3)
        route = jnp.einsum('bhnd,bhmd->bhnm', q, centroids) * scale
        _, topk_idx = jax.lax.top_k(route, kl)
        gather = jax.vmap(jax.vmap(lambda segs, ix: segs[ix]))
        sel_k = gather(k_seg, topk_idx).reshape(B, H, N, kl * seg, Dh)
        sel_v = gather(v_seg, topk_idx).reshape(B, H, N, kl * seg, Dh)
        attn = jnp.einsum('bhnd,bhnkd->bhnk', q, sel_k) * scale
        attn = jax.nn.softmax(attn, axis=-1)
        out = jnp.einsum('bhnk,bhnkd->bhnd', attn, sel_v)
        out = out.transpose(0, 2, 1, 3).reshape(B, N, C)
        return out @ w_proj.T + b_proj

    def _L0_ffn_ref(x, gate_Wk, gate_bk, expert_queries, Wqkv, bqkv, Wo, bo, g1, be1, W1, bf1, W2, bf2, g2, be2):
        import jax, jax.numpy as jnp
        import numpy as np
        B, S, D, F, E, K, H = (4, 256, 128, 512, 8, 2, 8)
        HEAD_DIM = D // H

        def _layernorm(x, g, b):
            m = x.mean(-1, keepdims=True)
            v = ((x - m) ** 2).mean(-1, keepdims=True)
            return (x - m) * jax.lax.rsqrt(v + 1e-05) * g + b

        def _expert(x, Wqkv, bqkv, Wo, bo, g1, be1, W1, bf1, W2, bf2, g2, be2):
            b, s, d = x.shape
            qkv = x @ Wqkv.T + bqkv
            q, k, v = jnp.split(qkv, 3, axis=-1)
            to_heads = lambda t: t.reshape(b, s, H, HEAD_DIM).transpose(0, 2, 1, 3)
            q, k, v = (to_heads(q), to_heads(k), to_heads(v))
            scale = 1.0 / np.sqrt(HEAD_DIM).astype(np.float32)
            attn = jax.nn.softmax(jnp.einsum('bhqd,bhkd->bhqk', q * scale, k), axis=-1)
            ctx = jnp.einsum('bhqk,bhkd->bhqd', attn, v).transpose(0, 2, 1, 3).reshape(b, s, d)
            ctx = ctx @ Wo.T + bo
            x = _layernorm(x + ctx, g1, be1)
            h = jax.nn.gelu(x @ W1.T + bf1, approximate=False)
            h = jax.nn.gelu(h @ W2.T + bf2, approximate=False)
            return _layernorm(x + h, g2, be2)
        keys = x @ gate_Wk.T + gate_bk
        scores = jnp.einsum('bsd,ed->bse', keys, expert_queries) * D ** (-0.5)
        probs = jax.nn.softmax(scores, axis=-1)
        _, idx = jax.lax.top_k(probs, K)
        mask = jax.nn.one_hot(idx, E, dtype=probs.dtype).sum(-2)
        gated = probs * mask
        gated = gated / (gated.sum(-1, keepdims=True) + 1e-09)
        eo = jax.vmap(_expert, in_axes=(None,) + (0,) * 12)(x, Wqkv, bqkv, Wo, bo, g1, be1, W1, bf1, W2, bf2, g2, be2)
        return jnp.einsum('ebsd,bse->bsd', eo, gated)
    h = _L0_tok_ref(x, L0_tok_W, L0_tok_b, L0_tok_class_token, L0_tok_pos_embed)
    h = jnp.concatenate([h, _L0_txt_ref(x_txt, L0_txt_W, L0_txt_b)], axis=1)
    h = h + _L0_attn_ref(_layernorm(h, axis=-1), L0_attn_w_qkv, L0_attn_w_proj, L0_attn_b_proj)
    h = h + _L0_ffn_ref(_layernorm(h, axis=-1), L0_ffn_gate_Wk, L0_ffn_gate_bk, L0_ffn_expert_queries, L0_ffn_Wqkv, L0_ffn_bqkv, L0_ffn_Wo, L0_ffn_bo, L0_ffn_g1, L0_ffn_be1, L0_ffn_W1, L0_ffn_bf1, L0_ffn_W2, L0_ffn_bf2, L0_ffn_g2, L0_ffn_be2)
    return h

_drawn_inputs = setup_inputs


def setup_inputs(seed=0):
    import zlib

    import numpy as np

    out = dict(_drawn_inputs(seed))
    spreads = {'L0_ffn_gate_bk': (0.0, 0.1),
     'L0_ffn_bqkv': (0.0, 0.718),
     'L0_ffn_bo': (0.0, 0.1),
     'L0_ffn_g1': (1.0, 0.2),
     'L0_ffn_be1': (0.0, 0.1),
     'L0_ffn_bf1': (0.0, 0.8),
     'L0_ffn_bf2': (0.0, 0.315),
     'L0_ffn_g2': (1.0, 0.2),
     'L0_ffn_be2': (0.0, 0.1)}
    factors = {'L0_tok_b': 2.827,
     'L0_txt_b': 2.715,
     'L0_ffn_Wqkv': 6.868,
     'L0_ffn_Wo': 3.761,
     'L0_ffn_W1': 4.114,
     'L0_ffn_W2': 3.643}
    for name, (base, spread) in spreads.items():
        noise = np.random.default_rng([zlib.crc32(name.encode()), seed]).standard_normal(out[name].shape)
        drawn = base * np.exp(spread * noise) if base else spread * noise
        out[name] = jnp.asarray(drawn.astype(out[name].dtype))
    for name, factor in factors.items():
        out[name] = (out[name] * factor).astype(out[name].dtype)
    return out
```

```python
from contextlib import ExitStack

import concourse.bass as bass
from concourse import mybir

F32 = mybir.dt.float32
F16 = mybir.dt.float16
BF16 = mybir.dt.bfloat16
I32 = mybir.dt.int32
ALU = mybir.AluOpType
ACT = mybir.ActivationFunctionType
AX = mybir.AxisListType.X

B = 64
D = 128
H = 8
DH = D // H
NP = 64
NCLS = 5
SEQT = 128
SEQ = 1 + NP + SEQT
NT = 1 + NP + NCLS
NTP = NT + 1
T0 = 1 + NP
SEGS = 64
SEGL = -(-SEQ // SEGS)
TOPK = 4
NSENT = 8 - TOPK
RW = SEGS + NSENT
UB = 8
NU = B // UB
UC = UB * NT
HC = UC // 2
RP = 112
RT = H * NT // RP
QC = H * NT + 128 - RP
E = 8
F = 512
FCH = F // D
KP = 112
KJ = 3 * 28 * 28 // KP
SCALE = DH ** -0.5
LN_EXP = "natural_log_exp_and_others"
EPS = 1e-5
NSTEP = UB + 3

CONST = dict(C=D, J=D, I=D, mask=H * NT, A=SEGS, tcol=NTP, M4=SEGS, MT=NTP, tval=1)
SHARED = dict(wq=D, wk=D, wv=D, wp=2 * D, gwk=D, eq=E, be2=D, pos=1 + NP, txtw=NCLS,
              bp=1, tokb=1, cls=1, txtb=1, gbk=1)
EATT = dict(wq=D, wk=D, wv=D, bq=1, bk=1)
EFFN = dict(wo=2 * D, w1=F, w2=F, pick=D, bv=2, bo=1, g1=1, be1=1, bf1=FCH, bf2=1, g2=1)


def columns(block):
    at, out = 0, {}
    for name, n in block.items():
        out[name] = (at, at + n)
        at += n
    return out, at


CCOL, CW = columns(CONST)
SCOL, SW = columns(SHARED)
ACOL, AW = columns(EATT)
FCOL, FW = columns(EFFN)


def build(nc, x_in, xt_in, xr_in, const_in, shared_in, tokw_in, eatt_in, effn_in, out):
    with ExitStack() as ctx:
        def sb(name, shape, dt=F32):
            return ctx.enter_context(nc.sbuf_tensor(name, shape, dt))

        def sem(name):
            return ctx.enter_context(nc.semaphore(name))

        const = sb("const", [128, CW])
        shared = sb("shared", [128, SW])
        tokw = sb("tokw", [KP, KJ, D])
        patches = sb("patches", [KP, 2, KJ, 4 * NP])
        eatt = [sb(f"eatt{i}", [128, AW]) for i in range(2)]
        effn = [sb(f"effn{i}", [128, FW]) for i in range(2)]
        text_i = sb("text_i", [128, B], I32)
        text_f = sb("text_f", [128, B])
        textrow = sb("textrow", [NT, UB * SEQT], I32)
        onehot = sb("onehot", [128, UB, NTP], BF16)
        onehot_t = sb("onehot_t", [NT, UB, SEQT])
        segof = sb("segof", [128, SEGS], BF16)
        ident16 = sb("ident16", [128, 128], BF16)
        maskf = sb("maskf", [128, H, NT])
        mask16 = sb("mask16", [128, H, NT], F16)
        ones16 = sb("ones16", [128, 128], BF16)
        sentinel = sb("sentinel", [1, RT, RW], BF16)
        count_t = sb("count_t", [SEGS, UB, NTP], BF16)
        count4 = sb("count4", [NTP, UB, SEGS])
        lnw = sb("lnw", [3, 8, UB * NCLS])
        lnn = sb("lnn", [3, UB, NT], BF16)
        lnpart = sb("lnpart", [3, 3, UB * NCLS], BF16)
        hA = sb("hA", [128, UB, NT])
        hB = sb("hB", [128, UC])
        xn = sb("xn", [128, UC])
        sq = sb("sq", [128, UC])
        sqf = sb("sqf", [128, UC])
        rs = sb("rs", [128, UC])
        rsf = sb("rsf", [128, UC])
        qf = sb("qf", [128, UC])
        kf = sb("kf", [128, UC])
        qh = sb("qh", [128, UC], F16)
        ql = sb("ql", [128, UC], F16)
        kh = sb("kh", [128, UC], F16)
        kl = sb("kl", [128, UC], F16)
        qxh = sb("qxh", [128, 2, QC], F16)
        qxl = sb("qxl", [128, 2, QC], F16)
        qxf = sb("qxf", [128, 2, QC])
        klm = sb("klm", [128, UB, NTP + RW])
        ktok = sb("ktok", [NT, UB * D])
        vtok = sb("vtok", [NT, UB * D + DH])
        top8 = sb("top8", [128, RT, 8])
        routed = sb("routed", [128, RT, RW])
        chosen = sb("chosen", [128, RT, SEGS], BF16)
        chosen_t = sb("chosen_t", [SEGS, QC], BF16)
        pen = sb("pen", [128, RT, NTP])
        negmax = sb("negmax", [128, 2, RT])
        den = sb("den", [128, 3, RT])
        rden = sb("rden", [128, 3, RT])
        probs = sb("probs", [128, 3, RT, NTP])
        probs_t = sb("probs_t", [NT, 2, H * NT])
        cx = sb("cx", [128, 2, 2, UB, NT])
        epsc = sb("epsc", [128, 1])
        bvo = sb("bvo", [128, 2])
        y = sb("y", [128, UC])
        z = sb("z", [128, UC])
        x1 = sb("x1", [128, UC])
        g = sb("g", [128, 2, UC])
        acc = sb("acc", [128, UC])
        gate = sb("gate", [RP, 6, RT, E])
        gate_s = sb("gate_s", [RP, 6, RT])
        gtop = sb("gtop", [RP, RT, 8])
        gall = sb("gall", [RP, RT, E + 6])
        gout = sb("gout", [RP, RT, E + 6])
        gate_t = sb("gate_t", [E, UC])
        htok = sb("htok", [NT, UB, D])
        outtext = sb("outtext", [SEQT, UB, D])

        pA = ctx.enter_context(nc.psum_tensor("pA", [128, 2, 512], F32))
        pB = ctx.enter_context(nc.psum_tensor("pB", [128, 2, 512], F32))
        pS = ctx.enter_context(nc.psum_tensor("pS", [128, 2, 512], F32))
        pP = ctx.enter_context(nc.psum_tensor("pP", [128, 2, 512], F32))
        PTL = 4
        pAu, pBu = pA[:, :, 0:HC], pB[:, :, 0:HC]

        CREDIT = 3
        names_n = ("qxl_ready", "qx_ready", "scores_done", "max_ready", "exp_done", "rden_ready", "norm_ready",
                   "pt_done", "pt_act", "pt_dve", "ctx_done", "ctx_ready")
        (qxl_ready, qx_ready, scores_done, max_ready, exp_done, rden_ready, norm_ready,
         pt_done, pt_act, pt_dve, ctx_done, ctx_ready) = n_sems = [sem(n) for n in names_n]
        l_sel, l_selt, l_selc, l_w, l_sm = l_sems = [sem(n) for n in ("l_sel", "l_selt", "l_selc", "l_w", "l_sm")]
        s_const, s_shared, s_tokw, s_text = (sem(n) for n in ("s_const", "s_shared", "s_tokw", "s_text"))
        s_textrow = sem("s_textrow")
        s_patch = [sem(f"s_patch{i}") for i in range(2)]
        s_eatt = [sem(f"s_eatt{i}") for i in range(2)]
        s_effn = [sem(f"s_effn{i}") for i in range(2)]
        s_out = sem("s_out")
        s_init = sem("s_init")
        s_dve = sem("s_dve")
        (e_mm0, e_mm1, e_ev, u_oh, u_oht, u_cnt, u_cnt_t, u_cnt4, u_n0, u_ln, u_lnn,
         n1_c, n1_sq, n1_v, n1_r, n1_x, l_q, l_qe, l_k, l_ke, l_kt, l_kte, l_v, l_ve, l_kc, l_kce,
         l_pr, l_hb, n2_c, n2_sq, n2_v, n2_r, n2_x, g_key, g_keye, g_sc, g_max, g_exp, g_gate, g_gt, g_gte,
         g_b2, g_acc, o_t, o_te, o_x, o_xe, o_st) = (sem(n) for n in (
             "e_mm0", "e_mm1", "e_ev", "u_oh", "u_oht", "u_cnt", "u_cnt_t", "u_cnt4", "u_n0", "u_ln", "u_lnn",
             "n1_c", "n1_sq", "n1_v", "n1_r", "n1_x", "l_q", "l_qe", "l_k", "l_ke", "l_kt", "l_kte", "l_v", "l_ve",
             "l_kc", "l_kce", "l_pr", "l_hb", "n2_c", "n2_sq", "n2_v", "n2_r", "n2_x", "g_key", "g_keye", "g_sc",
             "g_max", "g_exp", "g_gate", "g_gt", "g_gte", "g_b2", "g_acc", "o_t", "o_te", "o_x", "o_xe", "o_st"))
        (a_q, a_k, a_qf, a_kf, a_qh, a_kh, a_ql, a_kl, a_v, a_ve,
         f_wo, f_y, f_c1, f_sq1, f_v1, f_r1, f_z, f_x1, f_h2, f_y2, f_c2, f_sq2, f_v2, f_r2, f_g, f_rg, f_t, f_acc,
         f_bvoe, f_bvo) = (
            sem(n) for n in (
                "a_q", "a_k", "a_qf", "a_kf", "a_qh", "a_kh", "a_ql", "a_kl", "a_v", "a_ve",
                "f_wo", "f_y", "f_c1", "f_sq1", "f_v1", "f_r1", "f_z", "f_x1", "f_h2", "f_y2", "f_c2", "f_sq2",
                "f_v2", "f_r2", "f_g", "f_rg", "f_t", "f_acc", "f_bvoe", "f_bvo"))
        f_w1 = [[sem(f"f_w1_{i}_{k}") for k in range(2)] for i in range(FCH)]
        f_ge = [[sem(f"f_ge_{i}_{k}") for k in range(2)] for i in range(FCH)]
        f_l1, f_l2, n1_l, n2_l = (sem(n) for n in ("f_l1", "f_l2", "n1_l", "n2_l"))
        f_w2p = [sem(f"f_w2p_{i}") for i in range(FCH)]
        l_den, g_top, g_msk, g_rec, u_lne = (sem(n) for n in ("l_den", "g_top", "g_msk", "g_rec", "u_lne"))
        passed_dve, passed_pe = sem("passed_dve"), sem("passed_pe")
        t_chain = sem("t_chain")
        u_chain = sem("u_chain")

        def cc(name, p=128, a=0, b=None):
            lo, hi = CCOL[name]
            return const[0:p, lo + a:(hi if b is None else lo + b)]

        def sc(name, p=128, a=0, b=None):
            lo, hi = SCOL[name]
            return shared[0:p, lo + a:(hi if b is None else lo + b)]

        def ea(par, name, a=0, b=None):
            lo, hi = ACOL[name]
            return eatt[par][:, lo + a:(hi if b is None else lo + b)]

        def ef(par, name, a=0, b=None, p=128):
            lo, hi = FCOL[name]
            return effn[par][0:p, lo + a:(hi if b is None else lo + b)]

        def halves(t):
            return t.rearrange("p (k c) -> p k c", k=2)

        block = ctx.enter_context(nc.Block())

        @block.sync
        def _(sp):
            sp.dma_start(const[:, :], const_in).then_inc(s_const, 16)
            sp.dma_start(tokw[:, :, :], tokw_in).then_inc(s_tokw, 16)
            for hf in range(2):
                sp.dma_start(patches[:, hf], x_in[0, hf]).then_inc(s_patch[hf], 16)
            sp.dma_start(shared[:, :], shared_in).then_inc(s_shared, 16)
            sp.dma_start(text_i[:, :], xt_in).then_inc(s_text, 16)

            def unit(u, last):
                sp.wait_ge(o_x, u)
                sp.wait_ge(u_oht, u)
                sp.dma_start(textrow[:, :], xr_in[bass.ds(u, 1), :].broadcast_to((NT, UB * SEQT))).then_inc(s_textrow, 16)
                for e in range(E):
                    par = e % 2
                    if e < 2:
                        sp.wait_ge(a_v, u * 8)
                        sp.wait_ge(a_k, u * 8)
                    else:
                        sp.wait_ge(a_v, u * 8 + e - 1)
                    sp.wait_ge(a_qf, u * 8 + max(e - 1, 0))
                    sp.wait_ge(a_qh, u * 8 + max(e - 1, 0))
                    sp.wait_ge(a_kf, u * 8 + max(e - 1, 0))
                    sp.wait_ge(a_kh, u * 8 + max(e - 1, 0))
                    sp.dma_start(eatt[par][:, :], eatt_in[e]).then_inc(s_eatt[par], 16)
                    sp.wait_ge(f_acc, u * 8 + max(e - 1, 0))
                    sp.dma_start(effn[par][:, :], effn_in[e]).then_inc(s_effn[par], 16)
                    if e == 1 and not last:
                        for hf in range(2):
                            sp.wait_ge((e_mm0, e_mm1)[hf], u + 1)
                            sp.dma_start(patches[:, hf], x_in[bass.ds(u + 1, 1), hf].rearrange("a p k c -> (a p) k c")).then_inc(s_patch[hf], 16)
                sp.wait_ge(o_te, u + 1)
                sp.dma_start(out[bass.ds(u * UB, UB), 0:T0, :].rearrange("b t d -> t b d"), htok[0:T0, :, :]).then_inc(s_out, 16)
                sp.wait_ge(o_xe, u + 1)
                sp.dma_start(out[bass.ds(u * UB, UB), T0:SEQ, :].rearrange("b t d -> t b d"), outtext[:, :, :]).then_inc(s_out, 16)

            with sp.Fori(0, NU - 1) as u:
                unit(u, False)
            unit(NU - 1, True)
            sp.wait_ge(s_out, NU * 32)

        @block.tensor
        def _(pe):
            mm = nc.tensor.matmul

            def over_halves(psum, lhsT, rhs, start=True, stop=True):
                for k in range(2):
                    last = mm(psum[:, k, 0:HC], lhsT, halves(rhs)[:, k], start=start, stop=stop)
                return last

            def transpose_probs(N, b):
                pe.wait_ge(norm_ready, N + b + 1 + CREDIT)
                pe.wait_ge(pt_act, N + b + CREDIT)
                for j in range(RT):
                    o = pS[0:NT, b % 2, j * RP:(j + 1) * RP] if j < PTL else pP[0:NT, 0, 0:RP]
                    last = nc.tensor.transpose(o, probs[0:RP, b % 3, j, 0:NT], cc("I", RP, 0, RP))
                last.then_inc(pt_done, 1)

            def weigh_values(N, b):
                pe.wait_ge(pt_act, N + b + 1 + CREDIT)
                pe.wait_ge(pt_dve, N + b + 1 + CREDIT)
                pe.wait_ge(ctx_ready, N + b + CREDIT)
                for h in range(H):
                    s = 32 * (h % 4)
                    at = (h // 4) * NT
                    last = mm(pP[s:s + 32, 1, at:at + NT], vtok[:, b * D + h * DH:b * D + h * DH + 32],
                              probs_t[:, b % 2, h * NT:(h + 1) * NT], start=True, stop=True, tile_position=(0, s))
                last.then_inc(ctx_done, 1)

            def scores(N, b):
                pe.wait_ge(qx_ready, N + b + 1 + CREDIT)
                pe.wait_ge(qxl_ready, N + b + 1 + CREDIT)
                pe.wait_ge(pt_dve, N + b - 1 + CREDIT)
                mm(pS[:, b % 2, 0:RT * NT], ones16[0:3, :], lnn[:, b:b + 1, :].broadcast_to((3, RT, NT)), start=True, stop=False,
                   skip_group_check=True)
                for j in range(RT):
                    o = pS[:, b % 2, j * NT:(j + 1) * NT]
                    rows = slice(j * RP, j * RP + 128)
                    cols = slice(b * NT, (b + 1) * NT)
                    mm(o, qxh[:, b % 2, rows], kh[:, cols], start=False, stop=False, skip_group_check=True)
                    mm(o, qxh[:, b % 2, rows], kl[:, cols], start=False, stop=False, skip_group_check=True)
                    last = mm(o, qxl[:, b % 2, rows], kh[:, cols], start=False, stop=True, skip_group_check=True)
                last.then_inc(scores_done, 1)

            def project(G, par, wait_att):
                wait_att()
                last = over_halves(pA, ea(par, "wq"), xn[:, :])
                last.then_inc(a_q, 1)
                last = over_halves(pB, ea(par, "wk"), xn[:, :])
                last.then_inc(a_k, 1)
                pe.wait_ge(a_qf, G + 1)
                pe.wait_ge(a_qh, G + 1)
                for b in range(UB):
                    last = mm(pA[0:NT, b // 4, (b % 4) * D:(b % 4 + 1) * D], xn[:, b * NT:(b + 1) * NT], ea(par, "wv"),
                              start=True, stop=True)
                last.then_inc(a_v, 1)

            def ffn_step(G, par, k):
                if k == 0:
                    for g2 in range(2):
                        last = mm(pB[:, 0, HC:HC + 1], ef(par, "wo", g2 * D, (g2 + 1) * D), ef(par, "bv", g2, g2 + 1),
                                  start=(g2 == 0), stop=(g2 == 1))
                    last.then_inc(f_bvo, 1)
                    for half in range(2):
                        for g2 in range(2):
                            rhs = cx[:, par, g2, half * 4:half * 4 + 4, :].rearrange("p b t -> p (b t)")
                            last = mm(pA[:, half, 0:HC], ef(par, "wo", g2 * D, (g2 + 1) * D), rhs,
                                      start=(g2 == 0), stop=(g2 == 1))
                    last.then_inc(f_wo, 1)
                elif k == 1:
                    pe.wait_ge(f_y, G)
                    over_halves(pB, cc("C"), y[:, :]).then_inc(f_c1, 1)
                elif k == 2:
                    pe.wait_ge(f_sq1, G)
                    over_halves(pA, cc("J"), sqf[:, :]).then_inc(f_v1, 1)
                elif k == 4:
                    pe.wait_ge(f_x1, G)
                    for c in range(FCH + 1):
                        for hf in range(2):
                            if c >= 1:
                                pe.wait_ge(f_ge[c - 1][hf], G)
                            if c < FCH:
                                mm(pA[:, hf, 0:HC], ef(par, "w1", c * D, (c + 1) * D), halves(x1[:, :])[:, hf],
                                   start=True, stop=True).then_inc(f_w1[c][hf], 1)
                            if c >= 1:
                                last = mm(pB[:, hf, 0:HC], ef(par, "w2", (c - 1) * D, c * D), halves(g[:, (c - 1) % 2, :])[:, hf],
                                          start=(c == 1), stop=(c == FCH), skip_group_check=True)
                        if c >= 1:
                            last.then_inc(f_w2p[c - 1], 1)
                elif k == 6:
                    pe.wait_ge(f_y2, G)
                    over_halves(pA, cc("C"), y[:, :]).then_inc(f_c2, 1)
                elif k == 7:
                    pe.wait_ge(f_sq2, G)
                    over_halves(pB, cc("J"), sqf[:, :]).then_inc(f_v2, 1)
                elif k == 9:
                    pe.wait_ge(f_l2, G)
                    over_halves(pB, ef(par, "pick", p=E), gate_t[:, :]).then_inc(f_g, 1)

            def steps(NBr, Gf, parf):
                for i in range(NSTEP):
                    if NBr is not None:
                        if 0 <= i - 2 < UB:
                            transpose_probs(NBr, i - 2)
                        if 0 <= i - 3 < UB:
                            weigh_values(NBr, i - 3)
                        if i < UB:
                            scores(NBr, i)
                    if Gf is not None:
                        ffn_step(Gf, parf, i)

            pe.wait_ge(s_const, 16)
            pe.wait_ge(s_tokw, 16)
            pe.wait_ge(s_shared, 16)
            pe.wait_ge(s_init, 1)
            with pe.Fori(0, NU) as u:
                for hf in range(2):
                    pe.wait_ge(s_patch[hf], (u + 1) * 16)
                    if hf == 0:
                        pe.wait_ge(f_t, u * 8)
                        pe.wait_ge(o_te, u)
                    for j in range(KJ):
                        last = mm(pA[:, hf, 0:4 * NP], tokw[:, j, :], patches[:, hf, j, :], start=(j == 0), stop=(j == KJ - 1))
                    last.then_inc((e_mm0, e_mm1)[hf], 1)
                pe.wait_ge(u_oh, u + 1)
                pe.wait_ge(o_xe, u)
                pe.wait_ge(f_rg, u * 8)
                for k in range(2):
                    last = mm(pB[0:SEGS, k, 0:4 * NTP], segof[:, :], onehot[:, 4 * k:4 * k + 4, :].rearrange("p b t -> p (b t)"),
                              start=True, stop=True)
                last.then_inc(u_cnt, 1)
                for b in range(UB):
                    last = mm(pS[0:NTP, 0, b * SEGS:(b + 1) * SEGS], onehot[:, b, :], segof[:, :], start=True, stop=True)
                last = mm(pS[0:3, 1, 0:UB * NCLS], ones16[:, 0:3], onehot[:, :, T0:NT], start=True, stop=True)
                last.then_inc(u_n0, 1)
                pe.wait_ge(e_ev, 2 * u + 2)
                pe.wait_ge(u_cnt_t, u + 1)
                over_halves(pB, cc("C"), hA[:, :, :].rearrange("p b t -> p (b t)")).then_inc(n1_c, 1)
                pe.wait_ge(n1_sq, u + 1)
                over_halves(pA, cc("J"), sq[:, :]).then_inc(n1_v, 1)
                pe.wait_ge(n1_x, u + 1)
                over_halves(pA, sc("wq"), xn[:, :]).then_inc(l_q, 1)
                over_halves(pB, sc("wk"), xn[:, :]).then_inc(l_k, 1)
                pe.wait_ge(l_qe, u + 1)
                for b in range(UB):
                    last = mm(pA[0:NT, b // 4, (b % 4) * D:(b % 4 + 1) * D], xn[:, b * NT:(b + 1) * NT], sc("wk"), start=True, stop=True)
                last.then_inc(l_kt, 1)
                pe.wait_ge(l_kte, u + 1)
                pe.wait_ge(l_ke, u + 1)
                for b in range(UB):
                    last = mm(pA[0:NT, b // 4, (b % 4) * D:(b % 4 + 1) * D], xn[:, b * NT:(b + 1) * NT], sc("wv"), start=True, stop=True)
                last.then_inc(l_v, 1)
                pe.wait_ge(u_cnt4, u + 1)
                for b in range(UB):
                    last = mm(pB[:, 0, b * SEGS:(b + 1) * SEGS], ktok[:, b * D:(b + 1) * D], count4[0:NT, b, :], start=True, stop=True)
                last.then_inc(l_kc, 1)
                pe.wait_ge(l_kce, u + 1)
                pe.wait_ge(l_ve, u + 1)
                pe.wait_ge(u_lnn, u + 1)
                NB = pe.snap(u * 72)
                LB = pe.snap(u * 8)
                for i in range(NSTEP):
                    b = i - 1
                    if 0 <= b < UB:
                        pe.wait_ge(l_sel, LB + b + 1)
                        pe.wait_ge(l_selc, LB + b)
                        pe.sem_inc(passed_pe, 1)
                        pt = pB[0:SEGS, 0, 0:RT * RP // 2].bitcast(BF16)
                        for j in range(RT):
                            last = nc.tensor.transpose(pt[:, j * RP:(j + 1) * RP], chosen[0:RP, j, :], ident16[0:RP, 0:RP])
                        last.then_inc(l_selt, 1)
                    b = i - 2
                    if 0 <= b < UB:
                        transpose_probs(NB, b)
                    b = i - 1
                    if 0 <= b < UB:
                        pe.wait_ge(l_selc, LB + b + 1)
                        pe.wait_ge(rden_ready, NB + b + CREDIT)
                        for j in range(RT):
                            last = mm(pB[:, 1, j * NTP:(j + 1) * NTP], chosen_t[:, j * RP:j * RP + 128], count_t[:, b, :], start=True, stop=True)
                        last.then_inc(l_w, 1)
                    b = i - 3
                    if 0 <= b < UB:
                        weigh_values(NB, b)
                    b = i
                    if b < UB:
                        pe.wait_ge(qx_ready, NB + b + 1 + CREDIT)
                        pe.wait_ge(pt_dve, NB + b - 1 + CREDIT)
                        if b >= 2:
                            pe.wait_ge(l_sel, LB + b - 1)
                        mm(pA[:, b % 2, 0:RT * RW], ones16[0:1, :], sentinel[:, :, :].rearrange("p j w -> p (j w)"),
                           start=True, stop=False, skip_group_check=True)
                        for j in range(RT):
                            rows = slice(j * RP, j * RP + 128)
                            mm(pA[:, b % 2, j * RW:(j + 1) * RW], qxf[:, b % 2, rows], klm[:, b, NTP:NTP + RW],
                               start=False, stop=True, skip_group_check=True)
                            last = mm(pS[:, b % 2, j * NTP:(j + 1) * NTP], qxf[:, b % 2, rows], klm[:, b, 0:NTP], start=True, stop=True)
                        last.then_inc(scores_done, 1)
                pe.wait_ge(ctx_ready, NB + UB + CREDIT)
                for half in range(2):
                    for g2 in range(2):
                        last = mm(pA[:, half, 0:HC], sc("wp", 128, g2 * D, (g2 + 1) * D),
                                  cx[:, 1, g2, half * 4:half * 4 + 4, :].rearrange("p b t -> p (b t)"), start=(g2 == 0), stop=(g2 == 1))
                last.then_inc(l_pr, 1)
                pe.wait_ge(l_hb, u + 1)
                over_halves(pB, cc("C"), hB[:, :]).then_inc(n2_c, 1)
                pe.wait_ge(n2_sq, u + 1)
                over_halves(pA, cc("J"), sq[:, :]).then_inc(n2_v, 1)
                pe.wait_ge(n2_x, u + 1)
                over_halves(pA, sc("gwk"), xn[:, :]).then_inc(g_key, 1)
                pe.wait_ge(g_keye, u + 1)
                for j in range(RT):
                    last = mm(pS[0:RP, 0, j * E:(j + 1) * E], qf[:, j * RP:(j + 1) * RP], sc("eq"), start=True, stop=True)
                last.then_inc(g_sc, 1)
                pe.wait_ge(g_gate, u + 1)
                for j in range(RT):
                    last = nc.tensor.transpose(pP[0:E, j // 4, (j % 4) * RP:(j % 4 + 1) * RP], gate[:, 5, j, :], cc("I", RP, 0, RP))
                last.then_inc(g_gt, 1)
                pe.wait_ge(g_gte, 2 * u + 2)
                over_halves(pA, sc("be2", E), gate_t[:, :]).then_inc(g_b2, 1)
                pe.wait_ge(g_acc, u + 1)

                def attention(N, G, par):
                    project(G, par, lambda: pe.wait_ge(s_eatt[par], 16 * (u * 4 + 1)))
                    pe.wait_ge(a_kl, G + 1)
                    pe.wait_ge(a_ve, G + 1)
                    steps(N, None, None)

                def both(N, G, par, wait_count):
                    pe.wait_ge(f_t, G - 1)
                    pe.wait_ge(f_rg, G - 1)
                    project(G, par, lambda: pe.wait_ge(s_eatt[par], wait_count))
                    pe.wait_ge(a_kl, G + 1)
                    pe.wait_ge(a_kf, G + 1)
                    pe.wait_ge(a_kh, G + 1)
                    pe.wait_ge(a_ve, G + 1)
                    pe.wait_ge(s_effn[1 - par], wait_count if par == 1 else wait_count - 16)
                    pe.wait_ge(ctx_ready, N + CREDIT)
                    steps(N, G, 1 - par)

                attention(pe.snap(u * 72 + 8), pe.snap(u * 8), 0)
                with pe.Fori(0, 3) as t:
                    both(pe.snap(u * 72 + 16 + t * 16), pe.snap(u * 8 + 1 + t * 2), 1, 16 * (u * 4 + t + 1))
                    both(pe.snap(u * 72 + 24 + t * 16), pe.snap(u * 8 + 2 + t * 2), 0, 16 * (u * 4 + t + 2))
                both(pe.snap(u * 72 + 64), pe.snap(u * 8 + 7), 1, 16 * (u * 4 + 4))
                pe.wait_ge(f_t, u * 8 + 7)
                pe.wait_ge(f_rg, u * 8 + 7)
                pe.wait_ge(a_ve, u * 8 + 8)
                pe.wait_ge(s_effn[1], 16 * (u * 4 + 4))
                pe.wait_ge(ctx_ready, u * 72 + 72 + CREDIT)
                steps(None, pe.snap(u * 8 + 8), 1)
                pe.wait_ge(f_acc, u * 8 + 8)
                for b in range(UB):
                    last = nc.tensor.transpose(pA[0:NT, b // 4, (b % 4) * D:(b % 4 + 1) * D], acc[:, b * NT:(b + 1) * NT], cc("I"))
                last.then_inc(o_t, 1)
                pe.wait_ge(o_te, u + 1)
                pe.wait_ge(u_oht, u + 1)
                for b in range(UB):
                    last = mm(pB[:, b // 4, (b % 4) * D:(b % 4 + 1) * D], onehot_t[:, b, :], htok[:, b, :], start=True, stop=True)
                last.then_inc(o_x, 1)

        @block.scalar
        def _(act):
            def A(out_, in_, f, **kw):
                return nc.scalar.activation(out_, in_, f, **kw)

            def evac_probs(N, b):
                act.wait_ge(pt_done, N + b + 1 + CREDIT)
                act.wait_ge(ctx_done, N + b - 1 + CREDIT)
                A(probs_t[:, b % 2, PTL * RP:RT * RP], pP[0:NT, 0, 0:RP], ACT.Copy).then_inc(pt_act, 1)

            def evac_ctx(N, b, par):
                act.wait_ge(ctx_done, N + b + 1 + CREDIT)
                A(cx[:, par, :, b, :], pP[:, 1, 0:2 * NT].rearrange("p (g t) -> p g t", g=2), ACT.Copy)\
                    .then_inc(ctx_ready, 1)

            def exps(N, b):
                act.wait_ge(max_ready, N + b + 1 + CREDIT)
                act.wait_ge(pt_done, N + b - 2 + CREDIT)
                act.wait_ge(norm_ready, N + b - 2 + CREDIT)
                for j in range(RT):
                    last = A(probs[0:RP, b % 3, j, 0:NT], pS[0:RP, b % 2, j * NT:(j + 1) * NT], ACT.Exp,
                             bias=negmax[0:RP, b % 2, j:j + 1], accum_out=den[0:RP, b % 3, j:j + 1])
                last.then_inc(exp_done, 1)

            def project(G, par):
                act.wait_ge(a_q, G + 1)
                A(qf[:, :].rearrange("p (k c) -> p k c", k=2), pAu, ACT.Identity, bias=ea(par, "bq"), scale=1.0).then_inc(a_qf, 1)
                act.wait_ge(a_kf, G + 1)
                A(kh[:, :], kf[:, :], ACT.Copy).then_inc(a_kh, 1)
                act.wait_ge(a_v, G + 1)
                A(vtok[:, 0:UB * D].rearrange("p (k c) -> p k c", k=2), pA[0:NT, :, :], ACT.Copy).then_inc(a_ve, 1)

            def rstd(psum, buf, v, l, r, n):
                act.wait_ge(v, n)
                A(halves(buf[:, :]), psum, ACT.Ln, bias=epsc[:, 0:1]).then_inc(l, 1)
                act.wait_ge(l, n)
                A(buf[:, :], buf[:, :], ACT.Exp, scale=-0.5).then_inc(r, 1)

            def ffn_step(G, par, k):
                if k == 1:
                    act.wait_ge(f_c1, G)
                    A(halves(sqf[:, :]), pBu, ACT.Square).then_inc(f_sq1, 1)
                elif k == 2:
                    rstd(pAu, rsf, f_v1, f_l1, f_r1, G)
                elif k == 4:
                    act.preload_act_table_set("gelu_and_others")
                    for c in range(FCH):
                        if c >= 2:
                            act.wait_ge(f_w2p[c - 2], G)
                        for hf in range(2):
                            act.wait_ge(f_w1[c][hf], G)
                            A(halves(g[:, c % 2, :])[:, hf], pA[:, hf, 0:HC], ACT.Gelu, bias=ef(par, "bf1", c, c + 1)).then_inc(f_ge[c][hf], 1)
                    act.wait_ge(f_w2p[FCH - 1], G)
                    A(halves(z[:, :]), pBu, ACT.Gelu, bias=ef(par, "bf2")).then_inc(f_h2, 1)
                    act.preload_act_table_set(LN_EXP)
                elif k == 6:
                    act.wait_ge(f_c2, G)
                    A(halves(sqf[:, :]), pAu, ACT.Square).then_inc(f_sq2, 1)
                elif k == 7:
                    rstd(pBu, rsf, f_v2, f_l2, f_r2, G)

            def steps(NBr, par, Gf):
                for i in range(NSTEP):
                    if NBr is not None:
                        if 0 <= i - 2 < UB:
                            evac_probs(NBr, i - 2)
                        if 0 <= i - 3 < UB:
                            evac_ctx(NBr, i - 3, par)
                        if i < UB:
                            exps(NBr, i)
                    if Gf is not None:
                        ffn_step(Gf, 1 - par, i)

            for s in (exp_done, pt_act, ctx_ready):
                act.sem_inc(s, CREDIT)
            act.wait_ge(s_const, 16)
            act.wait_ge(s_init, 1)
            act.preload_act_table_set(LN_EXP)
            with act.Fori(0, NU) as u:
                act.wait_ge(u_ln, u + 1)
                A(lnw[:, 2, :], lnw[:, 1, :], ACT.Ln).then_inc(u_lne, 1)
                act.wait_ge(n1_c, u + 1)
                A(halves(sq[:, :]), pBu, ACT.Square).then_inc(n1_sq, 1)
                rstd(pAu, rs, n1_v, n1_l, n1_r, u + 1)
                act.wait_ge(l_kt, u + 1)
                A(ktok[:, :].rearrange("p (k c) -> p k c", k=2), pA[0:NT, :, :], ACT.Copy).then_inc(l_kte, 1)
                act.wait_ge(l_v, u + 1)
                A(vtok[:, 0:UB * D].rearrange("p (k c) -> p k c", k=2), pA[0:NT, :, :], ACT.Copy).then_inc(l_ve, 1)
                act.wait_ge(l_kc, u + 1)
                A(klm[:, :, NTP:NTP + SEGS], pB[:, 0, :].rearrange("p (b m) -> p b m", b=UB), ACT.Copy).then_inc(l_kce, 1)
                NB = act.snap(u * 72)
                LB = act.snap(u * 8)
                for i in range(NSTEP):
                    b = i - 1
                    if 0 <= b < UB:
                        act.wait_ge(l_selt, LB + b + 1)
                        act.wait_ge(l_w, LB + b)
                        A(chosen_t[:, 0:RT * RP], pB[0:SEGS, 0, 0:RT * RP // 2].bitcast(BF16), ACT.Copy).then_inc(l_selc, 1)
                    if 0 <= i - 2 < UB:
                        evac_probs(NB, i - 2)
                    if 0 <= i - 3 < UB:
                        evac_ctx(NB, i - 3, 1)
                    b = i - 1
                    if 0 <= b < UB:
                        act.wait_ge(l_sm, LB + b + 1)
                        A(probs[0:RP, b % 3, :, :], probs[0:RP, b % 3, :, :], ACT.Exp).then_inc(exp_done, 1)
                act.wait_ge(n2_c, u + 1)
                A(halves(sq[:, :]), pBu, ACT.Square).then_inc(n2_sq, 1)
                rstd(pAu, rs, n2_v, n2_l, n2_r, u + 1)
                act.wait_ge(g_max, u + 1)
                A(gate[:, 1], gate[:, 0], ACT.Exp, scale=float(D) ** -0.5).then_inc(g_exp, 1)

                def attention(N, G, par, count):
                    act.wait_ge(s_eatt[par], count)
                    project(G, par)
                    steps(N, par, None)

                def both(N, G, par, count):
                    act.wait_ge(s_eatt[par], count)
                    act.wait_ge(s_effn[1 - par], count if par == 1 else count - 16)
                    act.wait_ge(ctx_done, N + CREDIT)
                    project(G, par)
                    steps(N, par, G)

                attention(act.snap(u * 72 + 8), act.snap(u * 8), 0, 16 * (u * 4 + 1))
                with act.Fori(0, 3) as t:
                    both(act.snap(u * 72 + 16 + t * 16), act.snap(u * 8 + 1 + t * 2), 1, 16 * (u * 4 + t + 1))
                    both(act.snap(u * 72 + 24 + t * 16), act.snap(u * 8 + 2 + t * 2), 0, 16 * (u * 4 + t + 2))
                both(act.snap(u * 72 + 64), act.snap(u * 8 + 7), 1, 16 * (u * 4 + 4))
                act.wait_ge(s_effn[1], 16 * (u * 4 + 4))
                steps(None, 0, act.snap(u * 8 + 8))
                act.wait_ge(o_t, u + 1)
                act.wait_ge(s_out, u * 32)
                A(htok[:, :, :].rearrange("p (k b) d -> p k (b d)", k=2), pA[0:NT, :, :], ACT.Copy).then_inc(o_te, 1)

        @block.gpsimd
        def _(pool):
            pool.sem_inc(norm_ready, CREDIT)
            pool.sem_inc(qxl_ready, CREDIT)
            pool.wait_ge(s_init, 1)

            def norm(N, b, w):
                pool.wait_ge(rden_ready, N + b + 1 + CREDIT)
                p = probs[0:RP, b % 3, :, 0:w]
                nc.gpsimd.tensor_tensor(p, p, rden[0:RP, b % 3, :, None].broadcast_to((RP, RT, w)), ALU.mult).then_inc(norm_ready, 1)

            def mask_low(N, b):
                pool.wait_ge(scores_done, N + b - 1 + CREDIT)
                nc.gpsimd.tensor_tensor(qxl[:, b % 2, 0:H * NT].rearrange("p (h t) -> p h t", h=H), mask16[:, :, :],
                                        ql[:, None, b * NT:(b + 1) * NT].broadcast_to((128, H, NT)), ALU.mult).then_inc(qxl_ready, 1)

            with pool.Fori(0, NU) as u:
                NB = pool.snap(u * 72)
                for b in range(UB):
                    norm(NB, b, NTP)
                    pool.sem_inc(qxl_ready, 1)
                with pool.Fori(0, E) as e:
                    N = pool.snap(u * 72 + 8 + e * 8)
                    pool.wait_ge(a_ql, u * 8 + e + 1)
                    for i in range(UB + 2):
                        if i < UB:
                            mask_low(N, i)
                        if i >= 2:
                            norm(N, i - 2, NT)

        @block.vector
        def _(dve):
            V = nc.vector
            for s in (qx_ready, scores_done, max_ready, rden_ready, pt_done, pt_dve, ctx_done):
                dve.sem_inc(s, CREDIT)

            def bc(ap, dim, n):
                shape = list(ap.shape)
                shape[dim] = n
                return ap.broadcast_to(tuple(shape))

            dve.wait_ge(s_const, 16)
            dve.wait_ge(s_shared, 16)
            dve.wait_ge(s_text, 16)
            n = 0
            for ins in (
                lambda: V.tensor_copy(segof[:, :], cc("A")),
                lambda: V.tensor_copy(ident16[:, :], cc("I")),
                lambda: V.tensor_scalar(mask16[:, :, :].rearrange("p h t -> p (h t)"), cc("mask"), SCALE, None, ALU.mult),
                lambda: V.tensor_scalar(maskf[:, :, :].rearrange("p h t -> p (h t)"), cc("mask"), SCALE, None, ALU.mult),
                lambda: V.memset(ones16[:, :], 1.0),
                lambda: V.memset(sentinel[:, :, 0:SEGS], 0.0),
                lambda: V.memset(sentinel[:, :, SEGS:RW], 1e38),
                lambda: V.memset(epsc[:, :], EPS),
                lambda: V.memset(lnn[:, :, :], 0.0),
                lambda: V.memset(qxh[:, :, :], 0.0),
                lambda: V.memset(qxl[:, :, :], 0.0),
                lambda: V.memset(qxf[:, :, :], 0.0),
                lambda: V.memset(klm[:, :, :], 0.0),
                lambda: V.memset(chosen_t[:, :], 0.0),
                lambda: V.memset(vtok[:, UB * D:], 0.0),
                lambda: V.memset(gall[:, :, 0:6], 4.0),
                lambda: V.tensor_copy(text_f[:, :], text_i[:, :]),
                lambda: V.tensor_scalar(hA[:, :, 0:1], bc(sc("pos", 128, 0, 1)[:, None, :], 1, UB), sc("cls"), None, ALU.mult),
                lambda: V.tensor_scalar(hA[:, :, T0:NT], bc(sc("txtw")[:, None, :], 1, UB), sc("txtb"), None, ALU.add),
            ):
                n += 1
                ins().then_inc(s_dve, 1)
            dve.wait_ge(s_dve, n)
            dve.sem_inc(s_init, 1)

            def mask_high(N, b):
                dve.wait_ge(scores_done, N + b - 1 + CREDIT)
                V.tensor_tensor(qxh[:, b % 2, 0:H * NT].rearrange("p (h t) -> p h t", h=H), mask16[:, :, :],
                                bc(qh[:, None, b * NT:(b + 1) * NT], 1, H), ALU.mult).then_inc(qx_ready, 1)

            def negmax_of(N, b):
                dve.wait_ge(scores_done, N + b + 1 + CREDIT)
                dve.wait_ge(exp_done, N + b - 1 + CREDIT)
                V.tensor_reduce(negmax[0:RP, b % 2, :], pS[0:RP, b % 2, 0:RT * NT].rearrange("p (j t) -> p j t", j=RT),
                                AX, ALU.max, negate=True).then_inc(max_ready, 1)

            def recip(N, b):
                dve.wait_ge(exp_done, N + b + 1 + CREDIT)
                dve.wait_ge(norm_ready, N + b - 2 + CREDIT)
                V.reciprocal(rden[0:RP, b % 3, :], den[0:RP, b % 3, :]).then_inc(rden_ready, 1)

            def evac_probs(N, b):
                dve.wait_ge(pt_done, N + b + 1 + CREDIT)
                dve.wait_ge(ctx_done, N + b - 1 + CREDIT)
                V.tensor_copy(probs_t[:, b % 2, 0:PTL * RP], pS[0:NT, b % 2, 0:PTL * RP]).then_inc(pt_dve, 1)

            def project(G, par):
                dve.wait_ge(a_qf, G + 1)
                V.tensor_copy(qh[:, :], qf[:, :]).then_inc(a_qh, 1)
                dve.wait_ge(a_k, G + 1)
                V.tensor_scalar(halves(kf[:, :]), pBu, ea(par, "bk"), None, ALU.add).then_inc(a_kf, 1)
                dve.wait_ge(a_qh, G + 1)
                V.tensor_tensor(ql[:, :], qf[:, :], qh[:, :], ALU.subtract).then_inc(a_ql, 1)
                dve.wait_ge(a_kf, G + 1)
                dve.wait_ge(a_kh, G + 1)
                V.tensor_tensor(kl[:, :], kf[:, :], kh[:, :], ALU.subtract).then_inc(a_kl, 1)

            def ffn_step(G, par, k):
                if k == 0:
                    dve.wait_ge(f_bvo, G)
                    V.tensor_tensor(bvo[:, 0:1], pB[:, 0, HC:HC + 1], ef(par, "bo"), ALU.add).then_inc(f_bvoe, 1)
                    dve.wait_ge(f_bvoe, G)
                    dve.wait_ge(f_wo, G)
                    V.scalar_tensor_tensor(halves(y[:, :]), pAu, bvo[:, 0:1], halves(xn[:, :]), ALU.add, ALU.add).then_inc(f_y, 1)
                elif k == 2:
                    dve.wait_ge(f_r1, G)
                    V.tensor_tensor(halves(z[:, :]), pBu, halves(rsf[:, :]), ALU.mult).then_inc(f_z, 1)
                    dve.wait_ge(f_z, G)
                    V.tensor_scalar(x1[:, :], z[:, :], ef(par, "g1"), ef(par, "be1"), ALU.mult, ALU.add).then_inc(f_x1, 1)
                elif k == 5:
                    dve.wait_ge(f_h2, G)
                    V.tensor_tensor(y[:, :], z[:, :], x1[:, :], ALU.add).then_inc(f_y2, 1)
                elif k == 9:
                    dve.wait_ge(f_g, G)
                    dve.wait_ge(f_r2, G)
                    V.tensor_tensor(halves(rsf[:, :]), pBu, halves(rsf[:, :]), ALU.mult).then_inc(f_rg, 1)
                    dve.wait_ge(f_rg, G)
                    V.tensor_tensor(halves(z[:, :]), pAu, halves(rsf[:, :]), ALU.mult).then_inc(f_t, 1)
                    dve.wait_ge(f_t, G)
                    V.scalar_tensor_tensor(acc[:, :], z[:, :], ef(par, "g2"), acc[:, :], ALU.mult, ALU.add).then_inc(f_acc, 1)

            def steps(NBr, par, Gf):
                if NBr is not None:
                    mask_high(NBr, 0)
                for i in range(NSTEP):
                    if NBr is not None:
                        if 0 <= i - 1 < UB:
                            recip(NBr, i - 1)
                        if 0 <= i - 2 < UB:
                            evac_probs(NBr, i - 2)
                        if i + 1 < UB:
                            mask_high(NBr, i + 1)
                        if i < UB:
                            negmax_of(NBr, i)
                    if Gf is not None:
                        ffn_step(Gf, 1 - par, i)

            NLINK = 5
            NUCH = 15

            with dve.Fori(0, NU) as u:
                CH = dve.snap(u * NUCH)
                links = [0]

                def link(ins, own=False):
                    links[0] += 1
                    ins.then_inc(u_chain, 1)
                    dve.wait_ge(u_chain, CH + links[0])
                    if own:
                        dve.sem_inc(passed_dve, 1)

                dve.wait_ge(u_n0, u)
                dve.wait_ge(u_cnt, u)
                V.tensor_tensor(onehot[:, :, :], bc(text_f[:, bass.ds(u * UB, UB)][:, :, None], 2, NTP), bc(cc("tcol")[:, None, :], 1, UB),
                                ALU.is_equal).then_inc(u_oh, 1)
                dve.wait_ge(s_textrow, u * 16 + 16)
                dve.wait_ge(o_x, u)
                V.tensor_scalar(onehot_t[:, :, :].rearrange("p b j -> p (b j)"), textrow[:, :], cc("tval", NT), None, ALU.is_equal)\
                    .then_inc(u_oht, 1)
                dve.wait_ge(u_cnt, u + 1)
                for k in range(2):
                    last = V.tensor_tensor(count_t[:, 4 * k:4 * k + 4, :], pB[0:SEGS, k, 0:4 * NTP].rearrange("p (b t) -> p b t", b=4),
                                           bc(cc("MT", SEGS)[:, None, :], 1, 4), ALU.add)
                last.then_inc(u_cnt_t, 1)
                dve.wait_ge(u_n0, u + 1)
                V.scalar_tensor_tensor(count4[:, :, :], pS[0:NTP, 0, :].rearrange("p (b m) -> p b m", b=UB), 1.0 / SEGL,
                                       bc(cc("M4", NTP)[:, None, :], 1, UB), ALU.mult, ALU.add).then_inc(u_cnt4, 1)
                link(V.tensor_copy(lnw[:, 0, :], pS[0:3, 1, 0:UB * NCLS]))
                V.tensor_scalar(lnw[:, 1, :], lnw[:, 0, :], 1.0, None, ALU.max).then_inc(u_ln, 1)
                link(V.tensor_scalar(lnw[:, 3, :], lnw[:, 0, :], 0.5, -1e30, ALU.is_lt, ALU.mult))
                dve.wait_ge(u_lne, u + 1)
                link(V.tensor_tensor(lnw[:, 4, :], lnw[:, 2, :], lnw[:, 3, :], ALU.add))
                link(V.tensor_copy(lnpart[:, 0, :], lnw[:, 4, :]))
                link(V.tensor_tensor(lnw[:, 5, :], lnw[:, 4, :], lnpart[:, 0, :], ALU.subtract))
                link(V.tensor_copy(lnpart[:, 1, :], lnw[:, 5, :]))
                link(V.tensor_tensor(lnpart[:, 2, :], lnw[:, 5, :], lnpart[:, 1, :], ALU.subtract))
                link(V.tensor_scalar(lnw[:, 6, :], lnpart[:, 0, :], cc("I", 3, 0, 1), None, ALU.mult))
                link(V.scalar_tensor_tensor(lnw[:, 7, :], lnpart[:, 1, :], cc("I", 3, 1, 2), lnw[:, 6, :], ALU.mult, ALU.add))
                V.scalar_tensor_tensor(lnn[:, :, T0:NT], lnpart[:, 2, :].rearrange("p (b c) -> p b c", b=UB), cc("I", 3, 2, 3),
                                       lnw[:, 7, :].rearrange("p (b c) -> p b c", b=UB), ALU.mult, ALU.add).then_inc(u_lnn, 1)
                for hf in range(2):
                    dve.wait_ge((e_mm0, e_mm1)[hf], u + 1)
                    V.scalar_tensor_tensor(hA[:, 4 * hf:4 * hf + 4, 1:T0], pA[:, hf, 0:4 * NP].rearrange("p (b t) -> p b t", b=4),
                                           sc("tokb"), bc(sc("pos", 128, 1, 1 + NP)[:, None, :], 1, 4), ALU.add, ALU.mult)\
                        .then_inc(e_ev, 1)
                dve.wait_ge(n1_r, u + 1)
                V.tensor_tensor(halves(xn[:, :]), pBu, halves(rs[:, :]), ALU.mult).then_inc(n1_x, 1)
                dve.wait_ge(l_q, u + 1)
                V.tensor_copy(halves(qf[:, :]), pAu).then_inc(l_qe, 1)
                dve.wait_ge(l_k, u + 1)
                for k in range(2):
                    last = V.tensor_copy(klm[:, 4 * k:4 * k + 4, 0:NT], pB[:, k, 0:HC].rearrange("p (b t) -> p b t", b=4))
                last.then_inc(l_ke, 1)
                dve.wait_ge(l_qe, u + 1)
                NB = dve.snap(u * 72)
                LB = dve.snap(u * 8)
                TB = dve.snap(u * (8 * NLINK))

                def mask_f(b):
                    dve.wait_ge(scores_done, NB + b - 1 + CREDIT)
                    V.tensor_tensor(qxf[:, b % 2, 0:H * NT].rearrange("p (h t) -> p h t", h=H),
                                    maskf[:, :, :],
                                    bc(qf[:, None, b * NT:(b + 1) * NT], 1, H), ALU.mult).then_inc(qx_ready, 1)

                mask_f(0)
                tl = [0]

                def tlink(ins, own=False):
                    tl[0] += 1
                    ins.then_inc(t_chain, 1)
                    dve.wait_ge(t_chain, TB + tl[0])
                    if own:
                        dve.sem_inc(passed_dve, 1)

                def choose(b):
                    dve.wait_ge(scores_done, NB + b + 1 + CREDIT)
                    dve.sem_inc(passed_dve, 1)
                    for j in range(RT):
                        last = V.max(top8[0:RP, j, :], pA[0:RP, b % 2, j * RW:(j + 1) * RW])
                    tlink(last, own=True)
                    for j in range(RT):
                        last = V.match_replace(routed[0:RP, j, :], top8[0:RP, j, :], pA[0:RP, b % 2, j * RW:(j + 1) * RW], -3e38)
                    tlink(last)
                    dve.wait_ge(l_selt, LB + b)
                    V.tensor_scalar(chosen[0:RP, :, :], routed[0:RP, :, 0:SEGS], -2e38, None, ALU.is_le).then_inc(l_sel, 1)

                def key_counts(b):
                    return pB[0:RP, 1, 0:RT * NTP].rearrange("p (j t) -> p j t", j=RT)

                def scores_of_chosen(b):
                    dve.wait_ge(l_w, LB + b + 1)
                    s = pS[0:RP, b % 2, 0:RT * NTP].rearrange("p (j t) -> p j t", j=RT)
                    tlink(V.tensor_scalar(pen[0:RP, :, :], key_counts(b), 0.0, -1e30, ALU.is_equal, ALU.mult))
                    tlink(V.tensor_tensor(pen[0:RP, :, :], pen[0:RP, :, :], s, ALU.add))
                    tlink(V.tensor_reduce(negmax[0:RP, b % 2, :], pen[0:RP, :, :], AX, ALU.max, negate=True))
                    dve.wait_ge(pt_done, NB + b - 2 + CREDIT)
                    V.tensor_tensor(probs[0:RP, b % 3, :, :], pen[0:RP, :, :], bc(negmax[0:RP, b % 2, :, None], 2, NTP), ALU.add)\
                        .then_inc(l_sm, 1)

                def weigh(b):
                    p = probs[0:RP, b % 3, :, :]
                    dve.wait_ge(exp_done, NB + b + 1 + CREDIT)
                    V.tensor_tensor(p, p, key_counts(b), ALU.mult).then_inc(max_ready, 1)
                    dve.wait_ge(max_ready, NB + b + 1 + CREDIT)
                    V.tensor_reduce(den[0:RP, b % 3, :], p, AX, ALU.add).then_inc(l_den, 1)
                    dve.wait_ge(l_den, LB + b + 1)
                    V.reciprocal(rden[0:RP, b % 3, :], den[0:RP, b % 3, :]).then_inc(rden_ready, 1)

                for i in range(NSTEP):
                    if i + 1 < UB:
                        mask_f(i + 1)
                    if 0 <= i - 2 < UB:
                        evac_probs(NB, i - 2)
                    if 0 <= i - 1 < UB:
                        scores_of_chosen(i - 1)
                    if i < UB:
                        choose(i)
                    if 0 <= i - 1 < UB:
                        weigh(i - 1)
                dve.wait_ge(l_pr, u + 1)
                V.scalar_tensor_tensor(halves(hB[:, :]), pAu, sc("bp"), halves(hA[:, :, :].rearrange("p b t -> p (b t)")), ALU.add, ALU.add)\
                    .then_inc(l_hb, 1)
                dve.wait_ge(n2_r, u + 1)
                V.tensor_tensor(halves(xn[:, :]), pBu, halves(rs[:, :]), ALU.mult).then_inc(n2_x, 1)
                dve.wait_ge(g_key, u + 1)
                V.tensor_scalar(halves(qf[:, :]), pAu, sc("gbk"), None, ALU.add).then_inc(g_keye, 1)
                dve.wait_ge(g_sc, u + 1)
                s = pS[0:RP, 0, 0:RT * E].rearrange("p (j e) -> p j e", j=RT)
                link(V.tensor_reduce(gate_s[:, 0, :], s, AX, ALU.max, negate=True))
                V.tensor_tensor(gate[:, 0], s, bc(gate_s[:, 0, :, None], 2, E), ALU.add).then_inc(g_max, 1)
                dve.wait_ge(g_exp, u + 1)
                link(V.tensor_reduce(gate_s[:, 1, :], gate[:, 1], AX, ALU.add))
                link(V.reciprocal(gate_s[:, 2, :], gate_s[:, 1, :]))
                link(V.tensor_tensor(gall[:, :, 6:6 + E], gate[:, 1], bc(gate_s[:, 2, :, None], 2, E), ALU.mult), own=True)
                for j in range(RT):
                    last = V.max(gtop[:, j, :], gall[:, j, :])
                last.then_inc(g_top, 1)
                dve.wait_ge(g_top, 2 * u + 1)
                dve.sem_inc(passed_dve, 1)
                for j in range(RT):
                    last = V.match_replace(gout[:, j, :], gtop[:, j, :], gall[:, j, :], -1.0)
                last.then_inc(g_top, 1)
                dve.wait_ge(g_top, 2 * u + 2)
                V.scalar_tensor_tensor(gate[:, 2], gout[:, :, 6:6 + E], 0.0, gall[:, :, 6:6 + E], ALU.is_lt, ALU.mult).then_inc(g_msk, 1)
                dve.wait_ge(g_msk, u + 1)
                link(V.tensor_reduce(gate_s[:, 3, :], gate[:, 2], AX, ALU.add))
                link(V.tensor_scalar(gate_s[:, 4, :], gate_s[:, 3, :], 1e-9, None, ALU.add))
                V.reciprocal(gate_s[:, 5, :], gate_s[:, 4, :]).then_inc(g_rec, 1)
                dve.wait_ge(g_rec, u + 1)
                V.tensor_tensor(gate[:, 5], gate[:, 2], bc(gate_s[:, 5, :, None], 2, E), ALU.mult).then_inc(g_gate, 1)
                assert links[0] == NUCH, links
                dve.wait_ge(g_gt, u + 1)
                V.tensor_copy(gate_t[:, 0:4 * RP], pP[0:E, 0, 0:4 * RP]).then_inc(g_gte, 1)
                V.tensor_copy(gate_t[:, 4 * RP:RT * RP], pP[0:E, 1, 0:RP]).then_inc(g_gte, 1)
                dve.wait_ge(g_b2, u + 1)
                V.tensor_tensor(halves(acc[:, :]), pAu, halves(hB[:, :]), ALU.add).then_inc(g_acc, 1)

                def attention(N, G, par, count):
                    dve.wait_ge(s_eatt[par], count)
                    project(G, par)
                    steps(N, par, None)

                def both(N, G, par, count):
                    dve.wait_ge(s_eatt[par], count)
                    dve.wait_ge(s_effn[1 - par], count if par == 1 else count - 16)
                    project(G, par)
                    steps(N, par, G)

                attention(dve.snap(u * 72 + 8), dve.snap(u * 8), 0, 16 * (u * 4 + 1))
                with dve.Fori(0, 3) as t:
                    both(dve.snap(u * 72 + 16 + t * 16), dve.snap(u * 8 + 1 + t * 2), 1, 16 * (u * 4 + t + 1))
                    both(dve.snap(u * 72 + 24 + t * 16), dve.snap(u * 8 + 2 + t * 2), 0, 16 * (u * 4 + t + 2))
                both(dve.snap(u * 72 + 64), dve.snap(u * 8 + 7), 1, 16 * (u * 4 + 4))
                dve.wait_ge(s_effn[1], 16 * (u * 4 + 4))
                steps(None, 0, dve.snap(u * 8 + 8))
                dve.wait_ge(o_x, u + 1)
                dve.wait_ge(s_out, u * 32)
                V.tensor_copy(outtext[:, :, :].rearrange("p (k b) d -> p k (b d)", k=2), pB[:, :, :]).then_inc(o_xe, 1)


def kernel(**inputs):
    import numpy as np
    import concourse.bacc as bacc
    from concourse.bass_utils import run_bass_kernel_spmd

    a = {k: np.asarray(v) for k, v in inputs.items()}
    f32 = np.float32

    def strips(wt):
        w = wt.reshape(2, 4, DH, -1)
        o = np.zeros((2, 4, 32, w.shape[-1]), f32)
        o[:, :, :DH] = w
        return o.reshape(2, 128, -1).transpose(1, 0, 2)

    def put(shape_cols, width, parts):
        blk = np.zeros((128, width), f32)
        for name, v in parts.items():
            lo, hi = shape_cols[name]
            v = np.asarray(v)
            blk[:v.shape[0], lo:hi] = v.reshape(v.shape[0], -1)
        return blk

    pos_of = np.arange(SEQT)
    seg_of = (T0 + pos_of) // SEGL
    A = np.zeros((SEQT, SEGS), f32)
    A[pos_of, seg_of] = 1
    M = np.zeros((NTP, SEGS), f32)
    for t in range(T0):
        M[t, t // SEGL] += 1
    for t in range(SEQ, SEGS * SEGL):
        M[NT, t // SEGL] += 1
    tval = np.full((NTP,), -1.0, f32)
    tval[T0:NT] = np.arange(NCLS)
    mask = (np.arange(128)[:, None] // DH == np.arange(H)[None]).astype(f32)
    const = put(CCOL, CW, dict(
        C=np.eye(128, dtype=f32) - f32(1 / 128), J=np.full((128, 128), 1 / 128, f32), I=np.eye(128, dtype=f32),
        mask=np.repeat(mask, NT, axis=1), A=A, tcol=np.tile(tval, (128, 1)), M4=M / SEGL, MT=M.T, tval=tval[:, None]))
    wqkv = a["L0_attn_w_qkv"].reshape(3, D, D)
    shared = put(SCOL, SW, dict(
        wq=wqkv[0].T, wk=wqkv[1].T, wv=wqkv[2].T, wp=strips(a["L0_attn_w_proj"].T), gwk=a["L0_ffn_gate_Wk"].T,
        eq=a["L0_ffn_expert_queries"].T, be2=a["L0_ffn_be2"], pos=a["L0_tok_pos_embed"].T, txtw=a["L0_txt_W"],
        bp=a["L0_attn_b_proj"][:, None], tokb=a["L0_tok_b"][:, None], cls=a["L0_tok_class_token"].T,
        txtb=a["L0_txt_b"][:, None], gbk=a["L0_ffn_gate_bk"][:, None]))
    tokw = np.ascontiguousarray(a["L0_tok_W"].T.reshape(KJ, KP, D).transpose(1, 0, 2))
    eatt, effn = [], []
    for e in range(E):
        w, bqkv = a["L0_ffn_Wqkv"][e].reshape(3, D, D), a["L0_ffn_bqkv"][e].reshape(3, D, 1)
        eatt.append(put(ACOL, AW, dict(wq=w[0].T, wk=w[1].T, wv=w[2].T, bq=bqkv[0], bk=bqkv[1])))
        pick = np.zeros((E, D), f32)
        pick[e] = 1
        effn.append(put(FCOL, FW, dict(
            wo=strips(a["L0_ffn_Wo"][e].T), w1=a["L0_ffn_W1"][e].T,
            w2=a["L0_ffn_W2"][e].T.reshape(FCH, D, D).transpose(1, 0, 2), pick=pick, bv=strips(bqkv[2])[:, :, 0],
            bo=a["L0_ffn_bo"][e][:, None], g1=a["L0_ffn_g1"][e][:, None], be1=a["L0_ffn_be1"][e][:, None],
            bf1=a["L0_ffn_bf1"][e].reshape(FCH, D).T, bf2=a["L0_ffn_bf2"][e][:, None], g2=a["L0_ffn_g2"][e][:, None])))
    x = a["x"].reshape(NU, 2, 4, 3, 8, 28, 8, 28).transpose(0, 1, 3, 5, 7, 2, 4, 6).reshape(NU, 2, KJ, KP, 4 * NP)
    arrays = dict(x_in=np.ascontiguousarray(x.transpose(0, 1, 3, 2, 4)), xt_in=np.ascontiguousarray(a["x_txt"].T),
                  xr_in=np.ascontiguousarray(a["x_txt"].reshape(NU, UB * SEQT)), const_in=const, shared_in=shared,
                  tokw_in=tokw, eatt_in=np.stack(eatt), effn_in=np.stack(effn))
    nc = bacc.Bacc("TRN2", target_bir_lowering=False, num_devices=1)
    args = [nc.dram_tensor(k, v.shape, mybir.dt.from_np(v.dtype), kind="ExternalInput").ap() for k, v in arrays.items()]
    args.append(nc.dram_tensor("out", (B, SEQ, D), F32, kind="ExternalOutput").ap())
    build(nc, *args)
    r = run_bass_kernel_spmd(nc, [arrays], core_ids=[0])
    return r.results[0]["out"]
```

```python
from contextlib import ExitStack

import concourse.bass as bass
from concourse import mybir

F32 = mybir.dt.float32
F16 = mybir.dt.float16
BF16 = mybir.dt.bfloat16
I32 = mybir.dt.int32
ALU = mybir.AluOpType
ACT = mybir.ActivationFunctionType
AX = mybir.AxisListType.X

B = 64
D = 128
H = 8
DH = D // H
NP = 64
NCLS = 5
SEQT = 128
SEQ = 1 + NP + SEQT
NT = 1 + NP + NCLS
NTP = NT + 1
T0 = 1 + NP
SEGS = 64
SEGL = -(-SEQ // SEGS)
TOPK = 4
NSENT = 8 - TOPK
RW = SEGS + NSENT
UB = 8
NU = B // UB
UC = UB * NT
HC = UC // 2
RP = 112
RT = H * NT // RP
QC = H * NT + 128 - RP
E = 8
F = 512
FCH = F // D
KP = 112
KJ = 3 * 28 * 28 // KP
SCALE = DH ** -0.5
LN_EXP = "natural_log_exp_and_others"
EPS = 1e-5
NSTEP = UB + 4
WITHIN = {6: 0}
EMBED_FROM = 0
NPART = 3

CONST = dict(C=D, J=D, I=D, mask=H * NT, A=SEGS, tcol=NTP, M4=SEGS, MT=NTP, tval=1)
SHARED = dict(wq=D, wk=D, wv=D, wp=D, gwk=D, eq=E, be2=D, pos=1 + NP, txtw=NCLS,
              bp=1, tokb=1, cls=1, txtb=1, gbk=1)
EATT = dict(wq=D, wk=D, wv=D, bq=1, bk=1, bv=1)
EFFN = dict(wo=D, w1=F, w2=F, pick=D, bo=1, g1=1, be1=1, bf1=FCH, bf2=1, g2=1)


def columns(block):
    at, out = 0, {}
    for name, n in block.items():
        out[name] = (at, at + n)
        at += n
    return out, at


CCOL, CW = columns(CONST)
SCOL, SW = columns(SHARED)
ACOL, AW = columns(EATT)
FCOL, FW = columns(EFFN)


def build(nc, x_in, xt_in, xr_in, const_in, shared_in, tokw_in, eatt_in, effn_in, out):
    with ExitStack() as ctx:
        def sb(name, shape, dt=F32):
            return ctx.enter_context(nc.sbuf_tensor(name, shape, dt))

        def sem(name):
            return ctx.enter_context(nc.semaphore(name))

        const = sb("const", [128, CW])
        shared = sb("shared", [128, SW])
        tokw = sb("tokw", [KP, KJ, D])
        patches = sb("patches", [KP, 2, KJ, 4 * NP])
        eatt = [sb(f"eatt{i}", [128, AW]) for i in range(2)]
        effn = [sb(f"effn{i}", [128, FW]) for i in range(2)]
        text_i = sb("text_i", [128, B], I32)
        text_f = sb("text_f", [128, B])
        textrow = sb("textrow", [NT, UB * SEQT], I32)
        onehot = sb("onehot", [128, UB, NTP], BF16)
        onehot_t = sb("onehot_t", [NT, UB, SEQT])
        segof = sb("segof", [128, SEGS], BF16)
        ident16 = sb("ident16", [128, 128], BF16)
        maskf = sb("maskf", [128, H, NT])
        mask16 = sb("mask16", [128, H, NT], F16)
        ones16 = sb("ones16", [128, 128], BF16)
        sentinel = sb("sentinel", [1, RT, RW], BF16)
        count_t = sb("count_t", [SEGS, UB, NTP], BF16)
        count4 = sb("count4", [NTP, UB, SEGS])
        lnw = sb("lnw", [3, 8, UB * NCLS])
        lnn = sb("lnn", [3, UB, NT], BF16)
        lnpart = sb("lnpart", [3, 3, UB * NCLS], BF16)
        hA = sb("hA", [128, UB, NT])
        hB = sb("hB", [128, UC])
        xn = sb("xn", [128, UC])
        sq = sb("sq", [128, UC])
        sqf = sb("sqf", [128, UC])
        rs = sb("rs", [128, UC])
        rsf = sb("rsf", [128, UC])
        qf = sb("qf", [128, UC])
        kf = sb("kf", [128, UC])
        qh = sb("qh", [128, 2, UC], F16)
        ql = sb("ql", [128, 2, UC], F16)
        kh = sb("kh", [128, 2, UC], F16)
        kl = sb("kl", [128, 2, UC], F16)
        qxh = sb("qxh", [128, 2, QC], F16)
        qxl = sb("qxl", [128, 2, QC], F16)
        qxf = sb("qxf", [128, 3, QC])
        klm = sb("klm", [128, UB, NTP + RW])
        ktok = sb("ktok", [NT, UB * D])
        vtok = [sb(f"vtok{i}", [NT, UB * H // 2, 64]) for i in range(2)]
        top8 = sb("top8", [128, RT, 8])
        routed = sb("routed", [128, RT, RW])
        chosen = sb("chosen", [128, RT, SEGS], BF16)
        chosen_t = sb("chosen_t", [SEGS, QC], BF16)
        pen = sb("pen", [128, RT, NTP])
        kept = sb("kept", [128, RT, NTP])
        negmax = sb("negmax", [128, 2, RT])
        den = sb("den", [128, 4, RT])
        rden = sb("rden", [128, 4, RT])
        probs = sb("probs", [128, 4, RT, NTP])
        probs_t = sb("probs_t", [NT, 2, H * NT])
        cx = sb("cx", [128, 2, UB, NT])
        bvc = sb("bvc", [128, 2])
        cwo = sb("cwo", [128, D + 1])
        pick16 = sb("pick16", [NPART * E, D], BF16)
        epsc = sb("epsc", [128, 1])
        bigneg = sb("bigneg", [128, 1])
        y = sb("y", [128, UC])
        z = sb("z", [128, UC])
        x1 = sb("x1", [128, UC])
        g = sb("g", [128, 2, UC])
        acc = sb("acc", [128, UC])
        gate = sb("gate", [RP, 6, RT, E])
        gate_s = sb("gate_s", [RP, 6, RT])
        gtop = sb("gtop", [RP, RT, 8])
        gall = sb("gall", [RP, RT, E + 6])
        gout = sb("gout", [RP, RT, E + 6])
        gpart = sb("gpart", [RP, NPART, RT, E], BF16)
        gsum = sb("gsum", [RP, RT, NPART, E])
        gate_t = sb("gate_t", [NPART * E, UC])
        gate_t16 = sb("gate_t16", [NPART * E, UC], BF16)
        htok = sb("htok", [NT, UB, D])
        outtext = sb("outtext", [SEQT, UB, D])

        pA = ctx.enter_context(nc.psum_tensor("pA", [128, 2, 512], F32))
        pB = ctx.enter_context(nc.psum_tensor("pB", [128, 2, 512], F32))
        pS = ctx.enter_context(nc.psum_tensor("pS", [128, 2, 512], F32))
        pP = ctx.enter_context(nc.psum_tensor("pP", [128, 2, 512], F32))
        PTL = 4
        PR0 = 256
        pAu, pBu = pA[:, :, 0:HC], pB[:, :, 0:HC]

        CREDIT = 3
        names_n = ("qxl_ready", "qx_ready", "scores_done", "neg_ready", "den_ready", "max_ready", "exp_done", "rden_ready", "norm_ready",
                   "pt_done", "pt_rest", "pt_main", "ctx_done", "ctx_ready")
        (qxl_ready, qx_ready, scores_done, neg_ready, den_ready, max_ready, exp_done, rden_ready, norm_ready,
         pt_done, pt_rest, pt_main, ctx_done, ctx_ready) = n_sems = [sem(n) for n in names_n]
        l_r, l_mr, l_sel, l_selt, l_selc, l_w, l_pen, l_sm = (
            sem(n) for n in ("l_r", "l_mr", "l_sel", "l_selt", "l_selc", "l_w", "l_pen", "l_sm"))
        s_const, s_shared, s_tokw, s_text = (sem(n) for n in ("s_const", "s_shared", "s_tokw", "s_text"))
        s_textrow = sem("s_textrow")
        s_patch = [sem(f"s_patch{i}") for i in range(2)]
        s_eatt = [sem(f"s_eatt{i}") for i in range(2)]
        s_effn = [sem(f"s_effn{i}") for i in range(2)]
        s_out = sem("s_out")
        s_init = sem("s_init")
        s_dve = sem("s_dve")
        (e_mm0, e_mm1, e_ev, u_oh, u_oht, u_cnt, u_cnt_t, u_cnt4, u_n0, u_ln, u_lnn,
         n1_c, n1_sq, n1_v, n1_r, n1_x, l_q, l_qe, l_k, l_ke, l_kt, l_kte, l_v, l_ve, l_kc, l_kce,
         l_pr, l_hb, n2_c, n2_sq, n2_v, n2_r, n2_x, g_key, g_keye, g_sc, g_max, g_exp, g_gate, g_gt, g_gte,
         g_b2, g_acc, o_t, o_te, o_x, o_xe, o_st) = (sem(n) for n in (
             "e_mm0", "e_mm1", "e_ev", "u_oh", "u_oht", "u_cnt", "u_cnt_t", "u_cnt4", "u_n0", "u_ln", "u_lnn",
             "n1_c", "n1_sq", "n1_v", "n1_r", "n1_x", "l_q", "l_qe", "l_k", "l_ke", "l_kt", "l_kte", "l_v", "l_ve",
             "l_kc", "l_kce", "l_pr", "l_hb", "n2_c", "n2_sq", "n2_v", "n2_r", "n2_x", "g_key", "g_keye", "g_sc",
             "g_max", "g_exp", "g_gate", "g_gt", "g_gte", "g_b2", "g_acc", "o_t", "o_te", "o_x", "o_xe", "o_st"))
        (a_q, a_k, a_qf, a_kf, a_qh, a_kh, a_ql, a_kl, a_v, a_ve,
         f_wo, f_y, f_c1, f_sq1, f_v1, f_r1, f_z, f_x1, f_h2, f_y2, f_c2, f_sq2, f_v2, f_r2, f_g, f_rg, f_t, f_acc,
         a_bv, f_cw, f_cwe, f_pick) = (
            sem(n) for n in (
                "a_q", "a_k", "a_qf", "a_kf", "a_qh", "a_kh", "a_ql", "a_kl", "a_v", "a_ve",
                "f_wo", "f_y", "f_c1", "f_sq1", "f_v1", "f_r1", "f_z", "f_x1", "f_h2", "f_y2", "f_c2", "f_sq2",
                "f_v2", "f_r2", "f_g", "f_rg", "f_t", "f_acc", "a_bv", "f_cw", "f_cwe", "f_pick"))
        f_w1 = [[sem(f"f_w1_{i}_{k}") for k in range(2)] for i in range(FCH)]
        f_ge = [[sem(f"f_ge_{i}_{k}") for k in range(2)] for i in range(FCH)]
        f_l1, f_l2, n1_l, n2_l = (sem(n) for n in ("f_l1", "f_l2", "n1_l", "n2_l"))
        f_w2p = [sem(f"f_w2p_{i}") for i in range(FCH)]
        g_top, g_msk, g_rec, g_gated, u_lne = (sem(n) for n in ("g_top", "g_msk", "g_rec", "g_gated", "u_lne"))
        passed_dve, passed_pe, passed_pool = (sem(n) for n in ("passed_dve", "passed_pe", "passed_pool"))
        l_top, l_kept = sem("l_top"), sem("l_kept")
        u_chain = sem("u_chain")

        def cc(name, p=128, a=0, b=None):
            lo, hi = CCOL[name]
            return const[0:p, lo + a:(hi if b is None else lo + b)]

        def sc(name, p=128, a=0, b=None):
            lo, hi = SCOL[name]
            return shared[0:p, lo + a:(hi if b is None else lo + b)]

        def ea(par, name, a=0, b=None):
            lo, hi = ACOL[name]
            return eatt[par][:, lo + a:(hi if b is None else lo + b)]

        def ef(par, name, a=0, b=None, p=128):
            lo, hi = FCOL[name]
            return effn[par][0:p, lo + a:(hi if b is None else lo + b)]

        def halves(t):
            return t.rearrange("p (k c) -> p k c", k=2)

        block = ctx.enter_context(nc.Block())

        @block.sync
        def _(sp):
            sp.dma_start(const[:, :], const_in).then_inc(s_const, 16)
            sp.dma_start(tokw[:, :, :], tokw_in).then_inc(s_tokw, 16)
            for hf in range(2):
                sp.dma_start(patches[:, hf], x_in[0, hf]).then_inc(s_patch[hf], 16)
            sp.dma_start(shared[:, :], shared_in).then_inc(s_shared, 16)
            sp.dma_start(text_i[:, :], xt_in).then_inc(s_text, 16)

            def unit(u, last):
                sp.wait_ge(o_x, u)
                sp.wait_ge(u_oht, u)
                sp.dma_start(textrow[:, :], xr_in[bass.ds(u, 1), :].broadcast_to((NT, UB * SEQT))).then_inc(s_textrow, 16)
                def load_att(e):
                    sp.wait_ge(a_kf, u * 8 + max(e - 1, 0))
                    sp.wait_ge(a_ve, u * 8 + max(e - 1, 0))
                    sp.dma_start(eatt[e % 2][:, :], eatt_in[e]).then_inc(s_eatt[e % 2], 16)

                load_att(0)
                load_att(1)
                for e in range(E):
                    sp.wait_ge(f_acc, u * 8 + max(e - 1, 0))
                    sp.dma_start(effn[e % 2][:, :], effn_in[e]).then_inc(s_effn[e % 2], 16)
                    if e + 2 < E:
                        load_att(e + 2)
                    if e == 1 and not last:
                        for hf in range(2):
                            sp.wait_ge((e_mm0, e_mm1)[hf], u + 1)
                            sp.dma_start(patches[:, hf], x_in[bass.ds(u + 1, 1), hf].rearrange("a p k c -> (a p) k c")).then_inc(s_patch[hf], 16)
                sp.wait_ge(o_te, u + 1)
                sp.dma_start(out[bass.ds(u * UB, UB), 0:T0, :].rearrange("b t d -> t b d"), htok[0:T0, :, :]).then_inc(s_out, 16)
                sp.wait_ge(o_xe, u + 1)
                sp.dma_start(out[bass.ds(u * UB, UB), T0:SEQ, :].rearrange("b t d -> t b d"), outtext[:, :, :]).then_inc(s_out, 16)

            with sp.Fori(0, NU - 1) as u:
                unit(u, False)
            unit(NU - 1, True)
            sp.wait_ge(s_out, NU * 32)

        @block.tensor
        def _(pe):
            mm = nc.tensor.matmul

            def over_halves(psum, lhsT, rhs, start=True, stop=True):
                for k in range(2):
                    last = mm(psum[:, k, 0:HC], lhsT, halves(rhs)[:, k], start=start, stop=stop)
                return last

            def weigh_values(N, b, par):
                img = b % UB
                pe.wait_ge(pt_main, N + b + 1 + CREDIT)
                pe.wait_ge(pt_rest, N + b + 1 + CREDIT)
                pe.wait_ge(ctx_ready, N + b + CREDIT)
                for h in range(H):
                    s = 32 * (h // 2)
                    v = vtok[par][:, img * H // 2 + h // 2, 32 * (h % 2):32 * (h % 2) + 32]
                    last = mm(pP[s:s + 32, 1, 0:NT], v, probs_t[:, b % 2, h * NT:(h + 1) * NT],
                              start=(h % 2 == 0), stop=(h % 2 == 1), tile_position=(0, s))
                last.then_inc(ctx_done, 1)

            def transpose_probs(N, b):
                pe.wait_ge(norm_ready, N + b + 1 + CREDIT)
                pe.wait_ge(pt_main, N + b + CREDIT)
                pe.wait_ge(pt_rest, N + b + CREDIT)
                pe.wait_ge(ctx_ready, N + b - 1 + CREDIT)
                for j in reversed(range(RT)):
                    o = pP[0:NT, 0, j * RP:(j + 1) * RP] if j < PTL else pP[0:NT, 1, PR0:PR0 + RP]
                    last = nc.tensor.transpose(o, probs[0:RP, b % 4, j, 0:NT], cc("I", RP, 0, RP))
                last.then_inc(pt_done, 1)

            def scores(N, b, par):
                pe.wait_ge(qx_ready, N + b + 1 + CREDIT)
                pe.wait_ge(qxl_ready, N + b + 1 + CREDIT)
                pe.wait_ge(max_ready, N + b - 1 + CREDIT)
                mm(pS[:, b % 2, 0:RT * NT], ones16[0:3, :], lnn[:, b:b + 1, :].broadcast_to((3, RT, NT)), start=True, stop=False,
                   skip_group_check=True)
                for j in range(RT):
                    o = pS[:, b % 2, j * NT:(j + 1) * NT]
                    rows = slice(j * RP, j * RP + 128)
                    cols = slice(b * NT, (b + 1) * NT)
                    mm(o, qxh[:, b % 2, rows], kh[:, par, cols], start=False, stop=False, skip_group_check=True)
                    mm(o, qxh[:, b % 2, rows], kl[:, par, cols], start=False, stop=False, skip_group_check=True)
                    last = mm(o, qxl[:, b % 2, rows], kh[:, par, cols], start=False, stop=True, skip_group_check=True)
                last.then_inc(scores_done, 1)

            def project_qk(par):
                over_halves(pA, ea(par, "wq"), xn[:, :]).then_inc(a_q, 1)
                over_halves(pB, ea(par, "wk"), xn[:, :]).then_inc(a_k, 1)

            def project_v(par):
                for b in range(UB):
                    last = mm(pA[0:NT, b // 4, (b % 4) * D:(b % 4 + 1) * D], xn[:, b * NT:(b + 1) * NT], ea(par, "wv"),
                              start=True, stop=True)
                last.then_inc(a_v, 1)

            def embed(u, c):
                hf, j = c // KJ, c % KJ
                if j == 0:
                    pe.wait_ge(s_patch[hf], (u + 1) * 16)
                done = mm(pS[:, hf, 0:4 * NP], tokw[:, j, :], patches[:, hf, j, :], start=(j == 0), stop=(j == KJ - 1))
                if j == KJ - 1:
                    done.then_inc((e_mm0, e_mm1)[hf], 1)

            def gate_rows(G):
                pe.wait_ge(f_l2, G)
                pe.wait_ge(f_pick, G)
                over_halves(pB, pick16[:, :], gate_t16[:, :]).then_inc(f_g, 1)

            def body(N, G, par, next_weights, ffn_weights, att=True, closing=True, next_unit=None):
                ffn = ffn_weights is not None

                def attend(i):
                    if att:
                        scores(N, i, par)
                    if (-3 if ffn else 0) <= i - 3 < (UB if att else 0):
                        weigh_values(N, i - 3, par if i >= 3 else 1 - par)
                    if (-2 if ffn else 0) <= i - 2 < (UB if att else 0):
                        transpose_probs(N, i - 2)

                if att:
                    pe.wait_ge(a_kl, G + 1)
                    pe.wait_ge(a_kh, G + 1)
                    pe.wait_ge(a_ve, G + 1)
                for i in range(UB):
                    if not (ffn and i in WITHIN):
                        attend(i)
                    if i == 0 and closing:
                        gate_rows(G - 1)
                    if next_unit is not None and i >= EMBED_FROM:
                        if i == EMBED_FROM:
                            pe.wait_ge(max_ready, N + CREDIT)
                        n = UB - EMBED_FROM
                        for c in range((i - EMBED_FROM) * 2 * KJ // n, (i - EMBED_FROM + 1) * 2 * KJ // n):
                            embed(next_unit, c)
                    if i == 1:
                        if ffn:
                            pe.wait_ge(s_effn[1 - par], ffn_weights)
                            pe.wait_ge(f_t, G - 1)
                            mm(pA[:, 0, HC:HC + D], ef(1 - par, "wo"), cc("C"), start=True, stop=True)
                            mm(pA[:, 0, HC + D:HC + D + 1], cc("C"), ef(1 - par, "bo"), start=True, stop=True).then_inc(f_cw, 1)
                        if next_weights is not None:
                            pe.wait_ge(s_eatt[1 - par], next_weights)
                            project_qk(1 - par)
                    if i == 2 and next_weights is not None:
                        pe.wait_ge(a_qf, G + 2)
                        if ffn:
                            pe.wait_ge(f_cwe, G)
                        project_v(1 - par)
                    if not ffn:
                        continue
                    if i == 3:
                        pe.wait_ge(ctx_ready, N + CREDIT)
                        pe.wait_ge(f_cwe, G)
                        if next_weights is not None:
                            pe.wait_ge(a_kf, G + 2)
                        over_halves(pB, cwo[:, 0:D], cx[:, 1 - par, :, :].rearrange("p b t -> p (b t)")).then_inc(f_wo, 1)
                    elif i == 4:
                        pe.wait_ge(f_sq1, G)
                        if next_weights is not None:
                            pe.wait_ge(a_ve, G + 2)
                        over_halves(pA, cc("J"), sqf[:, :]).then_inc(f_v1, 1)
                    elif i == 5:
                        pe.wait_ge(f_x1, G)
                        for c in range(FCH + 1):
                            for hf in range(2):
                                if c >= 1:
                                    pe.wait_ge(f_ge[c - 1][hf], G)
                                if c < FCH:
                                    mm(pA[:, hf, 0:HC], ef(1 - par, "w1", c * D, (c + 1) * D), halves(x1[:, :])[:, hf],
                                       start=True, stop=True).then_inc(f_w1[c][hf], 1)
                                if c >= 1:
                                    last = mm(pB[:, hf, 0:HC], ef(1 - par, "w2", (c - 1) * D, c * D), halves(g[:, (c - 1) % 2, :])[:, hf],
                                              start=(c == 1), stop=(c == FCH), skip_group_check=True)
                            if c >= 1:
                                last.then_inc(f_w2p[c - 1], 1)
                            if att and c in WITHIN.values():
                                attend([i for i in WITHIN if WITHIN[i] == c][0])
                    elif i == 6:
                        pe.wait_ge(f_y2, G)
                        over_halves(pA, cc("C"), y[:, :]).then_inc(f_c2, 1)
                    elif i == 7:
                        pe.wait_ge(f_sq2, G)
                        over_halves(pB, cc("J"), sqf[:, :]).then_inc(f_v2, 1)
                if not att:
                    gate_rows(G)

            pe.wait_ge(s_const, 16)
            pe.wait_ge(s_tokw, 16)
            pe.wait_ge(s_shared, 16)
            pe.wait_ge(s_init, 1)
            for c in range(2 * KJ):
                embed(0, c)
            def unit(u, last_unit):
                pe.wait_ge(u_oh, u + 1)
                pe.wait_ge(o_xe, u)
                pe.wait_ge(f_rg, u * 8)
                for k in range(2):
                    last = mm(pB[0:SEGS, k, 0:4 * NTP], segof[:, :], onehot[:, 4 * k:4 * k + 4, :].rearrange("p b t -> p (b t)"),
                              start=True, stop=True)
                last.then_inc(u_cnt, 1)
                pe.wait_ge(e_ev, 2 * u + 2)
                for b in range(UB):
                    last = mm(pS[0:NTP, 0, b * SEGS:(b + 1) * SEGS], onehot[:, b, :], segof[:, :], start=True, stop=True)
                last = mm(pS[0:3, 1, 0:UB * NCLS], ones16[:, 0:3], onehot[:, :, T0:NT], start=True, stop=True)
                last.then_inc(u_n0, 1)
                pe.wait_ge(e_ev, 2 * u + 2)
                pe.wait_ge(u_cnt_t, u + 1)
                over_halves(pB, cc("C"), hA[:, :, :].rearrange("p b t -> p (b t)")).then_inc(n1_c, 1)
                pe.wait_ge(n1_sq, u + 1)
                pe.wait_ge(o_te, u)
                over_halves(pA, cc("J"), sq[:, :]).then_inc(n1_v, 1)
                pe.wait_ge(n1_x, u + 1)
                over_halves(pA, sc("wq"), xn[:, :]).then_inc(l_q, 1)
                over_halves(pB, sc("wk"), xn[:, :]).then_inc(l_k, 1)
                pe.wait_ge(l_qe, u + 1)
                for b in range(UB):
                    last = mm(pA[0:NT, b // 4, (b % 4) * D:(b % 4 + 1) * D], xn[:, b * NT:(b + 1) * NT], sc("wk"), start=True, stop=True)
                last.then_inc(l_kt, 1)
                pe.wait_ge(l_kte, u + 1)
                pe.wait_ge(l_ke, u + 1)
                for b in range(UB):
                    last = mm(pA[0:NT, b // 4, (b % 4) * D:(b % 4 + 1) * D], xn[:, b * NT:(b + 1) * NT], sc("wv"), start=True, stop=True)
                last.then_inc(l_v, 1)
                pe.wait_ge(u_cnt4, u + 1)
                for b in range(UB):
                    last = mm(pB[:, 0, b * SEGS:(b + 1) * SEGS], ktok[:, b * D:(b + 1) * D], count4[0:NT, b, :], start=True, stop=True)
                last.then_inc(l_kc, 1)
                pe.wait_ge(l_kce, u + 1)
                pe.wait_ge(l_ve, u + 1)
                pe.wait_ge(u_lnn, u + 1)
                NB = pe.snap(u * 72)
                LB = pe.snap(u * 8)
                for i in range(NSTEP):
                    b = i - 2
                    if 0 <= b < UB:
                        pe.wait_ge(l_sel, LB + b + 1)
                        pe.wait_ge(l_selc, LB + b)
                        pe.sem_inc(passed_pe, 1)
                        pt = pB[0:SEGS, 0, 0:RT * RP // 2].bitcast(BF16)
                        for j in range(RT):
                            last = nc.tensor.transpose(pt[:, j * RP:(j + 1) * RP], chosen[0:RP, j, :], ident16[0:RP, 0:RP])
                        last.then_inc(l_selt, 1)
                    b = i
                    if b < UB:
                        pe.wait_ge(qx_ready, NB + b + 1 + CREDIT)
                        if b >= 2:
                            pe.wait_ge(l_mr, LB + b - 1)
                        mm(pA[:, b % 2, 0:RT * RW], ones16[0:1, :], sentinel[:, :, :].rearrange("p j w -> p (j w)"),
                           start=True, stop=False, skip_group_check=True)
                        for j in range(RT):
                            last = mm(pA[:, b % 2, j * RW:(j + 1) * RW], qxf[:, b % 3, j * RP:j * RP + 128], klm[:, b, NTP:NTP + RW],
                                      start=False, stop=True, skip_group_check=True)
                        last.then_inc(l_r, 1)
                    b = i - 2
                    if 0 <= b < UB:
                        pe.wait_ge(l_selc, LB + b + 1)
                        pe.wait_ge(rden_ready, NB + b + CREDIT)
                        for j in range(RT):
                            last = mm(pB[:, 1, j * NTP:(j + 1) * NTP], chosen_t[:, j * RP:j * RP + 128], count_t[:, b, :], start=True, stop=True)
                        last.then_inc(l_w, 1)
                    b = i - 1
                    if 0 <= b < UB:
                        if b >= 2:
                            pe.wait_ge(l_sm, LB + b - 1)
                        for j in range(RT):
                            last = mm(pS[:, b % 2, j * NTP:(j + 1) * NTP], qxf[:, b % 3, j * RP:j * RP + 128], klm[:, b, 0:NTP],
                                      start=True, stop=True)
                        last.then_inc(scores_done, 1)
                    if 0 <= i - 4 < UB:
                        weigh_values(NB, i - 4, 1)
                    if 0 <= i - 3 < UB:
                        transpose_probs(NB, i - 3)
                pe.wait_ge(ctx_ready, NB + UB + CREDIT)
                over_halves(pA, sc("wp"), cx[:, 1, :, :].rearrange("p b t -> p (b t)")).then_inc(l_pr, 1)
                pe.wait_ge(l_hb, u + 1)
                over_halves(pB, cc("C"), hB[:, :]).then_inc(n2_c, 1)
                pe.wait_ge(n2_sq, u + 1)
                over_halves(pA, cc("J"), sq[:, :]).then_inc(n2_v, 1)
                pe.wait_ge(n2_x, u + 1)
                over_halves(pA, sc("gwk"), xn[:, :]).then_inc(g_key, 1)
                pe.wait_ge(g_keye, u + 1)
                for j in range(RT):
                    last = mm(pS[0:RP, 0, j * E:(j + 1) * E], qf[:, j * RP:(j + 1) * RP], sc("eq"), start=True, stop=True)
                last.then_inc(g_sc, 1)
                pe.wait_ge(s_eatt[0], u * 64 + 16)
                project_qk(0)
                pe.wait_ge(a_qf, u * 8 + 1)
                project_v(0)
                pe.wait_ge(g_gate, u + 1)
                for j in range(RT):
                    last = nc.tensor.transpose(pP[0:NPART * E, j // 4, (j % 4) * RP:(j % 4 + 1) * RP],
                                               gsum[:, j, :, :].rearrange("p n e -> p (n e)"), cc("I", RP, 0, RP))
                last.then_inc(g_gt, 1)
                pe.wait_ge(g_gte, 2 * u + 2)
                pe.wait_ge(a_ve, u * 8 + 1)
                over_halves(pA, sc("be2", NPART * E), gate_t[:, :]).then_inc(g_b2, 1)
                pe.wait_ge(g_acc, u + 1)

                body(pe.snap(u * 72 + 8), pe.snap(u * 8), 0, pe.snap(u * 64 + 16), None, closing=False)
                body(pe.snap(u * 72 + 16), pe.snap(u * 8 + 1), 1, pe.snap(u * 64 + 32), pe.snap(u * 64 + 16), closing=False)
                with pe.Fori(0, 2) as t:
                    body(pe.snap(u * 72 + 24 + t * 16), pe.snap(u * 8 + 2 + t * 2), 0,
                         pe.snap(u * 64 + t * 16 + 32), pe.snap(u * 64 + t * 16 + 16))
                    body(pe.snap(u * 72 + 32 + t * 16), pe.snap(u * 8 + 3 + t * 2), 1,
                         pe.snap(u * 64 + t * 16 + 48), pe.snap(u * 64 + t * 16 + 32))
                body(pe.snap(u * 72 + 56), pe.snap(u * 8 + 6), 0, pe.snap(u * 64 + 64), pe.snap(u * 64 + 48))
                body(pe.snap(u * 72 + 64), pe.snap(u * 8 + 7), 1, None, pe.snap(u * 64 + 64))
                body(pe.snap(u * 72 + 72), pe.snap(u * 8 + 8), 0, None, pe.snap(u * 64 + 64), att=False,
                     next_unit=None if last_unit else u + 1)
                pe.wait_ge(f_acc, u * 8 + 8)
                for b in range(UB):
                    last = nc.tensor.transpose(pA[0:NT, b // 4, (b % 4) * D:(b % 4 + 1) * D], acc[:, b * NT:(b + 1) * NT], cc("I"))
                last.then_inc(o_t, 1)
                pe.wait_ge(o_te, u + 1)
                pe.wait_ge(u_oht, u + 1)
                for b in range(UB):
                    last = mm(pB[:, b // 4, (b % 4) * D:(b % 4 + 1) * D], onehot_t[:, b, :], htok[:, b, :], start=True, stop=True)
                last.then_inc(o_x, 1)

            with pe.Fori(0, NU - 1) as u:
                unit(u, False)
            unit(NU - 1, True)

        @block.scalar
        def _(act):
            def A(out_, in_, f, **kw):
                return nc.scalar.activation(out_, in_, f, **kw)

            def evac_probs(N, b):
                act.wait_ge(pt_done, N + b + 1 + CREDIT)
                act.wait_ge(ctx_done, N + b - 1 + CREDIT)
                A(probs_t[:, b % 2, 0:PTL * RP], pP[0:NT, 0, 0:PTL * RP], ACT.Copy).then_inc(pt_main, 1)
                A(probs_t[:, b % 2, PTL * RP:RT * RP], pP[0:NT, 1, PR0:PR0 + RP], ACT.Copy).then_inc(pt_rest, 1)

            def evac_ctx(N, b, par, bias=True, last=False):
                act.wait_ge(ctx_done, N + b + 1 + CREDIT)
                if not last:
                    act.wait_ge(pt_done, N + b + 2 + CREDIT)
                kw = dict(bias=bvc[:, par:par + 1]) if bias else {}
                A(cx[:, par, b % UB, :], pP[:, 1, 0:NT], ACT.Identity, **kw).then_inc(ctx_ready, 1)

            def exps(N, b):
                act.wait_ge(max_ready, N + b + 1 + CREDIT)
                p = probs[0:RP, b % 4, :, 0:NT]
                A(p, p, ACT.Exp).then_inc(exp_done, 1)

            def project_q(G, par):
                act.wait_ge(a_q, G + 1)
                A(halves(qf[:, :]), pAu, ACT.Identity, bias=ea(par, "bq"), scale=1.0).then_inc(a_qf, 1)

            def project_k(G, par):
                act.wait_ge(a_kf, G + 1)
                A(kh[:, par, :], kf[:, :], ACT.Copy).then_inc(a_kh, 1)

            def spread(par):
                return vtok[par][:, :, :].rearrange("p q (a d) -> p q a d", a=4)[:, :, 0:4:3, :]

            def project_v(N, G, par):
                act.wait_ge(ctx_ready, N + CREDIT)
                A(bvc[:, par:par + 1], ea(par, "bv"), ACT.Copy).then_inc(a_bv, 1)
                act.wait_ge(a_bv, G + 1)
                act.wait_ge(a_v, G + 1)
                A(spread(par), pA[0:NT, :, :].rearrange("p k (q a d) -> p (k q) a d", a=2, d=DH), ACT.Copy).then_inc(a_ve, 1)

            def rstd(psum, buf, v, l, r, n):
                act.wait_ge(v, n)
                A(halves(buf[:, :]), psum, ACT.Ln, bias=epsc[:, 0:1]).then_inc(l, 1)
                act.wait_ge(l, n)
                A(buf[:, :], buf[:, :], ACT.Exp, scale=-0.5).then_inc(r, 1)

            def body(N, G, par, next_weights, ffn_weights, att=True):
                ffn = ffn_weights is not None

                def evacs(i):
                    if (-2 if ffn else 0) <= i - 2 < (UB if att else 0):
                        evac_probs(N, i - 2)
                    if (-3 if ffn else 0) <= i - 3 < (UB if att else 0):
                        evac_ctx(N, i - 3, par if i >= 3 else 1 - par, last=(not att and i == 2))

                for i in range(UB):
                    if ffn and i == 5:
                        rstd(pAu, rsf, f_v1, f_l1, f_r1, G)
                    if ffn and i == 4:
                        act.wait_ge(f_y, G)
                        A(sqf[:, :], y[:, :], ACT.Square).then_inc(f_sq1, 1)
                    if not (ffn and i in WITHIN):
                        evacs(i)
                    if att:
                        exps(N, i)
                    if next_weights is not None:
                        if i == 1:
                            act.wait_ge(s_eatt[1 - par], next_weights)
                            project_q(G + 1, 1 - par)
                        elif i == 2:
                            project_k(G + 1, 1 - par)
                        elif i == 3:
                            project_v(N, G + 1, 1 - par)
                    if not ffn:
                        continue
                    if i == 5:
                        act.preload_act_table_set("gelu_and_others")
                        act.wait_ge(s_effn[1 - par], ffn_weights)
                        for c in range(FCH):
                            if c >= 2:
                                act.wait_ge(f_w2p[c - 2], G)
                            for hf in range(2):
                                act.wait_ge(f_w1[c][hf], G)
                                A(halves(g[:, c % 2, :])[:, hf], pA[:, hf, 0:HC], ACT.Gelu, bias=ef(1 - par, "bf1", c, c + 1))\
                                    .then_inc(f_ge[c][hf], 1)
                            if att and c in WITHIN.values():
                                evacs([i for i in WITHIN if WITHIN[i] == c][0])
                        act.wait_ge(f_w2p[FCH - 1], G)
                        A(halves(z[:, :]), pBu, ACT.Gelu, bias=ef(1 - par, "bf2")).then_inc(f_h2, 1)
                        act.preload_act_table_set(LN_EXP)
                    elif i == 6:
                        act.wait_ge(f_c2, G)
                        A(halves(sqf[:, :]), pAu, ACT.Square).then_inc(f_sq2, 1)
                    elif i == 7:
                        rstd(pBu, rsf, f_v2, f_l2, f_r2, G)

            for s in (exp_done, pt_rest, pt_main, ctx_ready):
                act.sem_inc(s, CREDIT)
            act.wait_ge(s_const, 16)
            act.wait_ge(s_init, 1)
            act.preload_act_table_set(LN_EXP)
            with act.Fori(0, NU) as u:
                act.wait_ge(u_ln, u + 1)
                A(lnw[:, 2, :], lnw[:, 1, :], ACT.Ln).then_inc(u_lne, 1)
                act.wait_ge(n1_c, u + 1)
                A(halves(sq[:, :]), pBu, ACT.Square).then_inc(n1_sq, 1)
                rstd(pAu, rs, n1_v, n1_l, n1_r, u + 1)
                act.wait_ge(l_kt, u + 1)
                A(ktok[:, :].rearrange("p (k c) -> p k c", k=2), pA[0:NT, :, :], ACT.Copy).then_inc(l_kte, 1)
                act.wait_ge(l_v, u + 1)
                A(spread(1), pA[0:NT, :, :].rearrange("p k (q a d) -> p (k q) a d", a=2, d=DH), ACT.Copy).then_inc(l_ve, 1)
                act.wait_ge(l_kc, u + 1)
                A(klm[:, :, NTP:NTP + SEGS], pB[:, 0, :].rearrange("p (b m) -> p b m", b=UB), ACT.Copy).then_inc(l_kce, 1)
                NB = act.snap(u * 72)
                LB = act.snap(u * 8)
                for i in range(NSTEP):
                    b = i - 2
                    if 0 <= b < UB:
                        act.wait_ge(l_selt, LB + b + 1)
                        act.wait_ge(l_w, LB + b)
                        A(chosen_t[:, 0:RT * RP], pB[0:SEGS, 0, 0:RT * RP // 2].bitcast(BF16), ACT.Copy).then_inc(l_selc, 1)
                        act.wait_ge(l_w, LB + b + 1)
                        act.wait_ge(l_sm, LB + b)
                        A(pen[0:RP, :, :].rearrange("p j t -> p (j t)"), pB[0:RP, 1, 0:RT * NTP], ACT.Identity, bias=bigneg[0:RP, 0:1], scale=2e30)\
                            .then_inc(l_pen, 1)
                    if 0 <= i - 3 < UB:
                        evac_probs(NB, i - 3)
                    if 0 <= i - 4 < UB:
                        evac_ctx(NB, i - 4, 1, bias=False, last=(i - 4 == UB - 1))
                    if 0 <= b < UB:
                        act.wait_ge(l_sm, LB + b + 1)
                        A(probs[0:RP, b % 4, :, :], probs[0:RP, b % 4, :, :], ACT.Exp).then_inc(exp_done, 1)
                act.wait_ge(n2_c, u + 1)
                A(halves(sq[:, :]), pBu, ACT.Square).then_inc(n2_sq, 1)
                rstd(pAu, rs, n2_v, n2_l, n2_r, u + 1)
                act.wait_ge(g_max, u + 1)
                A(gate[:, 1], gate[:, 0], ACT.Exp, scale=float(D) ** -0.5).then_inc(g_exp, 1)

                act.wait_ge(s_eatt[0], u * 64 + 16)
                G = act.snap(u * 8)
                project_q(G, 0)
                project_k(G, 0)
                project_v(act.snap(u * 72 + 8), G, 0)
                body(act.snap(u * 72 + 8), act.snap(u * 8), 0, act.snap(u * 64 + 16), None)
                body(act.snap(u * 72 + 16), act.snap(u * 8 + 1), 1, act.snap(u * 64 + 32), act.snap(u * 64 + 16))
                with act.Fori(0, 2) as t:
                    body(act.snap(u * 72 + 24 + t * 16), act.snap(u * 8 + 2 + t * 2), 0,
                         act.snap(u * 64 + t * 16 + 32), act.snap(u * 64 + t * 16 + 16))
                    body(act.snap(u * 72 + 32 + t * 16), act.snap(u * 8 + 3 + t * 2), 1,
                         act.snap(u * 64 + t * 16 + 48), act.snap(u * 64 + t * 16 + 32))
                body(act.snap(u * 72 + 56), act.snap(u * 8 + 6), 0, act.snap(u * 64 + 64), act.snap(u * 64 + 48))
                body(act.snap(u * 72 + 64), act.snap(u * 8 + 7), 1, None, act.snap(u * 64 + 64))
                body(act.snap(u * 72 + 72), act.snap(u * 8 + 8), 0, None, act.snap(u * 64 + 64), att=False)
                act.wait_ge(o_t, u + 1)
                act.wait_ge(s_out, u * 32)
                A(htok[:, :, :].rearrange("p (k b) d -> p k (b d)", k=2), pA[0:NT, :, :], ACT.Copy).then_inc(o_te, 1)

        @block.gpsimd
        def _(pool):
            pool.sem_inc(norm_ready, CREDIT)
            pool.sem_inc(qxl_ready, CREDIT)
            pool.wait_ge(s_init, 1)

            def norm(N, b, w):
                pool.wait_ge(rden_ready, N + b + 1 + CREDIT)
                p = probs[0:RP, b % 4, :, 0:w]
                nc.gpsimd.tensor_tensor(p, p, rden[0:RP, b % 4, :, None].broadcast_to((RP, RT, w)), ALU.mult).then_inc(norm_ready, 1)

            def mask_f(N, b):
                pool.wait_ge(scores_done, N + b - 2 + CREDIT)
                nc.gpsimd.tensor_tensor(qxf[:, b % 3, 0:H * NT].rearrange("p (h t) -> p h t", h=H), maskf[:, :, :],
                                        qf[:, None, b * NT:(b + 1) * NT].broadcast_to((128, H, NT)), ALU.mult).then_inc(qx_ready, 1)

            def mark_chosen(L, b):
                pool.wait_ge(l_mr, L + b + 1)
                pool.wait_ge(l_selt, L + b)
                pool.sem_inc(passed_pool, 1)
                nc.gpsimd.tensor_scalar(chosen[0:RP, :, :], routed[0:RP, :, 0:SEGS], -2e38, None, ALU.is_le).then_inc(l_sel, 1)

            def low_q(G, par):
                pool.wait_ge(a_qh, G + 1)
                nc.gpsimd.tensor_tensor(ql[:, par, :], qf[:, :], qh[:, par, :], ALU.subtract).then_inc(a_ql, 1)

            def low_k(G, par):
                pool.wait_ge(a_kh, G + 1)
                nc.gpsimd.tensor_tensor(kl[:, par, :], kf[:, :], kh[:, par, :], ALU.subtract).then_inc(a_kl, 1)

            def body(N, G, par, next_weights, ffn_weights, att=True):
                for i in range(UB if att else 1):
                    if i >= 1 or ffn_weights is not None:
                        norm(N, i - 1, NT)
                    if next_weights is not None:
                        if i == 3:
                            low_q(G + 1, 1 - par)
                        elif i == 4:
                            low_k(G + 1, 1 - par)

            with pool.Fori(0, NU) as u:
                NB = pool.snap(u * 72)
                LB = pool.snap(u * 8)
                pool.wait_ge(l_qe, u + 1)
                mask_f(NB, 0)
                for i in range(NSTEP):
                    if i + 1 < UB:
                        mask_f(NB, i + 1)
                    if 0 <= i - 1 < UB:
                        mark_chosen(LB, i - 1)
                    if 0 <= i - 2 < UB:
                        norm(NB, i - 2, NTP)
                        pool.sem_inc(qxl_ready, 1)
                low_q(pool.snap(u * 8), 0)
                low_k(pool.snap(u * 8), 0)
                body(pool.snap(u * 72 + 8), pool.snap(u * 8), 0, True, None)
                body(pool.snap(u * 72 + 16), pool.snap(u * 8 + 1), 1, True, True)
                with pool.Fori(0, 2) as t:
                    body(pool.snap(u * 72 + 24 + t * 16), pool.snap(u * 8 + 2 + t * 2), 0,
                         True, True)
                    body(pool.snap(u * 72 + 32 + t * 16), pool.snap(u * 8 + 3 + t * 2), 1,
                         True, True)
                body(pool.snap(u * 72 + 56), pool.snap(u * 8 + 6), 0, True, True)
                body(pool.snap(u * 72 + 64), pool.snap(u * 8 + 7), 1, None, True)
                body(pool.snap(u * 72 + 72), pool.snap(u * 8 + 8), 0, None, True, att=False)

        @block.vector
        def _(dve):
            V = nc.vector
            for s in (qx_ready, scores_done, neg_ready, den_ready, max_ready, rden_ready, pt_done, ctx_done):
                dve.sem_inc(s, CREDIT)

            def bc(ap, dim, n):
                shape = list(ap.shape)
                shape[dim] = n
                return ap.broadcast_to(tuple(shape))

            dve.wait_ge(s_const, 16)
            dve.wait_ge(s_shared, 16)
            dve.wait_ge(s_text, 16)
            n = 0
            for ins in (
                lambda: V.tensor_copy(segof[:, :], cc("A")),
                lambda: V.tensor_copy(ident16[:, :], cc("I")),
                lambda: V.tensor_scalar(mask16[:, :, :].rearrange("p h t -> p (h t)"), cc("mask"), SCALE, None, ALU.mult),
                lambda: V.tensor_scalar(maskf[:, :, :].rearrange("p h t -> p (h t)"), cc("mask"), SCALE, None, ALU.mult),
                lambda: V.memset(ones16[:, :], 1.0),
                lambda: V.memset(sentinel[:, :, 0:SEGS], 0.0),
                lambda: V.memset(sentinel[:, :, SEGS:RW], 1e38),
                lambda: V.memset(epsc[:, :], EPS),
                lambda: V.memset(bigneg[:, :], -1e30),
                lambda: V.memset(lnn[:, :, :], 0.0),
                lambda: V.memset(qxh[:, :, :], 0.0),
                lambda: V.memset(qxl[:, :, :], 0.0),
                lambda: V.memset(qxf[:, :, :], 0.0),
                lambda: V.memset(klm[:, :, :], 0.0),
                lambda: V.memset(chosen_t[:, :], 0.0),
                lambda: V.memset(vtok[0][:, :, :], 0.0),
                lambda: V.memset(vtok[1][:, :, :], 0.0),
                lambda: V.memset(gall[:, :, 0:6], 4.0),
                lambda: V.tensor_copy(text_f[:, :], text_i[:, :]),
                lambda: V.tensor_scalar(hA[:, :, 0:1], bc(sc("pos", 128, 0, 1)[:, None, :], 1, UB), sc("cls"), None, ALU.mult),
                lambda: V.tensor_scalar(hA[:, :, T0:NT], bc(sc("txtw")[:, None, :], 1, UB), sc("txtb"), None, ALU.add),
            ):
                n += 1
                ins().then_inc(s_dve, 1)
            dve.wait_ge(s_dve, n)
            dve.sem_inc(s_init, 1)

            def mask_high(N, b, par):
                dve.wait_ge(scores_done, N + b - 1 + CREDIT)
                c = b % UB * NT
                V.tensor_tensor(qxh[:, b % 2, 0:H * NT].rearrange("p (h t) -> p h t", h=H), mask16[:, :, :],
                                bc(qh[:, par, c:c + NT][:, None, :], 1, H), ALU.mult).then_inc(qx_ready, 1)

            def mask_low(N, b, par):
                dve.wait_ge(scores_done, N + b - 1 + CREDIT)
                c = b % UB * NT
                V.tensor_tensor(qxl[:, b % 2, 0:H * NT].rearrange("p (h t) -> p h t", h=H), mask16[:, :, :],
                                        ql[:, par, c:c + NT][:, None, :].broadcast_to((128, H, NT)), ALU.mult).then_inc(qxl_ready, 1)

            def less_max(N, b):
                scores_b = pS[0:RP, b % 2, 0:RT * NT].rearrange("p (j t) -> p j t", j=RT)
                dve.wait_ge(scores_done, N + b + 1 + CREDIT)
                V.tensor_reduce(negmax[0:RP, b % 2, :], scores_b, AX, ALU.max, negate=True).then_inc(neg_ready, 1)
                dve.wait_ge(neg_ready, N + b + 1 + CREDIT)
                dve.wait_ge(pt_done, N + b - 2 + CREDIT)
                V.tensor_tensor(probs[0:RP, b % 4, :, 0:NT], scores_b, bc(negmax[0:RP, b % 2, :, None], 2, NT), ALU.add)\
                    .then_inc(max_ready, 1)

            def denominators(N, b):
                dve.wait_ge(exp_done, N + b + 1 + CREDIT)
                V.tensor_reduce(den[0:RP, b % 4, :], probs[0:RP, b % 4, :, 0:NT], AX, ALU.add).then_inc(den_ready, 1)
                dve.wait_ge(den_ready, N + b + 1 + CREDIT)
                dve.wait_ge(norm_ready, N + b - 2 + CREDIT)
                V.reciprocal(rden[0:RP, b % 4, :], den[0:RP, b % 4, :]).then_inc(rden_ready, 1)

            def project_q(G, par):
                dve.wait_ge(a_qf, G + 1)
                V.tensor_copy(qh[:, par, :], qf[:, :]).then_inc(a_qh, 1)

            def project_k(G, par):
                dve.wait_ge(a_k, G + 1)
                V.tensor_scalar(halves(kf[:, :]), pBu, ea(par, "bk"), None, ALU.add).then_inc(a_kf, 1)

            def add_expert(G, par):
                dve.wait_ge(f_g, G)
                dve.wait_ge(f_r2, G)
                V.tensor_tensor(halves(rsf[:, :]), pBu, halves(rsf[:, :]), ALU.mult).then_inc(f_rg, 1)
                dve.wait_ge(f_rg, G)
                V.tensor_tensor(halves(z[:, :]), pAu, halves(rsf[:, :]), ALU.mult).then_inc(f_t, 1)

            def accumulate(G, par):
                dve.wait_ge(f_t, G)
                V.scalar_tensor_tensor(acc[:, :], z[:, :], ef(par, "g2"), acc[:, :], ALU.mult, ALU.add).then_inc(f_acc, 1)

            def body(N, G, par, next_weights, ffn_weights, att=True, closing=True):
                ffn = ffn_weights is not None
                for i in range(UB):
                    if att and i + 1 < UB:
                        mask_high(N, i + 1, par)
                        mask_low(N, i + 1, par)
                    elif att and next_weights is not None:
                        dve.wait_ge(a_qh, G + 2)
                        mask_high(N, UB, 1 - par)
                        dve.wait_ge(a_ql, G + 2)
                        mask_low(N, UB, 1 - par)
                    if (att and i >= 1) or (i == 0 and ffn):
                        denominators(N, i - 1)
                    if i == 5 and ffn:
                        dve.wait_ge(f_r1, G)
                        V.tensor_tensor(z[:, :], y[:, :], rsf[:, :], ALU.mult).then_inc(f_z, 1)
                        dve.wait_ge(f_z, G)
                        V.tensor_scalar(x1[:, :], z[:, :], ef(1 - par, "g1"), ef(1 - par, "be1"), ALU.mult, ALU.add).then_inc(f_x1, 1)
                    if att:
                        less_max(N, i)
                    if i == 0 and closing:
                        add_expert(G - 1, par)
                    if i == 1 and closing:
                        accumulate(G - 1, par)
                    if i == 1:
                        if next_weights is not None:
                            dve.wait_ge(s_eatt[1 - par], next_weights)
                            project_k(G + 1, 1 - par)
                        if ffn:
                            dve.wait_ge(s_effn[1 - par], ffn_weights)
                            dve.wait_ge(f_cw, G)
                            if next_weights is not None:
                                dve.wait_ge(a_qf, G + 2)
                            V.tensor_copy(cwo[:, :], pA[:, 0, HC:HC + D + 1]).then_inc(f_cwe, 1)
                            V.tensor_copy(pick16[:, :], ef(1 - par, "pick", p=NPART * E)).then_inc(f_pick, 1)
                    elif i == 2 and next_weights is not None:
                        project_q(G + 1, 1 - par)
                    if not ffn:
                        continue
                    if i == 3:
                        dve.wait_ge(f_wo, G)
                        V.scalar_tensor_tensor(halves(y[:, :]), pBu, cwo[:, D:D + 1], halves(xn[:, :]), ALU.add, ALU.add).then_inc(f_y, 1)
                    elif i == 6:
                        dve.wait_ge(f_h2, G)
                        V.tensor_tensor(y[:, :], z[:, :], x1[:, :], ALU.add).then_inc(f_y2, 1)
                if not att:
                    add_expert(G, 1 - par)
                    accumulate(G, 1 - par)

            NUCH = 19

            with dve.Fori(0, NU) as u:
                CH = dve.snap(u * NUCH)
                links = [0]

                def link(ins, own=False):
                    links[0] += 1
                    ins.then_inc(u_chain, 1)
                    dve.wait_ge(u_chain, CH + links[0])
                    if own:
                        dve.sem_inc(passed_dve, 1)

                dve.wait_ge(u_n0, u)
                dve.wait_ge(u_cnt, u)
                V.tensor_tensor(onehot[:, :, :], bc(text_f[:, bass.ds(u * UB, UB)][:, :, None], 2, NTP), bc(cc("tcol")[:, None, :], 1, UB),
                                ALU.is_equal).then_inc(u_oh, 1)
                dve.wait_ge(s_textrow, u * 16 + 16)
                dve.wait_ge(o_x, u)
                V.tensor_scalar(onehot_t[:, :, :].rearrange("p b j -> p (b j)"), textrow[:, :], cc("tval", NT), None, ALU.is_equal)\
                    .then_inc(u_oht, 1)
                for hf in range(2):
                    dve.wait_ge((e_mm0, e_mm1)[hf], u + 1)
                    V.scalar_tensor_tensor(hA[:, 4 * hf:4 * hf + 4, 1:T0], pS[:, hf, 0:4 * NP].rearrange("p (b t) -> p b t", b=4),
                                           sc("tokb"), bc(sc("pos", 128, 1, 1 + NP)[:, None, :], 1, 4), ALU.add, ALU.mult)\
                        .then_inc(e_ev, 1)
                dve.wait_ge(u_cnt, u + 1)
                for k in range(2):
                    last = V.tensor_tensor(count_t[:, 4 * k:4 * k + 4, :], pB[0:SEGS, k, 0:4 * NTP].rearrange("p (b t) -> p b t", b=4),
                                           bc(cc("MT", SEGS)[:, None, :], 1, 4), ALU.add)
                last.then_inc(u_cnt_t, 1)
                dve.wait_ge(u_n0, u + 1)
                V.scalar_tensor_tensor(count4[:, :, :], pS[0:NTP, 0, :].rearrange("p (b m) -> p b m", b=UB), 1.0 / SEGL,
                                       bc(cc("M4", NTP)[:, None, :], 1, UB), ALU.mult, ALU.add).then_inc(u_cnt4, 1)
                link(V.tensor_copy(lnw[:, 0, :], pS[0:3, 1, 0:UB * NCLS]))
                V.tensor_scalar(lnw[:, 1, :], lnw[:, 0, :], 1.0, None, ALU.max).then_inc(u_ln, 1)
                link(V.tensor_scalar(lnw[:, 3, :], lnw[:, 0, :], 0.5, -1e30, ALU.is_lt, ALU.mult))
                dve.wait_ge(u_lne, u + 1)
                link(V.tensor_tensor(lnw[:, 4, :], lnw[:, 2, :], lnw[:, 3, :], ALU.add))
                link(V.tensor_copy(lnpart[:, 0, :], lnw[:, 4, :]))
                link(V.tensor_tensor(lnw[:, 5, :], lnw[:, 4, :], lnpart[:, 0, :], ALU.subtract))
                link(V.tensor_copy(lnpart[:, 1, :], lnw[:, 5, :]))
                link(V.tensor_tensor(lnpart[:, 2, :], lnw[:, 5, :], lnpart[:, 1, :], ALU.subtract))
                link(V.tensor_scalar(lnw[:, 6, :], lnpart[:, 0, :], cc("I", 3, 0, 1), None, ALU.mult))
                link(V.scalar_tensor_tensor(lnw[:, 7, :], lnpart[:, 1, :], cc("I", 3, 1, 2), lnw[:, 6, :], ALU.mult, ALU.add))
                V.scalar_tensor_tensor(lnn[:, :, T0:NT], lnpart[:, 2, :].rearrange("p (b c) -> p b c", b=UB), cc("I", 3, 2, 3),
                                       lnw[:, 7, :].rearrange("p (b c) -> p b c", b=UB), ALU.mult, ALU.add).then_inc(u_lnn, 1)
                dve.wait_ge(n1_r, u + 1)
                V.tensor_tensor(halves(xn[:, :]), pBu, halves(rs[:, :]), ALU.mult).then_inc(n1_x, 1)
                dve.wait_ge(l_q, u + 1)
                V.tensor_copy(halves(qf[:, :]), pAu).then_inc(l_qe, 1)
                dve.wait_ge(l_k, u + 1)
                for k in range(2):
                    last = V.tensor_copy(klm[:, 4 * k:4 * k + 4, 0:NT], pB[:, k, 0:HC].rearrange("p (b t) -> p b t", b=4))
                last.then_inc(l_ke, 1)
                dve.wait_ge(l_qe, u + 1)
                NB = dve.snap(u * 72)
                LB = dve.snap(u * 8)

                def choose(b):
                    dve.wait_ge(l_r, LB + b + 1)
                    dve.wait_ge(l_mr, LB + b)
                    dve.sem_inc(passed_dve, 1)
                    for j in range(RT):
                        last = V.max(top8[0:RP, j, :], pA[0:RP, b % 2, j * RW:(j + 1) * RW])
                    last.then_inc(l_top, 1)
                    dve.wait_ge(l_top, LB + b + 1)
                    dve.wait_ge(l_sel, LB + b)
                    dve.sem_inc(passed_dve, 1)
                    for j in range(RT):
                        last = V.match_replace(routed[0:RP, j, :], top8[0:RP, j, :], pA[0:RP, b % 2, j * RW:(j + 1) * RW], -3e38)
                    last.then_inc(l_mr, 1)

                def scores_of_chosen(b):
                    dve.wait_ge(scores_done, NB + b + 1 + CREDIT)
                    dve.wait_ge(l_pen, LB + b + 1)
                    s = pS[0:RP, b % 2, 0:RT * NTP].rearrange("p (j t) -> p j t", j=RT)
                    V.tensor_tensor(kept[0:RP, :, :], pen[0:RP, :, :], s, ALU.min).then_inc(l_kept, 1)
                    dve.wait_ge(l_kept, LB + b + 1)
                    V.tensor_reduce(negmax[0:RP, b % 2, :], kept[0:RP, :, :], AX, ALU.max, negate=True).then_inc(neg_ready, 1)
                    dve.wait_ge(neg_ready, NB + b + 1 + CREDIT)
                    dve.wait_ge(pt_done, NB + b - 2 + CREDIT)
                    V.tensor_tensor(probs[0:RP, b % 4, :, :], kept[0:RP, :, :], bc(negmax[0:RP, b % 2, :, None], 2, NTP), ALU.add)\
                        .then_inc(l_sm, 1)

                def weigh(b):
                    p = probs[0:RP, b % 4, :, :]
                    dve.wait_ge(exp_done, NB + b + 1 + CREDIT)
                    counts = pB[0:RP, 1, 0:RT * NTP].rearrange("p (j t) -> p j t", j=RT)
                    V.tensor_tensor(p, p, counts, ALU.mult).then_inc(max_ready, 1)
                    dve.wait_ge(max_ready, NB + b + 1 + CREDIT)
                    V.tensor_reduce(den[0:RP, b % 4, :], p, AX, ALU.add).then_inc(den_ready, 1)
                    dve.wait_ge(den_ready, NB + b + 1 + CREDIT)
                    V.reciprocal(rden[0:RP, b % 4, :], den[0:RP, b % 4, :]).then_inc(rden_ready, 1)

                for i in range(NSTEP):
                    if 0 <= i - 1 < UB:
                        choose(i - 1)
                    if 0 <= i - 2 < UB:
                        scores_of_chosen(i - 2)
                        weigh(i - 2)
                dve.wait_ge(l_pr, u + 1)
                V.scalar_tensor_tensor(halves(hB[:, :]), pAu, sc("bp"), halves(hA[:, :, :].rearrange("p b t -> p (b t)")), ALU.add, ALU.add)\
                    .then_inc(l_hb, 1)
                dve.wait_ge(n2_r, u + 1)
                V.tensor_tensor(halves(xn[:, :]), pBu, halves(rs[:, :]), ALU.mult).then_inc(n2_x, 1)
                dve.wait_ge(g_key, u + 1)
                V.tensor_scalar(halves(qf[:, :]), pAu, sc("gbk"), None, ALU.add).then_inc(g_keye, 1)
                dve.wait_ge(g_sc, u + 1)
                s = pS[0:RP, 0, 0:RT * E].rearrange("p (j e) -> p j e", j=RT)
                link(V.tensor_reduce(gate_s[:, 0, :], s, AX, ALU.max, negate=True))
                V.tensor_tensor(gate[:, 0], s, bc(gate_s[:, 0, :, None], 2, E), ALU.add).then_inc(g_max, 1)
                dve.wait_ge(s_eatt[0], u * 64 + 16)
                G = dve.snap(u * 8)
                project_k(G, 0)
                project_q(G, 0)
                dve.wait_ge(g_exp, u + 1)
                link(V.tensor_reduce(gate_s[:, 1, :], gate[:, 1], AX, ALU.add))
                link(V.reciprocal(gate_s[:, 2, :], gate_s[:, 1, :]))
                link(V.tensor_tensor(gall[:, :, 6:6 + E], gate[:, 1], bc(gate_s[:, 2, :, None], 2, E), ALU.mult), own=True)
                for j in range(RT):
                    last = V.max(gtop[:, j, :], gall[:, j, :])
                last.then_inc(g_top, 1)
                dve.wait_ge(g_top, 2 * u + 1)
                dve.sem_inc(passed_dve, 1)
                for j in range(RT):
                    last = V.match_replace(gout[:, j, :], gtop[:, j, :], gall[:, j, :], -1.0)
                last.then_inc(g_top, 1)
                dve.wait_ge(g_top, 2 * u + 2)
                V.scalar_tensor_tensor(gate[:, 2], gout[:, :, 6:6 + E], 0.0, gall[:, :, 6:6 + E], ALU.is_lt, ALU.mult).then_inc(g_msk, 1)
                dve.wait_ge(g_msk, u + 1)
                link(V.tensor_reduce(gate_s[:, 3, :], gate[:, 2], AX, ALU.add))
                link(V.tensor_scalar(gate_s[:, 4, :], gate_s[:, 3, :], 1e-9, None, ALU.add))
                V.reciprocal(gate_s[:, 5, :], gate_s[:, 4, :]).then_inc(g_rec, 1)
                dve.wait_ge(g_rec, u + 1)
                V.tensor_tensor(gate[:, 5], gate[:, 2], bc(gate_s[:, 5, :, None], 2, E), ALU.mult).then_inc(g_gated, 1)
                dve.wait_ge(g_gated, u + 1)
                link(V.tensor_copy(gpart[:, 0], gate[:, 5]))
                link(V.tensor_tensor(gate[:, 3], gate[:, 5], gpart[:, 0], ALU.subtract))
                link(V.tensor_copy(gpart[:, 1], gate[:, 3]))
                link(V.tensor_tensor(gpart[:, 2], gate[:, 3], gpart[:, 1], ALU.subtract))
                V.tensor_copy(gsum[:, :, :, :].rearrange("p j n e -> p n j e"), gpart[:, :, :, :]).then_inc(g_gate, 1)
                assert links[0] == NUCH, links
                dve.wait_ge(g_gt, u + 1)
                V.tensor_copy(gate_t[:, 0:4 * RP], pP[0:NPART * E, 0, 0:4 * RP])
                V.tensor_copy(gate_t[:, 4 * RP:RT * RP], pP[0:NPART * E, 1, 0:RP]).then_inc(g_gte, 1)
                dve.wait_ge(g_gte, 2 * u + 1)
                V.tensor_copy(gate_t16[:, :], gate_t[:, :]).then_inc(g_gte, 1)
                dve.wait_ge(g_b2, u + 1)
                V.tensor_tensor(halves(acc[:, :]), pAu, halves(hB[:, :]), ALU.add).then_inc(g_acc, 1)

                dve.wait_ge(a_qh, u * 8 + 1)
                mask_high(dve.snap(u * 72 + 8), 0, 0)
                dve.wait_ge(a_ql, u * 8 + 1)
                mask_low(dve.snap(u * 72 + 8), 0, 0)
                body(dve.snap(u * 72 + 8), dve.snap(u * 8), 0, dve.snap(u * 64 + 16), None, closing=False)
                body(dve.snap(u * 72 + 16), dve.snap(u * 8 + 1), 1, dve.snap(u * 64 + 32), dve.snap(u * 64 + 16), closing=False)
                with dve.Fori(0, 2) as t:
                    body(dve.snap(u * 72 + 24 + t * 16), dve.snap(u * 8 + 2 + t * 2), 0,
                         dve.snap(u * 64 + t * 16 + 32), dve.snap(u * 64 + t * 16 + 16))
                    body(dve.snap(u * 72 + 32 + t * 16), dve.snap(u * 8 + 3 + t * 2), 1,
                         dve.snap(u * 64 + t * 16 + 48), dve.snap(u * 64 + t * 16 + 32))
                body(dve.snap(u * 72 + 56), dve.snap(u * 8 + 6), 0, dve.snap(u * 64 + 64), dve.snap(u * 64 + 48))
                body(dve.snap(u * 72 + 64), dve.snap(u * 8 + 7), 1, None, dve.snap(u * 64 + 64))
                body(dve.snap(u * 72 + 72), dve.snap(u * 8 + 8), 0, None, dve.snap(u * 64 + 64), att=False)
                dve.wait_ge(o_x, u + 1)
                dve.wait_ge(s_out, u * 32)
                V.tensor_copy(outtext[:, :, :].rearrange("p (k b) d -> p k (b d)", k=2), pB[:, :, :]).then_inc(o_xe, 1)


def kernel(**inputs):
    import numpy as np
    import concourse.bacc as bacc
    from concourse.bass_utils import run_bass_kernel_spmd

    a = {k: np.asarray(v) for k, v in inputs.items()}
    f32 = np.float32

    def put(shape_cols, width, parts):
        blk = np.zeros((128, width), f32)
        for name, v in parts.items():
            lo, hi = shape_cols[name]
            v = np.asarray(v)
            blk[:v.shape[0], lo:hi] = v.reshape(v.shape[0], -1)
        return blk

    pos_of = np.arange(SEQT)
    seg_of = (T0 + pos_of) // SEGL
    A = np.zeros((SEQT, SEGS), f32)
    A[pos_of, seg_of] = 1
    M = np.zeros((NTP, SEGS), f32)
    for t in range(T0):
        M[t, t // SEGL] += 1
    for t in range(SEQ, SEGS * SEGL):
        M[NT, t // SEGL] += 1
    tval = np.full((NTP,), -1.0, f32)
    tval[T0:NT] = np.arange(NCLS)
    mask = (np.arange(128)[:, None] // DH == np.arange(H)[None]).astype(f32)
    const = put(CCOL, CW, dict(
        C=np.eye(128, dtype=f32) - f32(1 / 128), J=np.full((128, 128), 1 / 128, f32), I=np.eye(128, dtype=f32),
        mask=np.repeat(mask, NT, axis=1), A=A, tcol=np.tile(tval, (128, 1)), M4=M / SEGL, MT=M.T, tval=tval[:, None]))
    wqkv = a["L0_attn_w_qkv"].reshape(3, D, D)
    shared = put(SCOL, SW, dict(
        wq=wqkv[0].T, wk=wqkv[1].T, wv=wqkv[2].T, wp=a["L0_attn_w_proj"].T, gwk=a["L0_ffn_gate_Wk"].T,
        eq=a["L0_ffn_expert_queries"].T, be2=np.tile(a["L0_ffn_be2"], (NPART, 1)), pos=a["L0_tok_pos_embed"].T, txtw=a["L0_txt_W"],
        bp=a["L0_attn_b_proj"][:, None], tokb=a["L0_tok_b"][:, None], cls=a["L0_tok_class_token"].T,
        txtb=a["L0_txt_b"][:, None], gbk=a["L0_ffn_gate_bk"][:, None]))
    tokw = np.ascontiguousarray(a["L0_tok_W"].T.reshape(KJ, KP, D).transpose(1, 0, 2))
    eatt, effn = [], []
    for e in range(E):
        w, bqkv = a["L0_ffn_Wqkv"][e].reshape(3, D, D), a["L0_ffn_bqkv"][e].reshape(3, D, 1)
        eatt.append(put(ACOL, AW, dict(wq=w[0].T, wk=w[1].T, wv=w[2].T, bq=bqkv[0], bk=bqkv[1], bv=bqkv[2])))
        pick = np.zeros((NPART * E, D), f32)
        pick[e::E] = 1
        effn.append(put(FCOL, FW, dict(
            wo=a["L0_ffn_Wo"][e], w1=a["L0_ffn_W1"][e].T,
            w2=a["L0_ffn_W2"][e].T.reshape(FCH, D, D).transpose(1, 0, 2), pick=pick,
            bo=a["L0_ffn_bo"][e][:, None], g1=a["L0_ffn_g1"][e][:, None], be1=a["L0_ffn_be1"][e][:, None],
            bf1=a["L0_ffn_bf1"][e].reshape(FCH, D).T, bf2=a["L0_ffn_bf2"][e][:, None], g2=a["L0_ffn_g2"][e][:, None])))
    x = a["x"].reshape(NU, 2, 4, 3, 8, 28, 8, 28).transpose(0, 1, 3, 5, 7, 2, 4, 6).reshape(NU, 2, KJ, KP, 4 * NP)
    arrays = dict(x_in=np.ascontiguousarray(x.transpose(0, 1, 3, 2, 4)), xt_in=np.ascontiguousarray(a["x_txt"].T),
                  xr_in=np.ascontiguousarray(a["x_txt"].reshape(NU, UB * SEQT)), const_in=const, shared_in=shared,
                  tokw_in=tokw, eatt_in=np.stack(eatt), effn_in=np.stack(effn))
    nc = bacc.Bacc("TRN2", target_bir_lowering=False, num_devices=1)
    args = [nc.dram_tensor(k, v.shape, mybir.dt.from_np(v.dtype), kind="ExternalInput").ap() for k, v in arrays.items()]
    args.append(nc.dram_tensor("out", (B, SEQ, D), F32, kind="ExternalOutput").ap())
    build(nc, *args)
    r = run_bass_kernel_spmd(nc, [arrays], core_ids=[0])
    return r.results[0]["out"]
```

```python
from contextlib import ExitStack

import concourse.bass as bass
from concourse import mybir

F32 = mybir.dt.float32
F16 = mybir.dt.float16
BF16 = mybir.dt.bfloat16
I32 = mybir.dt.int32
ALU = mybir.AluOpType
ACT = mybir.ActivationFunctionType
AX = mybir.AxisListType.X

B = 64
D = 128
H = 8
DH = D // H
NP = 64
NCLS = 5
SEQT = 128
SEQ = 1 + NP + SEQT
NT = 1 + NP + NCLS
NTP = NT + 1
T0 = 1 + NP
SEGS = 64
SEGL = -(-SEQ // SEGS)
TOPK = 4
NSENT = 8 - TOPK
RW = SEGS + NSENT
UB = 8
NU = B // UB
UC = UB * NT
HC = UC // 2
RP = 112
RT = H * NT // RP
QC = H * NT + 128 - RP
E = 8
F = 512
FCH = F // D
KP = 112
KJ = 3 * 28 * 28 // KP
SCALE = DH ** -0.5
LN_EXP = "natural_log_exp_and_others"
EPS = 1e-5
NSTEP = UB + 4
WITHIN = 6
EMBED_FROM = 0
NPART = 3

CONST = dict(C=D, J=D, I=D, mask=H * NT, A=SEGS, tcol=NTP, M4=SEGS, MT=NTP, tval=1)
SHARED = dict(wq=D, wk=D, wv=D, wp=D, gwk=D, eq=E, be2=D, pos=1 + NP, txtw=NCLS,
              bp=1, tokb=1, cls=1, txtb=1, gbk=1)
EATT = dict(wq=D, wk=D, wv=D, bq=1, bk=1, bv=1)
EFFN = dict(wo=D, w1=F, w2=F, pick=D, bo=1, g1=1, be1=1, bf1=FCH, bf2=1, g2=1)


def columns(block):
    at, out = 0, {}
    for name, n in block.items():
        out[name] = (at, at + n)
        at += n
    return out, at


CCOL, CW = columns(CONST)
SCOL, SW = columns(SHARED)
ACOL, AW = columns(EATT)
FCOL, FW = columns(EFFN)


def build(nc, x_in, xt_in, xr_in, const_in, shared_in, tokw_in, eatt_in, effn_in, out):
    with ExitStack() as ctx:
        def sb(name, shape, dt=F32):
            return ctx.enter_context(nc.sbuf_tensor(name, shape, dt))

        def sem(name):
            return ctx.enter_context(nc.semaphore(name))

        const = sb("const", [128, CW])
        shared = sb("shared", [128, SW])
        tokw = sb("tokw", [KP, KJ, D])
        patches = sb("patches", [KP, 2, KJ, 4 * NP])
        eatt = [sb(f"eatt{i}", [128, AW]) for i in range(2)]
        effn = [sb(f"effn{i}", [128, FW]) for i in range(2)]
        text_i = sb("text_i", [128, B], I32)
        text_f = sb("text_f", [128, B])
        textrow = sb("textrow", [NT, UB * SEQT], I32)
        onehot = sb("onehot", [128, UB, NTP], BF16)
        onehot_t = sb("onehot_t", [NT, UB, SEQT])
        segof = sb("segof", [128, SEGS], BF16)
        ident16 = sb("ident16", [128, 128], BF16)
        maskf = sb("maskf", [128, H, NT])
        mask16 = sb("mask16", [128, H, NT], F16)
        ones16 = sb("ones16", [128, 128], BF16)
        sentinel = sb("sentinel", [1, RT, RW], BF16)
        count_t = sb("count_t", [SEGS, UB, NTP], BF16)
        count4 = sb("count4", [NTP, UB, SEGS])
        lnw = sb("lnw", [3, 8, UB * NCLS])
        lnn = sb("lnn", [3, UB, NT], BF16)
        lnpart = sb("lnpart", [3, 3, UB * NCLS], BF16)
        hA = sb("hA", [128, UB, NT])
        hB = sb("hB", [128, UC])
        xn = sb("xn", [128, UC])
        sq = sb("sq", [128, UC])
        sqf = sb("sqf", [128, UC])
        rs = sb("rs", [128, UC])
        rsf = sb("rsf", [128, UC])
        qf = sb("qf", [128, UC])
        kf = sb("kf", [128, UC])
        qh = sb("qh", [128, 2, UC], F16)
        ql = sb("ql", [128, 2, UC], F16)
        kh = sb("kh", [128, 2, UC], F16)
        kl = sb("kl", [128, 2, UC], F16)
        qxh = sb("qxh", [128, 2, QC], F16)
        qxl = sb("qxl", [128, 2, QC], F16)
        qxf = sb("qxf", [128, 3, QC])
        klm = sb("klm", [128, UB, NTP + RW])
        ktok = sb("ktok", [NT, UB * D])
        vtok = [sb(f"vtok{i}", [NT, UB * H // 2, 64]) for i in range(2)]
        top8 = sb("top8", [128, RT, 8])
        routed = sb("routed", [128, RT, RW])
        chosen = sb("chosen", [128, RT, SEGS], BF16)
        chosen_t = sb("chosen_t", [SEGS, QC], BF16)
        pen = sb("pen", [128, RT, NTP])
        kept = sb("kept", [128, RT, NTP])
        negmax = sb("negmax", [128, 2, RT])
        den = sb("den", [128, 4, RT])
        rden = sb("rden", [128, 4, RT])
        probs = sb("probs", [128, 4, RT, NTP])
        probs_t = sb("probs_t", [NT, 2, H * NT])
        cx = sb("cx", [128, 2, UB, NT])
        bvc = sb("bvc", [128, 2])
        cwo = sb("cwo", [128, D + 1])
        pick16 = sb("pick16", [NPART * E, D], BF16)
        epsc = sb("epsc", [128, 1])
        bigneg = sb("bigneg", [128, 1])
        y = sb("y", [128, UC])
        z = sb("z", [128, UC])
        x1 = sb("x1", [128, UC])
        g = sb("g", [128, 2, UC])
        acc = sb("acc", [128, UC])
        gate = sb("gate", [RP, 6, RT, E])
        gate_s = sb("gate_s", [RP, 6, RT])
        gtop = sb("gtop", [RP, RT, 8])
        gall = sb("gall", [RP, RT, E + 6])
        gout = sb("gout", [RP, RT, E + 6])
        gpart = sb("gpart", [RP, NPART, RT, E], BF16)
        gsum = sb("gsum", [RP, RT, NPART, E])
        gate_t = sb("gate_t", [NPART * E, UC])
        gate_t16 = sb("gate_t16", [NPART * E, UC], BF16)
        htok = sb("htok", [NT, UB, D])
        outtext = sb("outtext", [SEQT, UB, D])

        pA = ctx.enter_context(nc.psum_tensor("pA", [128, 2, 512], F32))
        pB = ctx.enter_context(nc.psum_tensor("pB", [128, 2, 512], F32))
        pS = ctx.enter_context(nc.psum_tensor("pS", [128, 2, 512], F32))
        pP = ctx.enter_context(nc.psum_tensor("pP", [128, 2, 512], F32))
        PTL = 4
        PR0 = 256
        pAu, pBu = pA[:, :, 0:HC], pB[:, :, 0:HC]

        CREDIT = 3
        names_n = ("qxl_ready", "qx_ready", "scores_done", "neg_ready", "den_ready", "max_ready", "exp_done", "rden_ready", "norm_ready",
                   "pt_done", "pt_rest", "pt_main", "ctx_done", "ctx_ready")
        (qxl_ready, qx_ready, scores_done, neg_ready, den_ready, max_ready, exp_done, rden_ready, norm_ready,
         pt_done, pt_rest, pt_main, ctx_done, ctx_ready) = (sem(n) for n in names_n)
        routes_done, best_marked, chosen_ready, chosen_t_done, chosen_t_ready, key_counts_done, pen_ready, lm_scores_ready = (
            sem(n) for n in ("routes_done", "best_marked", "chosen_ready", "chosen_t_done", "chosen_t_ready", "key_counts_done", "pen_ready", "lm_scores_ready"))
        s_const, s_shared, s_tokw, s_text = (sem(n) for n in ("s_const", "s_shared", "s_tokw", "s_text"))
        s_textrow = sem("s_textrow")
        s_patch = [sem(f"s_patch{i}") for i in range(2)]
        s_eatt = [sem(f"s_eatt{i}") for i in range(2)]
        s_effn = [sem(f"s_effn{i}") for i in range(2)]
        s_out = sem("s_out")
        s_init = sem("s_init")
        s_dve = sem("s_dve")
        (embedded_lo, embedded_hi, embeddings_ready, onehot_ready, onehot_t_ready, counts_done, count_t_ready, count4_ready, class_counts_done, lnarg_ready, lnn_ready,
         norm1_centred_done, norm1_sq_ready, norm1_var_done, norm1_rstd_ready, norm1_ready, lm_q_done, lm_q_ready, lm_k_done, lm_k_ready, lm_ktok_done, lm_ktok_ready, lm_v_done, lm_v_ready, centroids_done, centroids_ready,
         lm_proj_done, residual_ready, norm2_centred_done, norm2_sq_ready, norm2_var_done, norm2_rstd_ready, norm2_ready, gate_key_done, gate_key_ready, gate_scores_done, gate_less_max_ready, gate_exp_ready, gate_parts_ready, gate_t_done, gate_t_ready,
         gated_be2_done, acc_ready, out_rows_done, htok_ready, text_rows_done, outtext_ready) = (sem(n) for n in (
             "embedded_lo", "embedded_hi", "embeddings_ready", "onehot_ready", "onehot_t_ready", "counts_done", "count_t_ready", "count4_ready", "class_counts_done", "lnarg_ready", "lnn_ready",
             "norm1_centred_done", "norm1_sq_ready", "norm1_var_done", "norm1_rstd_ready", "norm1_ready", "lm_q_done", "lm_q_ready", "lm_k_done", "lm_k_ready", "lm_ktok_done", "lm_ktok_ready", "lm_v_done", "lm_v_ready",
             "centroids_done", "centroids_ready", "lm_proj_done", "residual_ready", "norm2_centred_done", "norm2_sq_ready", "norm2_var_done", "norm2_rstd_ready", "norm2_ready", "gate_key_done", "gate_key_ready", "gate_scores_done",
             "gate_less_max_ready", "gate_exp_ready", "gate_parts_ready", "gate_t_done", "gate_t_ready", "gated_be2_done", "acc_ready", "out_rows_done", "htok_ready", "text_rows_done", "outtext_ready"))
        (q_done, k_done, q_ready, k_ready, q_high_ready, k_high_ready, q_low_ready, k_low_ready, v_done, v_ready,
         wo_done, y1_ready, sq1_ready, var1_done, rstd1_ready, z_ready, x1_ready, second_ready, y2_ready, centred2_done, sq2_ready, var2_done, rstd2_ready, gate_rows_done, rstd_gate_ready, gated_ready, expert_added,
         bv_ready, cwo_done, cwo_ready, pick_ready) = (
            sem(n) for n in (
                "q_done", "k_done", "q_ready", "k_ready", "q_high_ready", "k_high_ready", "q_low_ready", "k_low_ready", "v_done", "v_ready",
                "wo_done", "y1_ready", "sq1_ready", "var1_done", "rstd1_ready", "z_ready", "x1_ready", "second_ready", "y2_ready", "centred2_done", "sq2_ready",
                "var2_done", "rstd2_ready", "gate_rows_done", "rstd_gate_ready", "gated_ready", "expert_added", "bv_ready", "cwo_done", "cwo_ready", "pick_ready"))
        hidden_done = [[sem(f"hidden_done_{i}_{k}") for k in range(2)] for i in range(FCH)]
        hidden_ready = [[sem(f"hidden_ready_{i}_{k}") for k in range(2)] for i in range(FCH)]
        log1_ready, log2_ready, norm1_log_ready, norm2_log_ready = (sem(n) for n in ("log1_ready", "log2_ready", "norm1_log_ready", "norm2_log_ready"))
        second_done = [sem(f"second_done_{i}") for i in range(FCH)]
        gate_top_ready, gate_best_ready, gate_rden_ready, gate_weights_ready, ln_ready = (sem(n) for n in ("gate_top_ready", "gate_best_ready", "gate_rden_ready", "gate_weights_ready", "ln_ready"))
        passed_dve, passed_pe, passed_pool = (sem(n) for n in ("passed_dve", "passed_pe", "passed_pool"))
        top8_ready, kept_ready = sem("top8_ready"), sem("kept_ready")
        u_chain = sem("u_chain")

        def cc(name, p=128, a=0, b=None):
            lo, hi = CCOL[name]
            return const[0:p, lo + a:(hi if b is None else lo + b)]

        def sc(name, p=128, a=0, b=None):
            lo, hi = SCOL[name]
            return shared[0:p, lo + a:(hi if b is None else lo + b)]

        def ea(par, name, a=0, b=None):
            lo, hi = ACOL[name]
            return eatt[par][:, lo + a:(hi if b is None else lo + b)]

        def ef(par, name, a=0, b=None, p=128):
            lo, hi = FCOL[name]
            return effn[par][0:p, lo + a:(hi if b is None else lo + b)]

        def halves(t):
            return t.rearrange("p (k c) -> p k c", k=2)

        block = ctx.enter_context(nc.Block())

        @block.sync
        def _(sp):
            sp.dma_start(const[:, :], const_in).then_inc(s_const, 16)
            sp.dma_start(tokw[:, :, :], tokw_in).then_inc(s_tokw, 16)
            for hf in range(2):
                sp.dma_start(patches[:, hf], x_in[0, hf]).then_inc(s_patch[hf], 16)
            sp.dma_start(shared[:, :], shared_in).then_inc(s_shared, 16)
            sp.dma_start(text_i[:, :], xt_in).then_inc(s_text, 16)

            def unit(u, last):
                sp.wait_ge(text_rows_done, u)
                sp.wait_ge(onehot_t_ready, u)
                sp.dma_start(textrow[:, :], xr_in[bass.ds(u, 1), :].broadcast_to((NT, UB * SEQT))).then_inc(s_textrow, 16)
                def load_att(e):
                    sp.wait_ge(k_ready, u * 8 + max(e - 1, 0))
                    sp.wait_ge(v_ready, u * 8 + max(e - 1, 0))
                    sp.dma_start(eatt[e % 2][:, :], eatt_in[e]).then_inc(s_eatt[e % 2], 16)

                load_att(0)
                load_att(1)
                for e in range(E):
                    sp.wait_ge(expert_added, u * 8 + max(e - 1, 0))
                    sp.dma_start(effn[e % 2][:, :], effn_in[e]).then_inc(s_effn[e % 2], 16)
                    if e + 2 < E:
                        load_att(e + 2)
                    if e == 1 and not last:
                        for hf in range(2):
                            sp.wait_ge((embedded_lo, embedded_hi)[hf], u + 1)
                            sp.dma_start(patches[:, hf], x_in[bass.ds(u + 1, 1), hf].rearrange("a p k c -> (a p) k c")).then_inc(s_patch[hf], 16)
                sp.wait_ge(htok_ready, u + 1)
                sp.dma_start(out[bass.ds(u * UB, UB), 0:T0, :].rearrange("b t d -> t b d"), htok[0:T0, :, :]).then_inc(s_out, 16)
                sp.wait_ge(outtext_ready, u + 1)
                sp.dma_start(out[bass.ds(u * UB, UB), T0:SEQ, :].rearrange("b t d -> t b d"), outtext[:, :, :]).then_inc(s_out, 16)

            with sp.Fori(0, NU - 1) as u:
                unit(u, False)
            unit(NU - 1, True)
            sp.wait_ge(s_out, NU * 32)

        @block.tensor
        def _(pe):
            mm = nc.tensor.matmul

            def over_halves(psum, lhsT, rhs, start=True, stop=True):
                for k in range(2):
                    last = mm(psum[:, k, 0:HC], lhsT, halves(rhs)[:, k], start=start, stop=stop)
                return last

            def weigh_values(N, b, par):
                img = b % UB
                pe.wait_ge(pt_main, N + b + 1 + CREDIT)
                pe.wait_ge(pt_rest, N + b + 1 + CREDIT)
                pe.wait_ge(ctx_ready, N + b + CREDIT)
                for h in range(H):
                    s = 32 * (h // 2)
                    v = vtok[par][:, img * H // 2 + h // 2, 32 * (h % 2):32 * (h % 2) + 32]
                    last = mm(pP[s:s + 32, 1, 0:NT], v, probs_t[:, b % 2, h * NT:(h + 1) * NT],
                              start=(h % 2 == 0), stop=(h % 2 == 1), tile_position=(0, s))
                last.then_inc(ctx_done, 1)

            def transpose_probs(N, b):
                pe.wait_ge(norm_ready, N + b + 1 + CREDIT)
                pe.wait_ge(pt_main, N + b + CREDIT)
                pe.wait_ge(pt_rest, N + b + CREDIT)
                pe.wait_ge(ctx_ready, N + b - 1 + CREDIT)
                for j in reversed(range(RT)):
                    o = pP[0:NT, 0, j * RP:(j + 1) * RP] if j < PTL else pP[0:NT, 1, PR0:PR0 + RP]
                    last = nc.tensor.transpose(o, probs[0:RP, b % 4, j, 0:NT], cc("I", RP, 0, RP))
                last.then_inc(pt_done, 1)

            def scores(N, b, par):
                pe.wait_ge(qx_ready, N + b + 1 + CREDIT)
                pe.wait_ge(qxl_ready, N + b + 1 + CREDIT)
                pe.wait_ge(max_ready, N + b - 1 + CREDIT)
                mm(pS[:, b % 2, 0:RT * NT], ones16[0:3, :], lnn[:, b:b + 1, :].broadcast_to((3, RT, NT)), start=True, stop=False,
                   skip_group_check=True)
                for j in range(RT):
                    o = pS[:, b % 2, j * NT:(j + 1) * NT]
                    rows = slice(j * RP, j * RP + 128)
                    cols = slice(b * NT, (b + 1) * NT)
                    mm(o, qxh[:, b % 2, rows], kh[:, par, cols], start=False, stop=False, skip_group_check=True)
                    mm(o, qxh[:, b % 2, rows], kl[:, par, cols], start=False, stop=False, skip_group_check=True)
                    last = mm(o, qxl[:, b % 2, rows], kh[:, par, cols], start=False, stop=True, skip_group_check=True)
                last.then_inc(scores_done, 1)

            def project_qk(par):
                over_halves(pA, ea(par, "wq"), xn[:, :]).then_inc(q_done, 1)
                over_halves(pB, ea(par, "wk"), xn[:, :]).then_inc(k_done, 1)

            def project_v(par):
                for b in range(UB):
                    last = mm(pA[0:NT, b // 4, (b % 4) * D:(b % 4 + 1) * D], xn[:, b * NT:(b + 1) * NT], ea(par, "wv"),
                              start=True, stop=True)
                last.then_inc(v_done, 1)

            def embed(u, c):
                hf, j = c // KJ, c % KJ
                if j == 0:
                    pe.wait_ge(s_patch[hf], (u + 1) * 16)
                done = mm(pS[:, hf, 0:4 * NP], tokw[:, j, :], patches[:, hf, j, :], start=(j == 0), stop=(j == KJ - 1))
                if j == KJ - 1:
                    done.then_inc((embedded_lo, embedded_hi)[hf], 1)

            def gate_rows(G):
                pe.wait_ge(log2_ready, G)
                pe.wait_ge(pick_ready, G)
                over_halves(pB, pick16[:, :], gate_t16[:, :]).then_inc(gate_rows_done, 1)

            def body(N, G, par, next_weights, ffn_weights, att=True, closing=True, next_unit=None):
                ffn = ffn_weights is not None

                def attend(i):
                    if att:
                        scores(N, i, par)
                    if (-3 if ffn else 0) <= i - 3 < (UB if att else 0):
                        weigh_values(N, i - 3, par if i >= 3 else 1 - par)
                    if (-2 if ffn else 0) <= i - 2 < (UB if att else 0):
                        transpose_probs(N, i - 2)

                if att:
                    pe.wait_ge(k_low_ready, G + 1)
                    pe.wait_ge(k_high_ready, G + 1)
                    pe.wait_ge(v_ready, G + 1)
                for i in range(UB):
                    if not (ffn and i == WITHIN):
                        attend(i)
                    if i == 0 and closing:
                        gate_rows(G - 1)
                    if next_unit is not None and i >= EMBED_FROM:
                        if i == EMBED_FROM:
                            pe.wait_ge(max_ready, N + CREDIT)
                        n = UB - EMBED_FROM
                        for c in range((i - EMBED_FROM) * 2 * KJ // n, (i - EMBED_FROM + 1) * 2 * KJ // n):
                            embed(next_unit, c)
                    if i == 1:
                        if ffn:
                            pe.wait_ge(s_effn[1 - par], ffn_weights)
                            pe.wait_ge(gated_ready, G - 1)
                            mm(pA[:, 0, HC:HC + D], ef(1 - par, "wo"), cc("C"), start=True, stop=True)
                            mm(pA[:, 0, HC + D:HC + D + 1], cc("C"), ef(1 - par, "bo"), start=True, stop=True).then_inc(cwo_done, 1)
                        if next_weights is not None:
                            pe.wait_ge(s_eatt[1 - par], next_weights)
                            project_qk(1 - par)
                    if i == 2 and next_weights is not None:
                        pe.wait_ge(q_ready, G + 2)
                        if ffn:
                            pe.wait_ge(cwo_ready, G)
                        project_v(1 - par)
                    if not ffn:
                        continue
                    if i == 3:
                        pe.wait_ge(ctx_ready, N + CREDIT)
                        pe.wait_ge(cwo_ready, G)
                        if next_weights is not None:
                            pe.wait_ge(k_ready, G + 2)
                        over_halves(pB, cwo[:, 0:D], cx[:, 1 - par, :, :].rearrange("p b t -> p (b t)")).then_inc(wo_done, 1)
                    elif i == 4:
                        pe.wait_ge(sq1_ready, G)
                        if next_weights is not None:
                            pe.wait_ge(v_ready, G + 2)
                        over_halves(pA, cc("J"), sqf[:, :]).then_inc(var1_done, 1)
                    elif i == 5:
                        pe.wait_ge(x1_ready, G)
                        for c in range(FCH + 1):
                            for hf in range(2):
                                if c >= 1:
                                    pe.wait_ge(hidden_ready[c - 1][hf], G)
                                if c < FCH:
                                    mm(pA[:, hf, 0:HC], ef(1 - par, "w1", c * D, (c + 1) * D), halves(x1[:, :])[:, hf],
                                       start=True, stop=True).then_inc(hidden_done[c][hf], 1)
                                if c >= 1:
                                    last = mm(pB[:, hf, 0:HC], ef(1 - par, "w2", (c - 1) * D, c * D), halves(g[:, (c - 1) % 2, :])[:, hf],
                                              start=(c == 1), stop=(c == FCH), skip_group_check=True)
                            if c >= 1:
                                last.then_inc(second_done[c - 1], 1)
                            if att and c == 0:
                                attend(WITHIN)
                    elif i == 6:
                        pe.wait_ge(y2_ready, G)
                        over_halves(pA, cc("C"), y[:, :]).then_inc(centred2_done, 1)
                    elif i == 7:
                        pe.wait_ge(sq2_ready, G)
                        over_halves(pB, cc("J"), sqf[:, :]).then_inc(var2_done, 1)
                if not att:
                    gate_rows(G)

            pe.wait_ge(s_const, 16)
            pe.wait_ge(s_tokw, 16)
            pe.wait_ge(s_shared, 16)
            pe.wait_ge(s_init, 1)
            for c in range(2 * KJ):
                embed(0, c)

            def unit(u, last_unit):
                pe.wait_ge(embeddings_ready, 2 * u + 2)
                pe.wait_ge(outtext_ready, u)
                over_halves(pB, cc("C"), hA[:, :, :].rearrange("p b t -> p (b t)")).then_inc(norm1_centred_done, 1)
                pe.wait_ge(onehot_ready, u + 1)
                for k in range(2):
                    last = mm(pP[0:SEGS, k, 0:4 * NTP], segof[:, :], onehot[:, 4 * k:4 * k + 4, :].rearrange("p b t -> p (b t)"),
                              start=True, stop=True)
                last.then_inc(counts_done, 1)
                for b in range(UB):
                    last = mm(pS[0:NTP, 0, b * SEGS:(b + 1) * SEGS], onehot[:, b, :], segof[:, :], start=True, stop=True)
                last = mm(pS[0:3, 1, 0:UB * NCLS], ones16[:, 0:3], onehot[:, :, T0:NT], start=True, stop=True)
                last.then_inc(class_counts_done, 1)
                pe.wait_ge(norm1_sq_ready, u + 1)
                pe.wait_ge(htok_ready, u)
                over_halves(pA, cc("J"), sq[:, :]).then_inc(norm1_var_done, 1)
                pe.wait_ge(norm1_ready, u + 1)
                over_halves(pA, sc("wq"), xn[:, :]).then_inc(lm_q_done, 1)
                over_halves(pB, sc("wk"), xn[:, :]).then_inc(lm_k_done, 1)
                pe.wait_ge(lm_q_ready, u + 1)
                for b in range(UB):
                    last = mm(pA[0:NT, b // 4, (b % 4) * D:(b % 4 + 1) * D], xn[:, b * NT:(b + 1) * NT], sc("wk"), start=True, stop=True)
                last.then_inc(lm_ktok_done, 1)
                pe.wait_ge(lm_ktok_ready, u + 1)
                pe.wait_ge(lm_k_ready, u + 1)
                for b in range(UB):
                    last = mm(pA[0:NT, b // 4, (b % 4) * D:(b % 4 + 1) * D], xn[:, b * NT:(b + 1) * NT], sc("wv"), start=True, stop=True)
                last.then_inc(lm_v_done, 1)
                pe.wait_ge(count4_ready, u + 1)
                for b in range(UB):
                    last = mm(pB[:, 0, b * SEGS:(b + 1) * SEGS], ktok[:, b * D:(b + 1) * D], count4[0:NT, b, :], start=True, stop=True)
                last.then_inc(centroids_done, 1)
                pe.wait_ge(centroids_ready, u + 1)
                pe.wait_ge(lm_v_ready, u + 1)
                pe.wait_ge(count_t_ready, u + 1)
                pe.wait_ge(lnn_ready, u + 1)
                NB = pe.snap(u * 72)
                LB = pe.snap(u * 8)
                for i in range(NSTEP):
                    b = i - 2
                    if 0 <= b < UB:
                        pe.wait_ge(chosen_ready, LB + b + 1)
                        pe.wait_ge(chosen_t_ready, LB + b)
                        pe.sem_inc(passed_pe, 1)
                        pt = pB[0:SEGS, 0, 0:RT * RP // 2].bitcast(BF16)
                        for j in range(RT):
                            last = nc.tensor.transpose(pt[:, j * RP:(j + 1) * RP], chosen[0:RP, j, :], ident16[0:RP, 0:RP])
                        last.then_inc(chosen_t_done, 1)
                    b = i
                    if b < UB:
                        pe.wait_ge(qx_ready, NB + b + 1 + CREDIT)
                        if b >= 2:
                            pe.wait_ge(best_marked, LB + b - 1)
                        mm(pA[:, b % 2, 0:RT * RW], ones16[0:1, :], sentinel[:, :, :].rearrange("p j w -> p (j w)"),
                           start=True, stop=False, skip_group_check=True)
                        for j in range(RT):
                            last = mm(pA[:, b % 2, j * RW:(j + 1) * RW], qxf[:, b % 3, j * RP:j * RP + 128], klm[:, b, NTP:NTP + RW],
                                      start=False, stop=True, skip_group_check=True)
                        last.then_inc(routes_done, 1)
                    b = i - 2
                    if 0 <= b < UB:
                        pe.wait_ge(chosen_t_ready, LB + b + 1)
                        pe.wait_ge(rden_ready, NB + b + CREDIT)
                        for j in range(RT):
                            last = mm(pB[:, 1, j * NTP:(j + 1) * NTP], chosen_t[:, j * RP:j * RP + 128], count_t[:, b, :], start=True, stop=True)
                        last.then_inc(key_counts_done, 1)
                    b = i - 1
                    if 0 <= b < UB:
                        if b >= 2:
                            pe.wait_ge(lm_scores_ready, LB + b - 1)
                        for j in range(RT):
                            last = mm(pS[:, b % 2, j * NTP:(j + 1) * NTP], qxf[:, b % 3, j * RP:j * RP + 128], klm[:, b, 0:NTP],
                                      start=True, stop=True)
                        last.then_inc(scores_done, 1)
                    if 0 <= i - 4 < UB:
                        weigh_values(NB, i - 4, 1)
                    if 0 <= i - 3 < UB:
                        transpose_probs(NB, i - 3)
                pe.wait_ge(ctx_ready, NB + UB + CREDIT)
                over_halves(pA, sc("wp"), cx[:, 1, :, :].rearrange("p b t -> p (b t)")).then_inc(lm_proj_done, 1)
                pe.wait_ge(residual_ready, u + 1)
                over_halves(pB, cc("C"), hB[:, :]).then_inc(norm2_centred_done, 1)
                pe.wait_ge(norm2_sq_ready, u + 1)
                over_halves(pA, cc("J"), sq[:, :]).then_inc(norm2_var_done, 1)
                pe.wait_ge(norm2_ready, u + 1)
                over_halves(pA, sc("gwk"), xn[:, :]).then_inc(gate_key_done, 1)
                pe.wait_ge(gate_key_ready, u + 1)
                for j in range(RT):
                    last = mm(pS[0:RP, 0, j * E:(j + 1) * E], qf[:, j * RP:(j + 1) * RP], sc("eq"), start=True, stop=True)
                last.then_inc(gate_scores_done, 1)
                pe.wait_ge(s_eatt[0], u * 64 + 16)
                project_qk(0)
                pe.wait_ge(q_ready, u * 8 + 1)
                project_v(0)
                pe.wait_ge(gate_parts_ready, u + 1)
                for j in range(RT):
                    last = nc.tensor.transpose(pP[0:NPART * E, j // 4, (j % 4) * RP:(j % 4 + 1) * RP],
                                               gsum[:, j, :, :].rearrange("p n e -> p (n e)"), cc("I", RP, 0, RP))
                last.then_inc(gate_t_done, 1)
                pe.wait_ge(gate_t_ready, 2 * u + 2)
                pe.wait_ge(v_ready, u * 8 + 1)
                over_halves(pA, sc("be2", NPART * E), gate_t[:, :]).then_inc(gated_be2_done, 1)
                pe.wait_ge(acc_ready, u + 1)

                body(pe.snap(u * 72 + 8), pe.snap(u * 8), 0, pe.snap(u * 64 + 16), None, closing=False)
                body(pe.snap(u * 72 + 16), pe.snap(u * 8 + 1), 1, pe.snap(u * 64 + 32), pe.snap(u * 64 + 16), closing=False)
                with pe.Fori(0, 2) as t:
                    body(pe.snap(u * 72 + 24 + t * 16), pe.snap(u * 8 + 2 + t * 2), 0,
                         pe.snap(u * 64 + t * 16 + 32), pe.snap(u * 64 + t * 16 + 16))
                    body(pe.snap(u * 72 + 32 + t * 16), pe.snap(u * 8 + 3 + t * 2), 1,
                         pe.snap(u * 64 + t * 16 + 48), pe.snap(u * 64 + t * 16 + 32))
                body(pe.snap(u * 72 + 56), pe.snap(u * 8 + 6), 0, pe.snap(u * 64 + 64), pe.snap(u * 64 + 48))
                body(pe.snap(u * 72 + 64), pe.snap(u * 8 + 7), 1, None, pe.snap(u * 64 + 64))
                body(pe.snap(u * 72 + 72), pe.snap(u * 8 + 8), 0, None, pe.snap(u * 64 + 64), att=False,
                     next_unit=None if last_unit else u + 1)
                pe.wait_ge(expert_added, u * 8 + 8)
                for b in range(UB):
                    last = nc.tensor.transpose(pA[0:NT, b // 4, (b % 4) * D:(b % 4 + 1) * D], acc[:, b * NT:(b + 1) * NT], cc("I"))
                last.then_inc(out_rows_done, 1)
                pe.wait_ge(htok_ready, u + 1)
                pe.wait_ge(onehot_t_ready, u + 1)
                for b in range(UB):
                    last = mm(pB[:, b // 4, (b % 4) * D:(b % 4 + 1) * D], onehot_t[:, b, :], htok[:, b, :], start=True, stop=True)
                last.then_inc(text_rows_done, 1)

            with pe.Fori(0, NU - 1) as u:
                unit(u, False)
            unit(NU - 1, True)

        @block.scalar
        def _(act):
            def A(out_, in_, f, **kw):
                return nc.scalar.activation(out_, in_, f, **kw)

            def evac_probs(N, b):
                act.wait_ge(pt_done, N + b + 1 + CREDIT)
                act.wait_ge(ctx_done, N + b - 1 + CREDIT)
                A(probs_t[:, b % 2, 0:PTL * RP], pP[0:NT, 0, 0:PTL * RP], ACT.Copy).then_inc(pt_main, 1)
                A(probs_t[:, b % 2, PTL * RP:RT * RP], pP[0:NT, 1, PR0:PR0 + RP], ACT.Copy).then_inc(pt_rest, 1)

            def evac_ctx(N, b, par, bias=True, last=False):
                act.wait_ge(ctx_done, N + b + 1 + CREDIT)
                if not last:
                    act.wait_ge(pt_done, N + b + 2 + CREDIT)
                kw = dict(bias=bvc[:, par:par + 1]) if bias else {}
                A(cx[:, par, b % UB, :], pP[:, 1, 0:NT], ACT.Identity, **kw).then_inc(ctx_ready, 1)

            def exps(N, b):
                act.wait_ge(max_ready, N + b + 1 + CREDIT)
                p = probs[0:RP, b % 4, :, 0:NT]
                A(p, p, ACT.Exp).then_inc(exp_done, 1)

            def project_q(G, par):
                act.wait_ge(q_done, G + 1)
                A(halves(qf[:, :]), pAu, ACT.Identity, bias=ea(par, "bq"), scale=1.0).then_inc(q_ready, 1)

            def project_k(G, par):
                act.wait_ge(k_ready, G + 1)
                A(kh[:, par, :], kf[:, :], ACT.Copy).then_inc(k_high_ready, 1)

            def spread(par):
                return vtok[par][:, :, :].rearrange("p q (a d) -> p q a d", a=4)[:, :, 0:4:3, :]

            def project_v(N, G, par):
                act.wait_ge(ctx_ready, N + CREDIT)
                A(bvc[:, par:par + 1], ea(par, "bv"), ACT.Copy).then_inc(bv_ready, 1)
                act.wait_ge(bv_ready, G + 1)
                act.wait_ge(v_done, G + 1)
                A(spread(par), pA[0:NT, :, :].rearrange("p k (q a d) -> p (k q) a d", a=2, d=DH), ACT.Copy).then_inc(v_ready, 1)

            def rstd(psum, buf, v, l, r, n):
                act.wait_ge(v, n)
                A(halves(buf[:, :]), psum, ACT.Ln, bias=epsc[:, 0:1]).then_inc(l, 1)
                act.wait_ge(l, n)
                A(buf[:, :], buf[:, :], ACT.Exp, scale=-0.5).then_inc(r, 1)

            def body(N, G, par, next_weights, ffn_weights, att=True):
                ffn = ffn_weights is not None

                def evacs(i):
                    if (-2 if ffn else 0) <= i - 2 < (UB if att else 0):
                        evac_probs(N, i - 2)
                    if (-3 if ffn else 0) <= i - 3 < (UB if att else 0):
                        evac_ctx(N, i - 3, par if i >= 3 else 1 - par, last=(not att and i == 2))

                for i in range(UB):
                    if ffn and i == 5:
                        rstd(pAu, rsf, var1_done, log1_ready, rstd1_ready, G)
                    if ffn and i == 4:
                        act.wait_ge(y1_ready, G)
                        A(sqf[:, :], y[:, :], ACT.Square).then_inc(sq1_ready, 1)
                    if not (ffn and i == WITHIN):
                        evacs(i)
                    if att:
                        exps(N, i)
                    if next_weights is not None:
                        if i == 1:
                            act.wait_ge(s_eatt[1 - par], next_weights)
                            project_q(G + 1, 1 - par)
                        elif i == 2:
                            project_k(G + 1, 1 - par)
                        elif i == 3:
                            project_v(N, G + 1, 1 - par)
                    if not ffn:
                        continue
                    if i == 5:
                        act.preload_act_table_set("gelu_and_others")
                        act.wait_ge(s_effn[1 - par], ffn_weights)
                        for c in range(FCH):
                            if c >= 2:
                                act.wait_ge(second_done[c - 2], G)
                            for hf in range(2):
                                act.wait_ge(hidden_done[c][hf], G)
                                A(halves(g[:, c % 2, :])[:, hf], pA[:, hf, 0:HC], ACT.Gelu, bias=ef(1 - par, "bf1", c, c + 1))\
                                    .then_inc(hidden_ready[c][hf], 1)
                            if att and c == 0:
                                evacs(WITHIN)
                        act.wait_ge(second_done[FCH - 1], G)
                        A(halves(z[:, :]), pBu, ACT.Gelu, bias=ef(1 - par, "bf2")).then_inc(second_ready, 1)
                        act.preload_act_table_set(LN_EXP)
                    elif i == 6:
                        act.wait_ge(centred2_done, G)
                        A(halves(sqf[:, :]), pAu, ACT.Square).then_inc(sq2_ready, 1)
                    elif i == 7:
                        rstd(pBu, rsf, var2_done, log2_ready, rstd2_ready, G)

            for s in (exp_done, pt_rest, pt_main, ctx_ready):
                act.sem_inc(s, CREDIT)
            act.wait_ge(s_const, 16)
            act.wait_ge(s_init, 1)
            act.preload_act_table_set(LN_EXP)
            with act.Fori(0, NU) as u:
                act.wait_ge(norm1_centred_done, u + 1)
                A(halves(sq[:, :]), pBu, ACT.Square).then_inc(norm1_sq_ready, 1)
                rstd(pAu, rs, norm1_var_done, norm1_log_ready, norm1_rstd_ready, u + 1)
                act.wait_ge(lm_ktok_done, u + 1)
                A(ktok[:, :].rearrange("p (k c) -> p k c", k=2), pA[0:NT, :, :], ACT.Copy).then_inc(lm_ktok_ready, 1)
                act.wait_ge(lm_v_done, u + 1)
                A(spread(1), pA[0:NT, :, :].rearrange("p k (q a d) -> p (k q) a d", a=2, d=DH), ACT.Copy).then_inc(lm_v_ready, 1)
                act.wait_ge(lnarg_ready, u + 1)
                A(lnw[:, 2, :], lnw[:, 1, :], ACT.Ln).then_inc(ln_ready, 1)
                act.wait_ge(centroids_done, u + 1)
                A(klm[:, :, NTP:NTP + SEGS], pB[:, 0, :].rearrange("p (b m) -> p b m", b=UB), ACT.Copy).then_inc(centroids_ready, 1)
                NB = act.snap(u * 72)
                LB = act.snap(u * 8)
                for i in range(NSTEP):
                    b = i - 2
                    if 0 <= b < UB:
                        act.wait_ge(chosen_t_done, LB + b + 1)
                        act.wait_ge(key_counts_done, LB + b)
                        A(chosen_t[:, 0:RT * RP], pB[0:SEGS, 0, 0:RT * RP // 2].bitcast(BF16), ACT.Copy).then_inc(chosen_t_ready, 1)
                        act.wait_ge(key_counts_done, LB + b + 1)
                        act.wait_ge(lm_scores_ready, LB + b)
                        A(pen[0:RP, :, :].rearrange("p j t -> p (j t)"), pB[0:RP, 1, 0:RT * NTP], ACT.Identity, bias=bigneg[0:RP, 0:1], scale=2e30)\
                            .then_inc(pen_ready, 1)
                    if 0 <= i - 3 < UB:
                        evac_probs(NB, i - 3)
                    if 0 <= i - 4 < UB:
                        evac_ctx(NB, i - 4, 1, bias=False, last=(i - 4 == UB - 1))
                    if 0 <= b < UB:
                        act.wait_ge(lm_scores_ready, LB + b + 1)
                        A(probs[0:RP, b % 4, :, :], probs[0:RP, b % 4, :, :], ACT.Exp).then_inc(exp_done, 1)
                act.wait_ge(norm2_centred_done, u + 1)
                A(halves(sq[:, :]), pBu, ACT.Square).then_inc(norm2_sq_ready, 1)
                rstd(pAu, rs, norm2_var_done, norm2_log_ready, norm2_rstd_ready, u + 1)
                act.wait_ge(gate_less_max_ready, u + 1)
                A(gate[:, 1], gate[:, 0], ACT.Exp, scale=float(D) ** -0.5).then_inc(gate_exp_ready, 1)

                act.wait_ge(s_eatt[0], u * 64 + 16)
                G = act.snap(u * 8)
                project_q(G, 0)
                project_k(G, 0)
                project_v(act.snap(u * 72 + 8), G, 0)
                body(act.snap(u * 72 + 8), act.snap(u * 8), 0, act.snap(u * 64 + 16), None)
                body(act.snap(u * 72 + 16), act.snap(u * 8 + 1), 1, act.snap(u * 64 + 32), act.snap(u * 64 + 16))
                with act.Fori(0, 2) as t:
                    body(act.snap(u * 72 + 24 + t * 16), act.snap(u * 8 + 2 + t * 2), 0,
                         act.snap(u * 64 + t * 16 + 32), act.snap(u * 64 + t * 16 + 16))
                    body(act.snap(u * 72 + 32 + t * 16), act.snap(u * 8 + 3 + t * 2), 1,
                         act.snap(u * 64 + t * 16 + 48), act.snap(u * 64 + t * 16 + 32))
                body(act.snap(u * 72 + 56), act.snap(u * 8 + 6), 0, act.snap(u * 64 + 64), act.snap(u * 64 + 48))
                body(act.snap(u * 72 + 64), act.snap(u * 8 + 7), 1, None, act.snap(u * 64 + 64))
                body(act.snap(u * 72 + 72), act.snap(u * 8 + 8), 0, None, act.snap(u * 64 + 64), att=False)
                act.wait_ge(out_rows_done, u + 1)
                act.wait_ge(s_out, u * 32)
                A(htok[:, :, :].rearrange("p (k b) d -> p k (b d)", k=2), pA[0:NT, :, :], ACT.Copy).then_inc(htok_ready, 1)

        @block.gpsimd
        def _(pool):
            pool.sem_inc(norm_ready, CREDIT)
            pool.sem_inc(qxl_ready, CREDIT)
            pool.wait_ge(s_init, 1)

            def norm(N, b, w):
                pool.wait_ge(rden_ready, N + b + 1 + CREDIT)
                p = probs[0:RP, b % 4, :, 0:w]
                nc.gpsimd.tensor_tensor(p, p, rden[0:RP, b % 4, :, None].broadcast_to((RP, RT, w)), ALU.mult).then_inc(norm_ready, 1)

            def mask_f(N, b):
                pool.wait_ge(scores_done, N + b - 2 + CREDIT)
                nc.gpsimd.tensor_tensor(qxf[:, b % 3, 0:H * NT].rearrange("p (h t) -> p h t", h=H), maskf[:, :, :],
                                        qf[:, None, b * NT:(b + 1) * NT].broadcast_to((128, H, NT)), ALU.mult).then_inc(qx_ready, 1)

            def mark_chosen(L, b):
                pool.wait_ge(best_marked, L + b + 1)
                pool.wait_ge(chosen_t_done, L + b)
                pool.sem_inc(passed_pool, 1)
                nc.gpsimd.tensor_scalar(chosen[0:RP, :, :], routed[0:RP, :, 0:SEGS], -2e38, None, ALU.is_le).then_inc(chosen_ready, 1)

            def low_q(G, par):
                pool.wait_ge(q_high_ready, G + 1)
                nc.gpsimd.tensor_tensor(ql[:, par, :], qf[:, :], qh[:, par, :], ALU.subtract).then_inc(q_low_ready, 1)

            def low_k(G, par):
                pool.wait_ge(k_high_ready, G + 1)
                nc.gpsimd.tensor_tensor(kl[:, par, :], kf[:, :], kh[:, par, :], ALU.subtract).then_inc(k_low_ready, 1)

            def body(N, G, par, next_weights, ffn_weights, att=True):
                for i in range(UB if att else 1):
                    if i >= 1 or ffn_weights is not None:
                        norm(N, i - 1, NT)
                    if next_weights is not None:
                        if i == 3:
                            low_q(G + 1, 1 - par)
                        elif i == 4:
                            low_k(G + 1, 1 - par)

            with pool.Fori(0, NU) as u:
                NB = pool.snap(u * 72)
                LB = pool.snap(u * 8)
                pool.wait_ge(lm_q_ready, u + 1)
                mask_f(NB, 0)
                for i in range(NSTEP):
                    if i + 1 < UB:
                        mask_f(NB, i + 1)
                    if 0 <= i - 1 < UB:
                        mark_chosen(LB, i - 1)
                    if 0 <= i - 2 < UB:
                        norm(NB, i - 2, NTP)
                        pool.sem_inc(qxl_ready, 1)
                low_q(pool.snap(u * 8), 0)
                low_k(pool.snap(u * 8), 0)
                body(pool.snap(u * 72 + 8), pool.snap(u * 8), 0, True, None)
                body(pool.snap(u * 72 + 16), pool.snap(u * 8 + 1), 1, True, True)
                with pool.Fori(0, 2) as t:
                    body(pool.snap(u * 72 + 24 + t * 16), pool.snap(u * 8 + 2 + t * 2), 0,
                         True, True)
                    body(pool.snap(u * 72 + 32 + t * 16), pool.snap(u * 8 + 3 + t * 2), 1,
                         True, True)
                body(pool.snap(u * 72 + 56), pool.snap(u * 8 + 6), 0, True, True)
                body(pool.snap(u * 72 + 64), pool.snap(u * 8 + 7), 1, None, True)
                body(pool.snap(u * 72 + 72), pool.snap(u * 8 + 8), 0, None, True, att=False)

        @block.vector
        def _(dve):
            V = nc.vector
            for s in (qx_ready, scores_done, neg_ready, den_ready, max_ready, rden_ready, pt_done, ctx_done):
                dve.sem_inc(s, CREDIT)

            def bc(ap, dim, n):
                shape = list(ap.shape)
                shape[dim] = n
                return ap.broadcast_to(tuple(shape))

            dve.wait_ge(s_const, 16)
            dve.wait_ge(s_shared, 16)
            dve.wait_ge(s_text, 16)
            n = 0
            for ins in (
                lambda: V.tensor_copy(segof[:, :], cc("A")),
                lambda: V.tensor_copy(ident16[:, :], cc("I")),
                lambda: V.tensor_scalar(mask16[:, :, :].rearrange("p h t -> p (h t)"), cc("mask"), SCALE, None, ALU.mult),
                lambda: V.tensor_scalar(maskf[:, :, :].rearrange("p h t -> p (h t)"), cc("mask"), SCALE, None, ALU.mult),
                lambda: V.memset(ones16[:, :], 1.0),
                lambda: V.memset(sentinel[:, :, 0:SEGS], 0.0),
                lambda: V.memset(sentinel[:, :, SEGS:RW], 1e38),
                lambda: V.memset(epsc[:, :], EPS),
                lambda: V.memset(bigneg[:, :], -1e30),
                lambda: V.memset(lnn[:, :, :], 0.0),
                lambda: V.memset(qxh[:, :, :], 0.0),
                lambda: V.memset(qxl[:, :, :], 0.0),
                lambda: V.memset(qxf[:, :, :], 0.0),
                lambda: V.memset(klm[:, :, :], 0.0),
                lambda: V.memset(chosen_t[:, :], 0.0),
                lambda: V.memset(vtok[0][:, :, :], 0.0),
                lambda: V.memset(vtok[1][:, :, :], 0.0),
                lambda: V.memset(gall[:, :, 0:6], 4.0),
                lambda: V.tensor_copy(text_f[:, :], text_i[:, :]),
                lambda: V.tensor_scalar(hA[:, :, 0:1], bc(sc("pos", 128, 0, 1)[:, None, :], 1, UB), sc("cls"), None, ALU.mult),
                lambda: V.tensor_scalar(hA[:, :, T0:NT], bc(sc("txtw")[:, None, :], 1, UB), sc("txtb"), None, ALU.add),
            ):
                n += 1
                ins().then_inc(s_dve, 1)
            dve.wait_ge(s_dve, n)
            dve.sem_inc(s_init, 1)

            def mask_high(N, b, par):
                dve.wait_ge(scores_done, N + b - 1 + CREDIT)
                c = b % UB * NT
                V.tensor_tensor(qxh[:, b % 2, 0:H * NT].rearrange("p (h t) -> p h t", h=H), mask16[:, :, :],
                                bc(qh[:, par, c:c + NT][:, None, :], 1, H), ALU.mult).then_inc(qx_ready, 1)

            def mask_low(N, b, par):
                dve.wait_ge(scores_done, N + b - 1 + CREDIT)
                c = b % UB * NT
                V.tensor_tensor(qxl[:, b % 2, 0:H * NT].rearrange("p (h t) -> p h t", h=H), mask16[:, :, :],
                                        ql[:, par, c:c + NT][:, None, :].broadcast_to((128, H, NT)), ALU.mult).then_inc(qxl_ready, 1)

            def less_max(N, b):
                scores_b = pS[0:RP, b % 2, 0:RT * NT].rearrange("p (j t) -> p j t", j=RT)
                dve.wait_ge(scores_done, N + b + 1 + CREDIT)
                V.tensor_reduce(negmax[0:RP, b % 2, :], scores_b, AX, ALU.max, negate=True).then_inc(neg_ready, 1)
                dve.wait_ge(neg_ready, N + b + 1 + CREDIT)
                dve.wait_ge(pt_done, N + b - 2 + CREDIT)
                V.tensor_tensor(probs[0:RP, b % 4, :, 0:NT], scores_b, bc(negmax[0:RP, b % 2, :, None], 2, NT), ALU.add)\
                    .then_inc(max_ready, 1)

            def denominators(N, b):
                dve.wait_ge(exp_done, N + b + 1 + CREDIT)
                V.tensor_reduce(den[0:RP, b % 4, :], probs[0:RP, b % 4, :, 0:NT], AX, ALU.add).then_inc(den_ready, 1)
                dve.wait_ge(den_ready, N + b + 1 + CREDIT)
                dve.wait_ge(norm_ready, N + b - 2 + CREDIT)
                V.reciprocal(rden[0:RP, b % 4, :], den[0:RP, b % 4, :]).then_inc(rden_ready, 1)

            def project_q(G, par):
                dve.wait_ge(q_ready, G + 1)
                V.tensor_copy(qh[:, par, :], qf[:, :]).then_inc(q_high_ready, 1)

            def project_k(G, par):
                dve.wait_ge(k_done, G + 1)
                V.tensor_scalar(halves(kf[:, :]), pBu, ea(par, "bk"), None, ALU.add).then_inc(k_ready, 1)

            def add_expert(G, par):
                dve.wait_ge(gate_rows_done, G)
                dve.wait_ge(rstd2_ready, G)
                V.tensor_tensor(halves(rsf[:, :]), pBu, halves(rsf[:, :]), ALU.mult).then_inc(rstd_gate_ready, 1)
                dve.wait_ge(rstd_gate_ready, G)
                V.tensor_tensor(halves(z[:, :]), pAu, halves(rsf[:, :]), ALU.mult).then_inc(gated_ready, 1)

            def accumulate(G, par):
                dve.wait_ge(gated_ready, G)
                V.scalar_tensor_tensor(acc[:, :], z[:, :], ef(par, "g2"), acc[:, :], ALU.mult, ALU.add).then_inc(expert_added, 1)

            def body(N, G, par, next_weights, ffn_weights, att=True, closing=True):
                ffn = ffn_weights is not None
                for i in range(UB):
                    if att and i + 1 < UB:
                        mask_high(N, i + 1, par)
                        mask_low(N, i + 1, par)
                    elif att and next_weights is not None:
                        dve.wait_ge(q_high_ready, G + 2)
                        mask_high(N, UB, 1 - par)
                        dve.wait_ge(q_low_ready, G + 2)
                        mask_low(N, UB, 1 - par)
                    if (att and i >= 1) or (i == 0 and ffn):
                        denominators(N, i - 1)
                    if i == 5 and ffn:
                        dve.wait_ge(rstd1_ready, G)
                        V.tensor_tensor(z[:, :], y[:, :], rsf[:, :], ALU.mult).then_inc(z_ready, 1)
                        dve.wait_ge(z_ready, G)
                        V.tensor_scalar(x1[:, :], z[:, :], ef(1 - par, "g1"), ef(1 - par, "be1"), ALU.mult, ALU.add).then_inc(x1_ready, 1)
                    if att:
                        less_max(N, i)
                    if i == 0 and closing:
                        add_expert(G - 1, par)
                    if i == 1 and closing:
                        accumulate(G - 1, par)
                    if i == 1:
                        if next_weights is not None:
                            dve.wait_ge(s_eatt[1 - par], next_weights)
                            project_k(G + 1, 1 - par)
                        if ffn:
                            dve.wait_ge(s_effn[1 - par], ffn_weights)
                            dve.wait_ge(cwo_done, G)
                            if next_weights is not None:
                                dve.wait_ge(q_ready, G + 2)
                            V.tensor_copy(cwo[:, :], pA[:, 0, HC:HC + D + 1]).then_inc(cwo_ready, 1)
                            V.tensor_copy(pick16[:, :], ef(1 - par, "pick", p=NPART * E)).then_inc(pick_ready, 1)
                    elif i == 2 and next_weights is not None:
                        project_q(G + 1, 1 - par)
                    if not ffn:
                        continue
                    if i == 3:
                        dve.wait_ge(wo_done, G)
                        V.scalar_tensor_tensor(halves(y[:, :]), pBu, cwo[:, D:D + 1], halves(xn[:, :]), ALU.add, ALU.add).then_inc(y1_ready, 1)
                    elif i == 6:
                        dve.wait_ge(second_ready, G)
                        V.tensor_tensor(y[:, :], z[:, :], x1[:, :], ALU.add).then_inc(y2_ready, 1)
                if not att:
                    add_expert(G, 1 - par)
                    accumulate(G, 1 - par)

            NUCH = 19

            with dve.Fori(0, NU) as u:
                CH = dve.snap(u * NUCH)
                links = [0]

                def link(ins, own=False):
                    links[0] += 1
                    ins.then_inc(u_chain, 1)
                    dve.wait_ge(u_chain, CH + links[0])
                    if own:
                        dve.sem_inc(passed_dve, 1)

                for hf in range(2):
                    dve.wait_ge((embedded_lo, embedded_hi)[hf], u + 1)
                    V.scalar_tensor_tensor(hA[:, 4 * hf:4 * hf + 4, 1:T0], pS[:, hf, 0:4 * NP].rearrange("p (b t) -> p b t", b=4),
                                           sc("tokb"), bc(sc("pos", 128, 1, 1 + NP)[:, None, :], 1, 4), ALU.add, ALU.mult)\
                        .then_inc(embeddings_ready, 1)
                dve.wait_ge(class_counts_done, u)
                dve.wait_ge(counts_done, u)
                V.tensor_tensor(onehot[:, :, :], bc(text_f[:, bass.ds(u * UB, UB)][:, :, None], 2, NTP), bc(cc("tcol")[:, None, :], 1, UB),
                                ALU.is_equal).then_inc(onehot_ready, 1)
                dve.wait_ge(s_textrow, u * 16 + 16)
                dve.wait_ge(text_rows_done, u)
                V.tensor_scalar(onehot_t[:, :, :].rearrange("p b j -> p (b j)"), textrow[:, :], cc("tval", NT), None, ALU.is_equal)\
                    .then_inc(onehot_t_ready, 1)
                dve.wait_ge(counts_done, u + 1)
                for k in range(2):
                    last = V.tensor_tensor(count_t[:, 4 * k:4 * k + 4, :], pP[0:SEGS, k, 0:4 * NTP].rearrange("p (b t) -> p b t", b=4),
                                           bc(cc("MT", SEGS)[:, None, :], 1, 4), ALU.add)
                last.then_inc(count_t_ready, 1)
                dve.wait_ge(class_counts_done, u + 1)
                V.scalar_tensor_tensor(count4[:, :, :], pS[0:NTP, 0, :].rearrange("p (b m) -> p b m", b=UB), 1.0 / SEGL,
                                       bc(cc("M4", NTP)[:, None, :], 1, UB), ALU.mult, ALU.add).then_inc(count4_ready, 1)
                dve.wait_ge(norm1_rstd_ready, u + 1)
                V.tensor_tensor(halves(xn[:, :]), pBu, halves(rs[:, :]), ALU.mult).then_inc(norm1_ready, 1)
                dve.wait_ge(lm_q_done, u + 1)
                V.tensor_copy(halves(qf[:, :]), pAu).then_inc(lm_q_ready, 1)
                dve.wait_ge(lm_k_done, u + 1)
                for k in range(2):
                    last = V.tensor_copy(klm[:, 4 * k:4 * k + 4, 0:NT], pB[:, k, 0:HC].rearrange("p (b t) -> p b t", b=4))
                last.then_inc(lm_k_ready, 1)
                link(V.tensor_copy(lnw[:, 0, :], pS[0:3, 1, 0:UB * NCLS]))
                V.tensor_scalar(lnw[:, 1, :], lnw[:, 0, :], 1.0, None, ALU.max).then_inc(lnarg_ready, 1)
                link(V.tensor_scalar(lnw[:, 3, :], lnw[:, 0, :], 0.5, -1e30, ALU.is_lt, ALU.mult))
                dve.wait_ge(ln_ready, u + 1)
                link(V.tensor_tensor(lnw[:, 4, :], lnw[:, 2, :], lnw[:, 3, :], ALU.add))
                link(V.tensor_copy(lnpart[:, 0, :], lnw[:, 4, :]))
                link(V.tensor_tensor(lnw[:, 5, :], lnw[:, 4, :], lnpart[:, 0, :], ALU.subtract))
                link(V.tensor_copy(lnpart[:, 1, :], lnw[:, 5, :]))
                link(V.tensor_tensor(lnpart[:, 2, :], lnw[:, 5, :], lnpart[:, 1, :], ALU.subtract))
                link(V.tensor_scalar(lnw[:, 6, :], lnpart[:, 0, :], cc("I", 3, 0, 1), None, ALU.mult))
                link(V.scalar_tensor_tensor(lnw[:, 7, :], lnpart[:, 1, :], cc("I", 3, 1, 2), lnw[:, 6, :], ALU.mult, ALU.add))
                V.scalar_tensor_tensor(lnn[:, :, T0:NT], lnpart[:, 2, :].rearrange("p (b c) -> p b c", b=UB), cc("I", 3, 2, 3),
                                       lnw[:, 7, :].rearrange("p (b c) -> p b c", b=UB), ALU.mult, ALU.add).then_inc(lnn_ready, 1)
                dve.wait_ge(lm_q_ready, u + 1)
                NB = dve.snap(u * 72)
                LB = dve.snap(u * 8)

                def choose(b):
                    dve.wait_ge(routes_done, LB + b + 1)
                    dve.wait_ge(best_marked, LB + b)
                    dve.sem_inc(passed_dve, 1)
                    for j in range(RT):
                        last = V.max(top8[0:RP, j, :], pA[0:RP, b % 2, j * RW:(j + 1) * RW])
                    last.then_inc(top8_ready, 1)
                    dve.wait_ge(top8_ready, LB + b + 1)
                    dve.wait_ge(chosen_ready, LB + b)
                    dve.sem_inc(passed_dve, 1)
                    for j in range(RT):
                        last = V.match_replace(routed[0:RP, j, :], top8[0:RP, j, :], pA[0:RP, b % 2, j * RW:(j + 1) * RW], -3e38)
                    last.then_inc(best_marked, 1)

                def scores_of_chosen(b):
                    dve.wait_ge(scores_done, NB + b + 1 + CREDIT)
                    dve.wait_ge(pen_ready, LB + b + 1)
                    s = pS[0:RP, b % 2, 0:RT * NTP].rearrange("p (j t) -> p j t", j=RT)
                    V.tensor_tensor(kept[0:RP, :, :], pen[0:RP, :, :], s, ALU.min).then_inc(kept_ready, 1)
                    dve.wait_ge(kept_ready, LB + b + 1)
                    V.tensor_reduce(negmax[0:RP, b % 2, :], kept[0:RP, :, :], AX, ALU.max, negate=True).then_inc(neg_ready, 1)
                    dve.wait_ge(neg_ready, NB + b + 1 + CREDIT)
                    dve.wait_ge(pt_done, NB + b - 2 + CREDIT)
                    V.tensor_tensor(probs[0:RP, b % 4, :, :], kept[0:RP, :, :], bc(negmax[0:RP, b % 2, :, None], 2, NTP), ALU.add)\
                        .then_inc(lm_scores_ready, 1)

                def weigh(b):
                    p = probs[0:RP, b % 4, :, :]
                    dve.wait_ge(exp_done, NB + b + 1 + CREDIT)
                    counts = pB[0:RP, 1, 0:RT * NTP].rearrange("p (j t) -> p j t", j=RT)
                    V.tensor_tensor(p, p, counts, ALU.mult).then_inc(max_ready, 1)
                    dve.wait_ge(max_ready, NB + b + 1 + CREDIT)
                    V.tensor_reduce(den[0:RP, b % 4, :], p, AX, ALU.add).then_inc(den_ready, 1)
                    dve.wait_ge(den_ready, NB + b + 1 + CREDIT)
                    V.reciprocal(rden[0:RP, b % 4, :], den[0:RP, b % 4, :]).then_inc(rden_ready, 1)

                for i in range(NSTEP):
                    if 0 <= i - 1 < UB:
                        choose(i - 1)
                    if 0 <= i - 2 < UB:
                        scores_of_chosen(i - 2)
                        weigh(i - 2)
                dve.wait_ge(lm_proj_done, u + 1)
                V.scalar_tensor_tensor(halves(hB[:, :]), pAu, sc("bp"), halves(hA[:, :, :].rearrange("p b t -> p (b t)")), ALU.add, ALU.add)\
                    .then_inc(residual_ready, 1)
                dve.wait_ge(norm2_rstd_ready, u + 1)
                V.tensor_tensor(halves(xn[:, :]), pBu, halves(rs[:, :]), ALU.mult).then_inc(norm2_ready, 1)
                dve.wait_ge(gate_key_done, u + 1)
                V.tensor_scalar(halves(qf[:, :]), pAu, sc("gbk"), None, ALU.add).then_inc(gate_key_ready, 1)
                dve.wait_ge(gate_scores_done, u + 1)
                s = pS[0:RP, 0, 0:RT * E].rearrange("p (j e) -> p j e", j=RT)
                link(V.tensor_reduce(gate_s[:, 0, :], s, AX, ALU.max, negate=True))
                V.tensor_tensor(gate[:, 0], s, bc(gate_s[:, 0, :, None], 2, E), ALU.add).then_inc(gate_less_max_ready, 1)
                dve.wait_ge(s_eatt[0], u * 64 + 16)
                G = dve.snap(u * 8)
                project_k(G, 0)
                project_q(G, 0)
                dve.wait_ge(gate_exp_ready, u + 1)
                link(V.tensor_reduce(gate_s[:, 1, :], gate[:, 1], AX, ALU.add))
                link(V.reciprocal(gate_s[:, 2, :], gate_s[:, 1, :]))
                link(V.tensor_tensor(gall[:, :, 6:6 + E], gate[:, 1], bc(gate_s[:, 2, :, None], 2, E), ALU.mult), own=True)
                for j in range(RT):
                    last = V.max(gtop[:, j, :], gall[:, j, :])
                last.then_inc(gate_top_ready, 1)
                dve.wait_ge(gate_top_ready, 2 * u + 1)
                dve.sem_inc(passed_dve, 1)
                for j in range(RT):
                    last = V.match_replace(gout[:, j, :], gtop[:, j, :], gall[:, j, :], -1.0)
                last.then_inc(gate_top_ready, 1)
                dve.wait_ge(gate_top_ready, 2 * u + 2)
                V.scalar_tensor_tensor(gate[:, 2], gout[:, :, 6:6 + E], 0.0, gall[:, :, 6:6 + E], ALU.is_lt, ALU.mult).then_inc(gate_best_ready, 1)
                dve.wait_ge(gate_best_ready, u + 1)
                link(V.tensor_reduce(gate_s[:, 3, :], gate[:, 2], AX, ALU.add))
                link(V.tensor_scalar(gate_s[:, 4, :], gate_s[:, 3, :], 1e-9, None, ALU.add))
                V.reciprocal(gate_s[:, 5, :], gate_s[:, 4, :]).then_inc(gate_rden_ready, 1)
                dve.wait_ge(gate_rden_ready, u + 1)
                V.tensor_tensor(gate[:, 5], gate[:, 2], bc(gate_s[:, 5, :, None], 2, E), ALU.mult).then_inc(gate_weights_ready, 1)
                dve.wait_ge(gate_weights_ready, u + 1)
                link(V.tensor_copy(gpart[:, 0], gate[:, 5]))
                link(V.tensor_tensor(gate[:, 3], gate[:, 5], gpart[:, 0], ALU.subtract))
                link(V.tensor_copy(gpart[:, 1], gate[:, 3]))
                link(V.tensor_tensor(gpart[:, 2], gate[:, 3], gpart[:, 1], ALU.subtract))
                V.tensor_copy(gsum[:, :, :, :].rearrange("p j n e -> p n j e"), gpart[:, :, :, :]).then_inc(gate_parts_ready, 1)
                assert links[0] == NUCH, links
                dve.wait_ge(gate_t_done, u + 1)
                V.tensor_copy(gate_t[:, 0:4 * RP], pP[0:NPART * E, 0, 0:4 * RP])
                V.tensor_copy(gate_t[:, 4 * RP:RT * RP], pP[0:NPART * E, 1, 0:RP]).then_inc(gate_t_ready, 1)
                dve.wait_ge(gate_t_ready, 2 * u + 1)
                V.tensor_copy(gate_t16[:, :], gate_t[:, :]).then_inc(gate_t_ready, 1)
                dve.wait_ge(gated_be2_done, u + 1)
                V.tensor_tensor(halves(acc[:, :]), pAu, halves(hB[:, :]), ALU.add).then_inc(acc_ready, 1)

                dve.wait_ge(q_high_ready, u * 8 + 1)
                mask_high(dve.snap(u * 72 + 8), 0, 0)
                dve.wait_ge(q_low_ready, u * 8 + 1)
                mask_low(dve.snap(u * 72 + 8), 0, 0)
                body(dve.snap(u * 72 + 8), dve.snap(u * 8), 0, dve.snap(u * 64 + 16), None, closing=False)
                body(dve.snap(u * 72 + 16), dve.snap(u * 8 + 1), 1, dve.snap(u * 64 + 32), dve.snap(u * 64 + 16), closing=False)
                with dve.Fori(0, 2) as t:
                    body(dve.snap(u * 72 + 24 + t * 16), dve.snap(u * 8 + 2 + t * 2), 0,
                         dve.snap(u * 64 + t * 16 + 32), dve.snap(u * 64 + t * 16 + 16))
                    body(dve.snap(u * 72 + 32 + t * 16), dve.snap(u * 8 + 3 + t * 2), 1,
                         dve.snap(u * 64 + t * 16 + 48), dve.snap(u * 64 + t * 16 + 32))
                body(dve.snap(u * 72 + 56), dve.snap(u * 8 + 6), 0, dve.snap(u * 64 + 64), dve.snap(u * 64 + 48))
                body(dve.snap(u * 72 + 64), dve.snap(u * 8 + 7), 1, None, dve.snap(u * 64 + 64))
                body(dve.snap(u * 72 + 72), dve.snap(u * 8 + 8), 0, None, dve.snap(u * 64 + 64), att=False)
                dve.wait_ge(text_rows_done, u + 1)
                dve.wait_ge(s_out, u * 32)
                V.tensor_copy(outtext[:, :, :].rearrange("p (k b) d -> p k (b d)", k=2), pB[:, :, :]).then_inc(outtext_ready, 1)


def kernel(**inputs):
    import numpy as np
    import concourse.bacc as bacc
    from concourse.bass_utils import run_bass_kernel_spmd

    a = {k: np.asarray(v) for k, v in inputs.items()}
    f32 = np.float32

    def put(shape_cols, width, parts):
        blk = np.zeros((128, width), f32)
        for name, v in parts.items():
            lo, hi = shape_cols[name]
            v = np.asarray(v)
            blk[:v.shape[0], lo:hi] = v.reshape(v.shape[0], -1)
        return blk

    pos_of = np.arange(SEQT)
    seg_of = (T0 + pos_of) // SEGL
    A = np.zeros((SEQT, SEGS), f32)
    A[pos_of, seg_of] = 1
    M = np.zeros((NTP, SEGS), f32)
    for t in range(T0):
        M[t, t // SEGL] += 1
    for t in range(SEQ, SEGS * SEGL):
        M[NT, t // SEGL] += 1
    tval = np.full((NTP,), -1.0, f32)
    tval[T0:NT] = np.arange(NCLS)
    mask = (np.arange(128)[:, None] // DH == np.arange(H)[None]).astype(f32)
    const = put(CCOL, CW, dict(
        C=np.eye(128, dtype=f32) - f32(1 / 128), J=np.full((128, 128), 1 / 128, f32), I=np.eye(128, dtype=f32),
        mask=np.repeat(mask, NT, axis=1), A=A, tcol=np.tile(tval, (128, 1)), M4=M / SEGL, MT=M.T, tval=tval[:, None]))
    wqkv = a["L0_attn_w_qkv"].reshape(3, D, D)
    shared = put(SCOL, SW, dict(
        wq=wqkv[0].T, wk=wqkv[1].T, wv=wqkv[2].T, wp=a["L0_attn_w_proj"].T, gwk=a["L0_ffn_gate_Wk"].T,
        eq=a["L0_ffn_expert_queries"].T, be2=np.tile(a["L0_ffn_be2"], (NPART, 1)), pos=a["L0_tok_pos_embed"].T, txtw=a["L0_txt_W"],
        bp=a["L0_attn_b_proj"][:, None], tokb=a["L0_tok_b"][:, None], cls=a["L0_tok_class_token"].T,
        txtb=a["L0_txt_b"][:, None], gbk=a["L0_ffn_gate_bk"][:, None]))
    tokw = np.ascontiguousarray(a["L0_tok_W"].T.reshape(KJ, KP, D).transpose(1, 0, 2))
    eatt, effn = [], []
    for e in range(E):
        w, bqkv = a["L0_ffn_Wqkv"][e].reshape(3, D, D), a["L0_ffn_bqkv"][e].reshape(3, D, 1)
        eatt.append(put(ACOL, AW, dict(wq=w[0].T, wk=w[1].T, wv=w[2].T, bq=bqkv[0], bk=bqkv[1], bv=bqkv[2])))
        pick = np.zeros((NPART * E, D), f32)
        pick[e::E] = 1
        effn.append(put(FCOL, FW, dict(
            wo=a["L0_ffn_Wo"][e], w1=a["L0_ffn_W1"][e].T,
            w2=a["L0_ffn_W2"][e].T.reshape(FCH, D, D).transpose(1, 0, 2), pick=pick,
            bo=a["L0_ffn_bo"][e][:, None], g1=a["L0_ffn_g1"][e][:, None], be1=a["L0_ffn_be1"][e][:, None],
            bf1=a["L0_ffn_bf1"][e].reshape(FCH, D).T, bf2=a["L0_ffn_bf2"][e][:, None], g2=a["L0_ffn_g2"][e][:, None])))
    x = a["x"].reshape(NU, 2, 4, 3, 8, 28, 8, 28).transpose(0, 1, 3, 5, 7, 2, 4, 6).reshape(NU, 2, KJ, KP, 4 * NP)
    arrays = dict(x_in=np.ascontiguousarray(x.transpose(0, 1, 3, 2, 4)), xt_in=np.ascontiguousarray(a["x_txt"].T),
                  xr_in=np.ascontiguousarray(a["x_txt"].reshape(NU, UB * SEQT)), const_in=const, shared_in=shared,
                  tokw_in=tokw, eatt_in=np.stack(eatt), effn_in=np.stack(effn))
    nc = bacc.Bacc("TRN2", target_bir_lowering=False, num_devices=1)
    args = [nc.dram_tensor(k, v.shape, mybir.dt.from_np(v.dtype), kind="ExternalInput").ap() for k, v in arrays.items()]
    args.append(nc.dram_tensor("out", (B, SEQ, D), F32, kind="ExternalOutput").ap())
    build(nc, *args)
    r = run_bass_kernel_spmd(nc, [arrays], core_ids=[0])
    return r.results[0]["out"]
```
